# Optimizing a Trainium2 kernel written in Bass

```python
import numpy as np
import jax
import jax.numpy as jnp

def _softmax(x, axis=-1):
    return jax.nn.softmax(x, axis=axis)

def _gelu(x):
    return jax.nn.gelu(x, approximate=True)

def _silu(x):
    return jax.nn.silu(x)

def _sigmoid(x):
    return jax.nn.sigmoid(x)

def _layernorm(x, axis=-1, eps=1e-05):
    m = jnp.mean(x, axis=axis, keepdims=True)
    v = jnp.var(x, axis=axis, keepdims=True)
    return (x - m) / jnp.sqrt(v + eps)

def _scatter_add(tgt, idx, src, axis=0):
    return tgt.at[idx].add(src)

def _segment_sum(src, seg, n):
    return jax.ops.segment_sum(src, seg, n)
kernel_name = 'mk_lm_tower_d1_tok_ids1024_r4_2f111e'

def setup_inputs(seed: int=0):
    np.random.seed(seed)
    _w = jnp.asarray

    def _rec_inputs():
        import jax
        import jax.numpy as jnp
        _rk = jax.random.key(seed)
        x = jax.random.randint(jax.random.fold_in(_rk, 1), (64, 256), 0, 7999, jnp.int32)
        return x
    x = _rec_inputs()

    def _L0_tok_setup():
        import jax, jax.numpy as jnp
        import numpy as np
        V = 8000
        H = 256
        DK = 128
        TMAX = 512
        N, T = (8, 512)
        EPS = 1e-05
        key = jax.random.key(seed)
        ks = jax.random.split(key, 12)
        s = 0.02
        return {'inputs': jax.random.randint(ks[0], (N, T), 0, V), 'tok_emb': jax.random.normal(ks[1], (V, H), dtype=jnp.float32) * s, 'pos_emb': jax.random.normal(ks[2], (TMAX, H), dtype=jnp.float32) * s, 'wq': jax.random.normal(ks[3], (DK, H), dtype=jnp.float32) * s, 'bq': jnp.zeros((DK,), jnp.float32), 'wk': jax.random.normal(ks[4], (DK, H), dtype=jnp.float32) * s, 'bk': jnp.zeros((DK,), jnp.float32), 'wv': jax.random.normal(ks[5], (DK, H), dtype=jnp.float32) * s, 'bv': jnp.zeros((DK,), jnp.float32), 'wo': jax.random.normal(ks[6], (H, 2 * DK), dtype=jnp.float32) * s, 'bo': jnp.zeros((H,), jnp.float32), 'gamma': jnp.ones((H,), jnp.float32), 'beta': jnp.zeros((H,), jnp.float32)}
    _L0_tok_all = _L0_tok_setup()
    _L0_tok_in = {k: v for k, v in _L0_tok_all.items() if k in ('tok_emb', 'pos_emb', 'wq', 'bq', 'wk', 'bk', 'wv', 'bv', 'wo', 'bo', 'gamma', 'beta')}
    del _L0_tok_all

    def _L0_attn_setup():
        import math
        import jax, jax.numpy as jnp
        import numpy as np
        D_MODEL = 256
        N_HEADS = 16
        D_HEAD = D_MODEL // N_HEADS

        def get_alibi_slopes(n_heads: int) -> np.ndarray:

            def pow2_slopes(n):
                start = 2 ** (-2 ** (-(math.log2(n) - 3)))
                return np.array([start * start ** i for i in range(n)], dtype=np.float32)
            if math.log2(n_heads).is_integer():
                return pow2_slopes(n_heads)
            closest = 2 ** math.floor(math.log2(n_heads))
            slopes = pow2_slopes(closest)
            extra = pow2_slopes(2 * closest)[0::2][:n_heads - closest]
            return np.concatenate([slopes, extra], axis=0)
        key = jax.random.key(seed)
        ks = jax.random.split(key, 9)
        B, S, D = (2, 512, D_MODEL)
        scale = 1.0 / math.sqrt(D)
        inp = {'x': jax.random.normal(ks[0], (B, S, D), dtype=jnp.float32), 'Wq': jax.random.normal(ks[1], (D, D), dtype=jnp.float32) * scale, 'bq': jnp.zeros((D,), dtype=jnp.float32), 'Wk': jax.random.normal(ks[2], (D, D), dtype=jnp.float32) * scale, 'bk': jnp.zeros((D,), dtype=jnp.float32), 'Wv': jax.random.normal(ks[3], (D, D), dtype=jnp.float32) * scale, 'bv': jnp.zeros((D,), dtype=jnp.float32), 'Wo': jax.random.normal(ks[4], (D, D), dtype=jnp.float32) * scale, 'bo': jnp.zeros((D,), dtype=jnp.float32)}
        return inp
    _L0_attn_all = _L0_attn_setup()
    _L0_attn_in = {k: v for k, v in _L0_attn_all.items() if k in ('Wq', 'bq', 'Wk', 'bk', 'Wv', 'bv', 'Wo', 'bo')}
    del _L0_attn_all

    def _L0_ffn_setup():
        import jax, jax.numpy as jnp
        import numpy as np
        B, K, D = (128, 32, 256)
        E = 32
        H = int(D * 0.25)

        def _rsqrt_uniform(key, shape, d):
            bound = d ** (-0.5)
            return jax.random.uniform(key, shape, jnp.float32, -bound, bound)
        key = jax.random.key(seed)
        ks = jax.random.split(key, 7)
        return {'x': jax.random.normal(ks[0], (B, K, D), jnp.float32), 'router_w': _rsqrt_uniform(ks[1], (E, D), D), 'router_b': _rsqrt_uniform(ks[2], (E,), D), 'weights1': _rsqrt_uniform(ks[3], (E, D, H), H), 'bias1': _rsqrt_uniform(ks[4], (E, H), H), 'weights2': _rsqrt_uniform(ks[5], (E, H, D), D), 'bias2': _rsqrt_uniform(ks[6], (E, D), D)}
    _L0_ffn_all = _L0_ffn_setup()
    _L0_ffn_in = {k: v for k, v in _L0_ffn_all.items() if k in ('router_w', 'router_b', 'weights1', 'bias1', 'weights2', 'bias2')}
    del _L0_ffn_all
    return {'x': x, 'L0_tok_tok_emb': _L0_tok_in['tok_emb'], 'L0_tok_pos_emb': _L0_tok_in['pos_emb'], 'L0_tok_wq': _L0_tok_in['wq'], 'L0_tok_bq': _L0_tok_in['bq'], 'L0_tok_wk': _L0_tok_in['wk'], 'L0_tok_bk': _L0_tok_in['bk'], 'L0_tok_wv': _L0_tok_in['wv'], 'L0_tok_bv': _L0_tok_in['bv'], 'L0_tok_wo': _L0_tok_in['wo'], 'L0_tok_bo': _L0_tok_in['bo'], 'L0_tok_gamma': _L0_tok_in['gamma'], 'L0_tok_beta': _L0_tok_in['beta'], 'L0_attn_Wq': _L0_attn_in['Wq'], 'L0_attn_bq': _L0_attn_in['bq'], 'L0_attn_Wk': _L0_attn_in['Wk'], 'L0_attn_bk': _L0_attn_in['bk'], 'L0_attn_Wv': _L0_attn_in['Wv'], 'L0_attn_bv': _L0_attn_in['bv'], 'L0_attn_Wo': _L0_attn_in['Wo'], 'L0_attn_bo': _L0_attn_in['bo'], 'L0_ffn_router_w': _L0_ffn_in['router_w'], 'L0_ffn_router_b': _L0_ffn_in['router_b'], 'L0_ffn_weights1': _L0_ffn_in['weights1'], 'L0_ffn_bias1': _L0_ffn_in['bias1'], 'L0_ffn_weights2': _L0_ffn_in['weights2'], 'L0_ffn_bias2': _L0_ffn_in['bias2']}

def reference(x, L0_tok_tok_emb, L0_tok_pos_emb, L0_tok_wq, L0_tok_bq, L0_tok_wk, L0_tok_bk, L0_tok_wv, L0_tok_bv, L0_tok_wo, L0_tok_bo, L0_tok_gamma, L0_tok_beta, L0_attn_Wq, L0_attn_bq, L0_attn_Wk, L0_attn_bk, L0_attn_Wv, L0_attn_bv, L0_attn_Wo, L0_attn_bo, L0_ffn_router_w, L0_ffn_router_b, L0_ffn_weights1, L0_ffn_bias1, L0_ffn_weights2, L0_ffn_bias2):
    import jax
    import jax.numpy as jnp

    def _L0_tok_ref(inputs, tok_emb, pos_emb, wq, bq, wk, bk, wv, bv, wo, bo, gamma, beta):
        import jax, jax.numpy as jnp
        import numpy as np
        V = 8000
        H = 256
        DK = 128
        TMAX = 512
        N, T = (8, 512)
        EPS = 1e-05
        x = tok_emb[inputs] + pos_emb[jnp.arange(inputs.shape[1])][None, :, :]
        q = jnp.einsum('nth,dh->ntd', x, wq) + bq
        k = jnp.einsum('nth,dh->ntd', x, wk) + bk
        v = jnp.einsum('nth,dh->ntd', x, wv) + bv
        scores = jnp.einsum('ntd,nsd->nts', q, k) / np.float32(np.sqrt(DK))
        attn = jax.nn.softmax(scores, axis=-1)
        head = jnp.einsum('nts,nsd->ntd', attn, v)
        h = jnp.concatenate([head, head], axis=-1)
        out = jnp.einsum('ntd,hd->nth', h, wo) + bo + x
        mu = jnp.mean(out, axis=-1, keepdims=True)
        var = jnp.mean(jnp.square(out - mu), axis=-1, keepdims=True)
        return (out - mu) * jax.lax.rsqrt(var + EPS) * gamma + beta

    def _L0_attn_ref(x, Wq, bq, Wk, bk, Wv, bv, Wo, bo):
        import math
        import jax, jax.numpy as jnp
        import numpy as np
        D_MODEL = 256
        N_HEADS = 16
        D_HEAD = D_MODEL // N_HEADS

        def get_alibi_slopes(n_heads: int) -> np.ndarray:

            def pow2_slopes(n):
                start = 2 ** (-2 ** (-(math.log2(n) - 3)))
                return np.array([start * start ** i for i in range(n)], dtype=np.float32)
            if math.log2(n_heads).is_integer():
                return pow2_slopes(n_heads)
            closest = 2 ** math.floor(math.log2(n_heads))
            slopes = pow2_slopes(closest)
            extra = pow2_slopes(2 * closest)[0::2][:n_heads - closest]
            return np.concatenate([slopes, extra], axis=0)
        B, S, D = x.shape
        H, Dh = (N_HEADS, D_HEAD)
        q = (x @ Wq.T + bq).reshape(B, S, H, Dh).transpose(0, 2, 1, 3)
        k = (x @ Wk.T + bk).reshape(B, S, H, Dh).transpose(0, 2, 1, 3)
        v = (x @ Wv.T + bv).reshape(B, S, H, Dh).transpose(0, 2, 1, 3)
        scores = jnp.einsum('bhqd,bhkd->bhqk', q, k) / math.sqrt(Dh)
        slopes = jnp.asarray(get_alibi_slopes(H), dtype=scores.dtype)
        pos = jnp.arange(S, dtype=scores.dtype)
        pos_diff = pos[None, :] - pos[:, None]
        alibi = slopes[:, None, None] * pos_diff[None, :, :]
        scores = scores + alibi[None]
        causal = jnp.tril(jnp.ones((S, S), dtype=bool))
        scores = jnp.where(causal[None, None], scores, -jnp.inf)
        weights = jax.nn.softmax(scores, axis=-1)
        y = jnp.einsum('bhqk,bhkd->bhqd', weights, v)
        y = y.transpose(0, 2, 1, 3).reshape(B, S, D)
        return y @ Wo.T + bo

    def _L0_ffn_ref(x, router_w, router_b, weights1, bias1, weights2, bias2):
        import jax, jax.numpy as jnp
        import numpy as np
        B, K, D = (128, 32, 256)
        E = 32
        H = int(D * 0.25)

        def _rsqrt_uniform(key, shape, d):
            bound = d ** (-0.5)
            return jax.random.uniform(key, shape, jnp.float32, -bound, bound)
        b, k, d = x.shape
        x_flat = x.reshape(-1, d)
        n = x_flat.shape[0]
        logits = x_flat @ router_w.T + router_b
        routed_idx = jnp.argmax(logits, axis=-1)

        def expert_mlp(w1, b1, w2, b2):
            h = jax.nn.relu(x_flat @ w1 + b1)
            return jax.nn.relu(h @ w2 + b2)
        y_all = jax.vmap(expert_mlp)(weights1, bias1, weights2, bias2)
        out_flat = y_all[routed_idx, jnp.arange(n)]
        return out_flat.reshape(b, k, d)
    h = _L0_tok_ref(x, L0_tok_tok_emb, L0_tok_pos_emb, L0_tok_wq, L0_tok_bq, L0_tok_wk, L0_tok_bk, L0_tok_wv, L0_tok_bv, L0_tok_wo, L0_tok_bo, L0_tok_gamma, L0_tok_beta)
    h = h + _L0_attn_ref(_layernorm(h, axis=-1), L0_attn_Wq, L0_attn_bq, L0_attn_Wk, L0_attn_bk, L0_attn_Wv, L0_attn_bv, L0_attn_Wo, L0_attn_bo)
    h = h + _L0_ffn_ref(_layernorm(h, axis=-1), L0_ffn_router_w, L0_ffn_router_b, L0_ffn_weights1, L0_ffn_bias1, L0_ffn_weights2, L0_ffn_bias2)
    return h

_drawn_inputs = setup_inputs


def setup_inputs(seed=0):
    import zlib

    import numpy as np

    out = dict(_drawn_inputs(seed))
    spreads = {'L0_tok_bq': (0.0, 2.0),
     'L0_tok_bk': (0.0, 2.0),
     'L0_tok_bv': (0.0, 0.1),
     'L0_tok_bo': (0.0, 0.1),
     'L0_tok_gamma': (1.0, 0.2),
     'L0_tok_beta': (0.0, 0.1),
     'L0_attn_bq': (0.0, 2.0),
     'L0_attn_bk': (0.0, 2.0),
     'L0_attn_bv': (0.0, 0.1),
     'L0_attn_bo': (0.0, 0.1)}
    factors = {'L0_tok_wq': 173.873,
     'L0_tok_wk': 64.0,
     'L0_tok_wv': 7.911,
     'L0_ffn_bias1': 7.658,
     'L0_ffn_bias2': 2.93}
    for name, (base, spread) in spreads.items():
        noise = np.random.default_rng([zlib.crc32(name.encode()), seed]).standard_normal(out[name].shape)
        drawn = base * np.exp(spread * noise) if base else spread * noise
        out[name] = jnp.asarray(drawn.astype(out[name].dtype))
    for name, factor in factors.items():
        out[name] = (out[name] * factor).astype(out[name].dtype)
    return out
```

```python
from contextlib import ExitStack

import concourse.bass as bass
from concourse import mybir

F32 = mybir.dt.float32
BF16 = mybir.dt.bfloat16
I32 = mybir.dt.int32
ALU = mybir.AluOpType
ACT = mybir.ActivationFunctionType
AX = mybir.AxisListType

P = 128
NS, T = 64, 256
D = 256
DK = 128
NH, DH = 16, 16
E, HID = 32, 64
EPS = 1e-5
TT = T // P
CC = D // P
NTOK = NS * T
NTILE = NTOK // P
MTILES = NTILE + E
PARTS = 6
QPART = (0, 1, 2, 0, 1, 0)
KPART = (0, 0, 0, 1, 1, 2)
MASKED = -1e30
SLOTS = NH

AHEAD = (("ids", 0), ("gather", 3), ("embed", 6), ("embed_turn", 7), ("tok_qkv", 8), ("tok_scores", 9),
         ("tok_softmax", 10), ("tok_turn", 11), ("tok_mix", 12), ("tok_out", 13), ("stats1", 14), ("rstd1", 15),
         ("norm1", 16), ("affine", 17), ("stats2", 18), ("rstd2", 19), ("norm2", 20), ("norm_turn", 20),
         ("project_qk", 21), ("project_v", 22), ("split", 22), ("stack", 23), ("residual", 24))
BEHIND = (("recip", 1), ("take_mix", 2), ("recip_turn", 3), ("scale_mix", 4), ("out2", 6), ("stats3", 7), ("rstd3", 8), ("norm3", 9),
          ("router_turn", 10), ("logits", 11), ("choose", 12), ("rank", 13), ("place", 14))


class Seq:

    def __init__(self, n, par, pair):
        self.n, self.par, self.pair = n, par, pair


def seq_at(pair, k):
    if isinstance(pair, int):
        n = 2 * pair + k
        return Seq(n, n % 2, n // 2) if 0 <= n < NS else None
    return Seq(2 * pair + k, k % 2, pair + k // 2)


def later(s, k=1):
    return not isinstance(s.n, int) or s.n >= k


def iteration(ops, pair, k):
    here, before = seq_at(pair, k), seq_at(pair, k - 1)
    ahead = (seq_at(pair, k + 2), seq_at(pair, k + 1))

    def call(name, *args):
        if name in ops and args[0] is not None:
            ops[name](*args)

    for slot in range(SLOTS):
        call("scores", here, slot)
        call("turn", *((here, slot - 2) if slot >= 2 else (before, slot - 2 + NH)))
        call("weights", here, slot)
        call("evacuate", *((here, slot - 2) if slot >= 2 else (before, slot - 2 + NH)))
        call("mix", *((here, slot - 3) if slot >= 3 else (before, slot - 3 + NH)))
        for name, at in AHEAD:
            if at % SLOTS == slot:
                call(name, ahead[at // SLOTS])
        for name, at in BEHIND:
            if at == slot:
                call(name, before)


def run_iterations(eng, ops):
    for it in range(-2, 3):
        iteration(ops, 0, it)
    last = (NS - 4) // 2
    with eng.Fori(1, last) as pair:
        iteration(ops, pair, 1)
        iteration(ops, pair, 2)
    for it in range(2 * last + 1, NS + 1):
        iteration(ops, 0, it)


def build(nc, a):
    slopes = [float((2.0 ** -0.5) * (2.0 ** -0.5) ** i) for i in range(NH)]
    out = a["out"]
    hidden = nc.dram_tensor("hidden_dram", (NTOK, D), F32)
    LIST = (E + 2) * NTOK
    lists = nc.dram_tensor("lists_dram", (LIST, 1), I32)

    with ExitStack() as ctx:
        def sb(name, shape, dt=F32):
            return ctx.enter_context(nc.sbuf_tensor(name, shape, dt))

        def sem(name):
            return ctx.enter_context(nc.semaphore(name))

        wq, wk, wv = (sb(n, [P, CC, DK]) for n in ("wq", "wk", "wv"))
        wo = sb("wo", [P, D])
        bqk = sb("bqk", [P, 2])
        bq_scaled = sb("bq_scaled", [P, 1])
        wq2, wk2, wv2, wo2 = (sb(n, [P, CC, D]) for n in ("wq2", "wk2", "wv2", "wo2"))
        bqk2 = sb("bqk2", [P, 2, 2])
        bv1 = sb("bv1", [P, 1])
        bv2 = sb("bv2", [P, 2])
        pos = sb("pos", [P, TT, D])
        tok_bias = sb("tok_bias", [P, TT, D])
        attn_bias = sb("attn_bias", [P, TT, D])
        gamma = sb("gamma", [P, TT, D])
        beta = sb("beta", [P, TT, D])
        router = sb("router", [P, CC, E])
        router_b = sb("router_b", [P, TT, E])
        w1 = sb("w1", [P, E, CC * HID + 1])
        w2 = sb("w2", [HID + 1, E, D])
        ident = sb("ident", [P, P])
        minus_half = sb("minus_half", [P, TT])
        rel = sb("rel", [P, 3 * P])
        alibi = sb("alibi", [P, NH, 3 * P])
        tri = sb("tri", [P, P], BF16)
        ones = sb("ones", [P, P], BF16)
        rev = sb("rev", [P, TT, E])
        base = sb("base", [P, E], BF16)
        number = [sb(f"number{i}", [P, TT], I32) for i in range(2)]
        two_sequences = sb("two_sequences", [P, TT], I32)

        ids = [sb(f"ids{i}", [P, TT], I32) for i in range(2)]
        x = [sb(f"x{i}", [P, TT, D]) for i in range(2)]
        xb = sb("xb", [P, TT, D])
        xT = sb("xT", [P, CC, T])
        qkT = sb("qkT", [P, 2, T])
        v1 = sb("v1", [P, TT, DK])
        nmax1, sum1, rsum1 = (sb(n, [P, TT]) for n in ("nmax1", "sum1", "rsum1"))
        p1 = sb("p1", [P, TT, T])
        pT1 = sb("pT1", [P, TT, T])
        headT = sb("headT", [P, T])
        h0 = sb("h0", [P, TT, D])
        bn = [sb(f"bn{i}", [P, TT, 6]) for i in range(3)]
        mv = [sb(f"mv{i}", [P, TT, 2]) for i in range(3)]
        ve = [sb(f"ve{i}", [P, TT]) for i in range(3)]
        rstd = [sb(f"rstd{i}", [P, TT]) for i in range(3)]
        xhat = sb("xhat", [P, TT, D])
        xg = sb("xg", [P, TT, D])
        h1 = sb("h1", [P, TT, D])
        h1b = [sb(f"h1b{i}", [P, TT, D]) for i in range(2)]
        xn = sb("xn", [P, TT, D])
        xnT = sb("xnT", [P, CC, T])
        part = [sb(f"part{i}", [P, 3, 2, T], BF16) for i in range(2)]
        rest = [sb(f"rest{i}", [P, 2, T]) for i in range(2)]
        qst = [sb(f"qst{i}", [PARTS * DH, NH, T], BF16) for i in range(2)]
        kst = [sb(f"kst{i}", [PARTS * DH, NH, T], BF16) for i in range(2)]
        vpad = [sb(f"vpad{i}", [P, TT, NH // 2, 4 * DH]) for i in range(2)]
        sc = [sb(f"sc{i}", [P, 3 * P]) for i in range(2)]
        nmax = sb("nmax", [P, 2, TT])
        pr = [sb(f"pr{i}", [P, 3 * P]) for i in range(2)]
        prT = [sb(f"prT{i}", [P, 3 * P]) for i in range(2)]
        sums = [sb(f"sums{i}", [P, TT, NH]) for i in range(2)]
        rsums = sb("rsums", [P, TT, NH])
        rexp = sb("rexp", [P, TT, D])
        yT, ynT = sb("yT", [P, 2, T]), sb("ynT", [P, 2, T])
        h2 = [sb(f"h2{i}", [P, TT, D]) for i in range(2)]
        xf = sb("xf", [P, TT, D])
        xfT = sb("xfT", [P, CC, T])
        lg, eq, onehot_f = (sb(n, [P, TT, E]) for n in ("lg", "eq", "onehot_f"))
        top, best = sb("top", [P, TT]), sb("best", [P, TT])
        onehot = sb("onehot", [P, TT, E], BF16)
        acc = sb("acc", [P, E], BF16)
        place_m = sb("place_m", [P, TT, E])
        place_f = sb("place_f", [P, TT])
        place_i = [sb(f"place_i{i}", [P, TT], I32) for i in range(2)]
        iota_t = sb("iota_t", [E, MTILES])
        count = sb("count", [E, 1])
        ntiles = sb("ntiles", [E, 1])
        tri_inc = sb("tri_inc", [E, E])
        cum = sb("cum", [E, 1])
        ones_col = sb("ones_col", [E, 1])
        table = sb("table", [1, 2, MTILES], I32)
        NB = 4
        eoid = sb("eoid", [P, 2 * NB], I32)
        eid = [eoid[:, i:i + 1] for i in range(NB)]
        oid = [eoid[:, NB + i:NB + i + 1] for i in range(NB)]

        spare, at = alibi[:].rearrange("p h k -> p (h k)"), [0]

        def in_alibi(width, rows=P):
            at[0] += width
            return spare[0:rows, at[0] - width:at[0]]

        he = [in_alibi(D) for _ in range(NB)]
        oe = [in_alibi(D) for _ in range(NB)]
        xe = [in_alibi(D) for _ in range(2)]
        xeT = [in_alibi(D).rearrange("p (c t) -> p c t", c=CC) for _ in range(2)]
        w1e = [in_alibi(CC * HID + 1) for _ in range(2)]
        hT = [in_alibi(P, HID + 1) for _ in range(2)]
        ebn = [in_alibi(6) for _ in range(NB)]
        emv = [in_alibi(2) for _ in range(NB)]
        eve = [in_alibi(1) for _ in range(NB)]
        ers = [in_alibi(1) for _ in range(NB)]
        below = in_alibi(NTILE, E)
        passed = in_alibi(MTILES, E)
        tab_f = in_alibi(4 * MTILES, 1).rearrange("p (n t) -> p n t", n=4)
        wo_a = xhat[:]
        row_bias = xg[:]
        bv_rep = rexp[:].rearrange("p t (a k) -> p (t a) k", a=2)
        sentinel = h2[0][:, 0, :].bitcast(I32)

        def bank(name):
            return ctx.enter_context(nc.psum_tensor(name, [P, 512], F32))

        ps_s = [bank("ps_s0"), bank("ps_s1")]
        ps_t = [bank("ps_t0"), bank("ps_t1")]
        ps_y = bank("ps_y")
        ps_a, ps_b = bank("ps_a"), bank("ps_b")
        ps_c = bank("ps_c")

        loaded = sem("loaded")
        experts_loaded = sem("experts_loaded")
        lists_clear = sem("lists_clear")
        pool_const = sem("pool_const")
        dve_const = sem("dve_const")
        pe_const = sem("pe_const")
        ids_in = [sem(f"ids_in{i}") for i in range(2)]
        rows_in = [sem(f"rows_in{i}") for i in range(2)]
        stacked = [sem(f"stacked{i}") for i in range(2)]
        h2_out = [sem(f"h2_out{i}") for i in range(2)]
        placed = [sem(f"placed{i}") for i in range(2)]
        x_ready, xb_ready = sem("x_ready"), sem("xb_ready")
        ve_ready = [sem(f"ve_ready{i}") for i in range(3)]
        rstd_ready = [sem(f"rstd_ready{i}") for i in range(3)]
        xg_ready, h1_ready, h1b_ready = sem("xg_ready"), sem("h1_ready"), sem("h1b_ready")
        part2_ready, part3_ready = sem("part2_ready"), sem("part3_ready")
        rexp_ready = sem("rexp_ready")
        number_ready = sem("number_ready")
        acc_half, acc_ready = sem("acc_half"), sem("acc_ready")
        xT_done, qk_done, v_done, s1_done, pT1_done = (sem(n) for n in ("xT_done", "qk_done", "v_done", "s1_done", "pT1_done"))
        head_done, out1_done, xnT_done = sem("head_done"), sem("out1_done"), sem("xnT_done")
        Q_done, K_done, V_done = sem("Q_done"), sem("K_done"), sem("V_done")
        scores_done, turn_done, mix_done = sem("scores_done"), sem("turn_done"), sem("mix_done")
        rT_done, out2_done, xfT_done, logits_done, rank_done = (sem(n) for n in ("rT_done", "out2_done", "xfT_done", "logits_done", "rank_done"))
        xT_ready, q_ready, p1_ready, pT1_ready, xnT_ready = (sem(n) for n in ("xT_ready", "q_ready", "p1_ready", "pT1_ready", "xnT_ready"))
        part1_ready = sem("part1_ready")
        vpad_ready = sem("vpad_ready")
        pr_ready = sem("pr_ready")
        prT_odd = sem("prT_odd")
        yT_ready, xfT_ready = sem("yT_ready"), sem("xfT_ready")
        k_ready, v_ready, nmax1_ready, rsum1_ready, head_ready, h0_ready = (
            sem(n) for n in ("k_ready", "v_ready", "nmax1_ready", "rsum1_ready", "head_ready", "h0_ready"))
        bn_ready = [sem(f"bn_ready{i}") for i in range(3)]
        mv_ready = [sem(f"mv_ready{i}") for i in range(3)]
        xhat_ready, xn_ready = sem("xhat_ready"), sem("xn_ready")
        rest_ready = sem("rest_ready")
        sc_ready = sem("sc_ready")
        prT_even = sem("prT_even")
        rsums_ready, ynT_ready, h2_ready, xf_ready = (sem(n) for n in ("rsums_ready", "ynT_ready", "h2_ready", "xf_ready"))
        route = sem("route")
        onehot_ready = sem("onehot_ready")
        place_step, place_ready = sem("place_step"), sem("place_ready")
        tab_pe, tab_dve = sem("tab_pe"), sem("tab_dve")
        eid_in = [sem(f"eid_in{i}") for i in range(NB)]
        he_in = [sem(f"he_in{i}") for i in range(NB)]
        oe_out = [sem(f"oe_out{i}") for i in range(NB)]
        he_clear = sem("he_clear")
        e_bn, e_mv, e_ve, e_rs, e_xe = (sem(n) for n in ("e_bn", "e_mv", "e_ve", "e_rs", "e_xe"))
        e_xeT, e_xeTs, e_w1, e_h, e_hs, e_y, e_o, e_oid = (sem(n) for n in ("e_xeT", "e_xeTs", "e_w1", "e_h", "e_hs", "e_y", "e_o", "e_oid"))

        passed_sp, passed_pool, passed_dve = sem("passed_sp"), sem("passed_pool"), sem("passed_dve")

        def wait_alone(eng, passed_waits, semaphore, value):
            eng.wait_ge(semaphore, value)
            eng.sem_inc(passed_waits, 1)

        row = lambda v: v.rearrange("(a n) -> a n", a=1)
        LOADS = [
            (pos[:], a["pos_emb"][0:T, :].rearrange("(t p) c -> p t c", p=P)),
            (wq[:], a["wqT"].rearrange("(c p) d -> p c d", p=P)), (wk[:], a["wkT"].rearrange("(c p) d -> p c d", p=P)),
            (wv[:], a["wvT"].rearrange("(c p) d -> p c d", p=P)), (wo_a, a["woT"].rearrange("(c p) d -> p c d", p=P)),
            (bqk[:, 0:1], a["bq"]), (bqk[:, 1:2], a["bk"]), (bv1[:], a["bv"]),
            (row_bias[:, 0, :], row(a["bo"]).to_broadcast([P, D])), (row_bias[:, 1, :], row(a["bo2"]).to_broadcast([P, D])),
            (gamma[:, 0, :], row(a["gamma"]).to_broadcast([P, D])), (gamma[:, 1, :], row(a["gamma"]).to_broadcast([P, D])),
            (beta[:, 0, :], row(a["beta"]).to_broadcast([P, D])), (beta[:, 1, :], row(a["beta"]).to_broadcast([P, D])),
            (wq2[:], a["wq2T"].rearrange("(c p) d -> p c d", p=P)), (wk2[:], a["wk2T"].rearrange("(c p) d -> p c d", p=P)),
            (wv2[:], a["wv2T"].rearrange("(c p) d -> p c d", p=P)), (wo2[:], a["wo2T"].rearrange("(c p) d -> p c d", p=P)),
            (bqk2[:, 0, :], a["bq2"]), (bqk2[:, 1, :], a["bk2"]), (bv2[:], a["bv2"]),
            (router[:], a["routerT"].rearrange("(c p) e -> p c e", p=P)),
            (router_b[:, 0, :], row(a["router_b"]).to_broadcast([P, E])), (router_b[:, 1, :], row(a["router_b"]).to_broadcast([P, E])),
        ]
        EXPERT_LOADS = [(w1[:, :, c * HID:(c + 1) * HID], a["w1"][:, c * P:(c + 1) * P, :].rearrange("e p m -> p e m"))
                        for c in range(CC)]
        EXPERT_LOADS += [(w1[0:HID, :, CC * HID:], a["b1T"].rearrange("m (e a) -> m e a", a=1)),
                         (w2[0:HID, :, :], a["w2"].rearrange("e m d -> m e d")), (w2[HID:HID + 1, :, :], a["b2"].rearrange("(a e) d -> a e d", a=1))]
        ALL_LOADED = 16 * len(LOADS)
        EXPERTS_LOADED = 16 * len(EXPERT_LOADS)
        POOL_CONST = 19
        DVE_CONST = NH + 6

        block = ctx.enter_context(nc.Block())

        @block.sync
        def _(sp):
            for dst, src in LOADS:
                sp.dma_start(dst, src).then_inc(loaded, 16)
            sp.wait_ge(pool_const, POOL_CONST)
            for dst, src in EXPERT_LOADS:
                sp.dma_start(dst, src, allow_slow_non_contiguous=True).then_inc(experts_loaded, 16)
            for i in range(LIST // (P * 256)):
                sp.dma_start(lists[i * P * 256:(i + 1) * P * 256, :].rearrange("(p n) a -> p (n a)", p=P),
                             sentinel).then_inc(lists_clear, 16)

            def load_ids(s):
                sp.wait_ge(pool_const, POOL_CONST)
                if later(s, 2):
                    sp.wait_ge(rows_in[s.par], 32 * s.pair)
                sp.dma_start(ids[s.par][:], a["ids"][bass.ds(s.n, 1), :, :].rearrange("a p t -> (a p) t")
                             ).then_inc(ids_in[s.par], 16)

            def stack(s):
                sp.wait_ge(pool_const, POOL_CONST)
                wait_alone(sp, passed_sp, part1_ready, 2 * s.n + 2)
                wait_alone(sp, passed_sp, part3_ready, 2 * s.n + 2)
                if later(s, 2):
                    sp.wait_ge(scores_done, NH * (s.n - 1))
                for b in range(PARTS):
                    for dst, src, which in ((qst, part[0], QPART), (kst, part[1], KPART)):
                        sp.dma_start(dst[s.par][DH * b:DH * (b + 1), :, :], src[:, which[b], :, :]
                                     ).then_inc(stacked[s.par], 16)

            def store_h2(s):
                sp.wait_ge(pool_const, POOL_CONST)
                sp.wait_ge(h2_ready, s.n + 1)
                sp.dma_start(hidden[bass.ds(s.n * T, T), :].rearrange("(t p) c -> p t c", p=P), h2[s.par][:]
                             ).then_inc(h2_out[s.par], 16)

            run_iterations(sp, dict(ids=load_ids, stack=stack, stats3=store_h2))

            sp.wait_ge(tab_dve, 4)
            for i in range(2):
                sp.wait_ge(placed[i], 32 * (NS // 2))
                sp.wait_ge(h2_out[i], 16 * (NS // 2))

            def load_tile(i, b):
                at = sp.value_load(table[0:1, 1, bass.ds(i, 1)], min_val=0, max_val=LIST - P)
                sp.dma_start(eid[b], lists[bass.ds(at, P), :]).then_inc(eid_in[b], 16)

            for i in range(5):
                if i >= NB:
                    sp.wait_ge(he_in[i % NB], 16)
                    sp.wait_ge(e_oid, i - NB + 1)
                load_tile(i, i % NB)
            with sp.Fori(0, MTILES // NB - 2) as r:
                for u in range(NB):
                    b = (u + 5) % NB
                    sp.wait_ge(pool_const, POOL_CONST)
                    sp.wait_ge(e_oid, NB * r + u + 2)
                    sp.wait_ge(he_in[b], 16 * (r + (u + 5) // NB))
                    load_tile(NB * r + u + 5, b)
            for i in range(MTILES - 2 * NB + 5, MTILES):
                sp.wait_ge(he_in[i % NB], 16 * (i // NB))
                sp.wait_ge(e_oid, i - NB + 1)
                load_tile(i, i % NB)

        @block.gpsimd
        def _(pool):
            g = nc.gpsimd
            g.memset(ident[:], 0.0).then_inc(pool_const, 1)
            g.memset(tri[:], 1.0).then_inc(pool_const, 1)
            g.memset(tri_inc[:], 1.0).then_inc(pool_const, 1)
            g.iota(rel[:, 0:P], [[1, P]], base=0, channel_multiplier=-1, allow_small_or_imprecise_dtypes=True).then_inc(pool_const, 1)
            g.iota(rel[:, P:3 * P], [[1, 2 * P]], base=-P, channel_multiplier=-1, allow_small_or_imprecise_dtypes=True).then_inc(pool_const, 1)
            pool.wait_ge(pool_const, 5)
            g.affine_select(out=ident[:], in_=ident[:], compare_op=ALU.not_equal, fill=1.0, base=0,
                            pattern=[[-1, P]], channel_multiplier=1).then_inc(pool_const, 1)
            g.affine_select(out=tri[:], in_=tri[:], compare_op=ALU.is_gt, fill=0.0, base=0,
                            pattern=[[1, P]], channel_multiplier=-1).then_inc(pool_const, 1)
            g.affine_select(out=tri_inc[:], in_=tri_inc[:], compare_op=ALU.is_ge, fill=0.0, base=0,
                            pattern=[[1, E]], channel_multiplier=-1).then_inc(pool_const, 1)
            g.affine_select(out=rel[:, 0:P], in_=rel[:, 0:P], compare_op=ALU.is_ge, fill=MASKED, base=0,
                            pattern=[[-1, P]], channel_multiplier=1).then_inc(pool_const, 1)
            g.affine_select(out=rel[:, P:3 * P], in_=rel[:, P:3 * P], compare_op=ALU.is_ge, fill=MASKED, base=P,
                            pattern=[[-1, 2 * P]], channel_multiplier=1).then_inc(pool_const, 1)
            g.memset(minus_half[:], -0.5).then_inc(pool_const, 1)
            g.memset(sentinel, NTOK).then_inc(pool_const, 1)
            g.memset(w1[:, :, CC * HID:], 0.0).then_inc(pool_const, 1)
            g.iota(rev[:], [[0, TT], [-1, E]], base=E, channel_multiplier=0, allow_small_or_imprecise_dtypes=True).then_inc(pool_const, 1)
            g.iota(base[:], [[NTOK // P, E]], base=0, channel_multiplier=0, allow_small_or_imprecise_dtypes=True).then_inc(pool_const, 1)
            for i in range(2):
                g.iota(number[i][:], [[P, TT]], base=i * T, channel_multiplier=1).then_inc(pool_const, 1)
            g.iota(two_sequences[:], [[0, TT]], base=2 * T, channel_multiplier=0).then_inc(pool_const, 1)
            g.iota(iota_t[:], [[1, MTILES]], base=0, channel_multiplier=0, allow_small_or_imprecise_dtypes=True).then_inc(pool_const, 1)
            pool.wait_ge(loaded, ALL_LOADED)
            pool.wait_ge(dve_const, DVE_CONST)
            pool.wait_ge(lists_clear, 16 * (LIST // (P * 256)))

            def gather(s):
                if later(s, 2):
                    pool.wait_ge(xT_done, s.n - 1)
                    pool.wait_ge(xb_ready, s.n - 1)
                wait_alone(pool, passed_pool, ids_in[s.par], 16 * (s.pair + 1))
                for t in range(TT):
                    g.indirect_dma_start(out=x[s.par][:, t, :], out_offset=None, in_=a["tok_emb"],
                                         in_offset=bass.IndirectOffsetOnAxis(ap=ids[s.par][:, t:t + 1], axis=0)
                                         ).then_inc(rows_in[s.par], 16)

            def embed(s):
                pool.wait_ge(rows_in[s.par], 32 * (s.pair + 1))
                g.tensor_tensor(x[s.par][:], x[s.par][:], pos[:], ALU.add).then_inc(x_ready, 1)
                pool.wait_ge(x_ready, s.n + 1)
                if later(s):
                    pool.wait_ge(h0_ready, s.n)
                g.tensor_tensor(xb[:], x[s.par][:], tok_bias[:], ALU.add).then_inc(xb_ready, 1)

            def rstd_of(i):
                def f(s):
                    wait_alone(pool, passed_pool, mv_ready[i], s.n + 1)
                    g.tensor_scalar(ve[i][:], mv[i][:, :, 1], EPS, None, ALU.add).then_inc(ve_ready[i], 1)
                    pool.wait_ge(ve_ready[i], s.n + 1)
                    g.tensor_tensor(rstd[i][:], ve[i][:], minus_half[:], ALU.pow).then_inc(rstd_ready[i], 1)
                return f

            def affine(s):
                pool.wait_ge(xhat_ready, s.n + 1)
                g.tensor_tensor(xg[:], xhat[:], gamma[:], ALU.mult).then_inc(xg_ready, 1)
                pool.wait_ge(xg_ready, s.n + 1)
                if later(s):
                    pool.wait_ge(xn_ready, s.n)
                    pool.wait_ge(h1b_ready, s.n)
                g.tensor_tensor(h1[:], xg[:], beta[:], ALU.add).then_inc(h1_ready, 1)

            def residual(s):
                pool.wait_ge(h1_ready, s.n + 1)
                if later(s, 2):
                    pool.wait_ge(h2_ready, s.n - 1)
                g.tensor_tensor(h1b[s.par][:], h1[:], attn_bias[:], ALU.add).then_inc(h1b_ready, 1)

            def split(s):
                for i in range(2):
                    if later(s):
                        pool.wait_ge(stacked[1 - s.par], 192 * (s.pair + s.par))
                    wait_alone(pool, passed_pool, rest_ready, 2 * s.n + i + 1)
                    g.tensor_copy(part[i][:, 1, :, :], rest[i][:]).then_inc(part2_ready, 1)
                    pool.wait_ge(part2_ready, 2 * s.n + i + 1)
                    g.tensor_tensor(part[i][:, 2, :, :], rest[i][:], part[i][:, 1, :, :], ALU.subtract).then_inc(part3_ready, 1)

            def recip(s):
                if later(s):
                    pool.wait_ge(rT_done, s.n)
                wait_alone(pool, passed_pool, rsums_ready, s.n + 1)
                g.tensor_copy(rexp[:].rearrange("p t (h d) -> p t h d", d=DH),
                              rsums[:, :, :, None].to_broadcast([P, TT, NH, DH])).then_inc(rexp_ready, 1)

            def rank(s):
                pool.wait_ge(rank_done, s.n + 1)
                g.tensor_tensor(acc[:], acc[:], onehot[:, 0, :], ALU.add).then_inc(acc_half, 1)
                pool.wait_ge(acc_half, s.n + 1)
                g.tensor_tensor(acc[:], acc[:], onehot[:, 1, :], ALU.add).then_inc(acc_ready, 1)

            def place(s):
                pool.wait_ge(place_ready, s.n + 1)
                if later(s, 2):
                    pool.wait_ge(placed[s.par], 32 * s.pair)
                    g.tensor_tensor(number[s.par][:], number[s.par][:], two_sequences[:], ALU.add).then_inc(number_ready, 1)
                    wait_alone(pool, passed_pool, number_ready, s.n - 1)
                for t in range(TT):
                    g.indirect_dma_start(out=lists[:, :], out_offset=bass.IndirectOffsetOnAxis(ap=place_i[s.par][:, t:t + 1], axis=0),
                                         in_=number[s.par][:, t:t + 1], in_offset=None).then_inc(placed[s.par], 16)

            run_iterations(pool, dict(gather=gather, embed=embed, rstd1=rstd_of(0), rstd2=rstd_of(1), rstd3=rstd_of(2), affine=affine,
                                      residual=residual, split=split, recip=recip, rank=rank, place=place))

            def fetch(i, b, turn, first=False):
                if first:
                    pool.wait_ge(he_clear, NB)
                else:
                    pool.wait_ge(e_o, i - NB + 1)
                wait_alone(pool, passed_pool, eid_in[b], 16 * (turn + 1))
                g.indirect_dma_start(out=he[b], out_offset=None, in_=hidden[:, :],
                                     in_offset=bass.IndirectOffsetOnAxis(ap=eid[b], axis=0),
                                     bounds_check=NTOK - 1, oob_is_err=False).then_inc(he_in[b], 16)

            def e_rstd(i, b):
                wait_alone(pool, passed_pool, e_mv, i + 1)
                g.tensor_scalar(eve[b], emv[b][:, 1:2], EPS, None, ALU.add).then_inc(e_ve, 1)
                pool.wait_ge(e_ve, i + 1)
                g.tensor_tensor(ers[b], eve[b], minus_half[:, 0:1], ALU.pow).then_inc(e_rs, 1)

            def send(i, b):
                wait_alone(pool, passed_pool, e_o, i + 1)
                g.indirect_dma_start(out=out, out_offset=bass.IndirectOffsetOnAxis(ap=oid[b], axis=0),
                                     in_=oe[b], in_offset=None, bounds_check=NTOK - 1, oob_is_err=False).then_inc(oe_out[b], 16)

            for i in range(3):
                fetch(i, i, 0, True)
            e_rstd(0, 0)
            e_rstd(1, 1)
            fetch(3, 3, 0, True)
            e_rstd(2, 2)
            send(0, 0)
            with pool.Fori(0, MTILES // NB - 1) as r:
                for u in range(NB):
                    fetch(NB * r + u + 4, u, r + 1)
                    e_rstd(NB * r + u + 3, (u + 3) % NB)
                    send(NB * r + u + 1, (u + 1) % NB)
            e_rstd(MTILES - 1, NB - 1)
            for i in range(MTILES - 3, MTILES):
                send(i, i % NB)
            for b in range(NB):
                pool.wait_ge(oe_out[b], 16 * (MTILES // NB))

        @block.scalar
        def _(act):
            s_ = nc.scalar
            act.wait_ge(loaded, ALL_LOADED)
            act.wait_ge(dve_const, DVE_CONST)

            def embed_turn(s):
                act.wait_ge(xT_done, s.n + 1)
                if later(s):
                    act.wait_ge(v_done, s.n)
                s_.activation(xT[:].rearrange("p c t -> p (c t)"), ps_a[:], ACT.Copy).then_inc(xT_ready, 1)

            def tok_qkv(s):
                act.wait_ge(qk_done, s.n + 1)
                if later(s):
                    act.wait_ge(s1_done, s.n)
                s_.activation(qkT[:, 0, :], ps_b[:, 0:T], ACT.Identity, bias=bq_scaled[:, 0:1], scale=DK ** -0.5).then_inc(q_ready, 1)

            def tok_softmax(s):
                act.wait_ge(nmax1_ready, s.n + 1)
                if later(s):
                    act.wait_ge(pT1_done, s.n)
                    act.wait_ge(rsum1_ready, s.n)
                for t in range(TT):
                    last = s_.activation(p1[:, t, :], ps_b[:, t * T:(t + 1) * T], ACT.Exp, bias=nmax1[:, t:t + 1],
                                         accum_out=sum1[:, t:t + 1])
                last.then_inc(p1_ready, 1)

            def tok_turn(s):
                act.wait_ge(pT1_done, s.n + 1)
                if later(s):
                    act.wait_ge(head_done, s.n)
                s_.activation(pT1[:].rearrange("p c t -> p (c t)"), ps_a[:], ACT.Copy).then_inc(pT1_ready, 1)

            def norm_turn(s):
                act.wait_ge(xnT_done, s.n + 1)
                if later(s):
                    act.wait_ge(V_done, s.n)
                s_.activation(xnT[:].rearrange("p c t -> p (c t)"), ps_b[:], ACT.Copy).then_inc(xnT_ready, 1)

            def project_qk(s):
                for i, (done, ps) in enumerate(((Q_done, ps_a), (K_done, ps_b))):
                    act.wait_ge(done, s.n + 1)
                    if later(s):
                        act.wait_ge(stacked[1 - s.par], 192 * (s.pair + s.par))
                        act.wait_ge(part3_ready, 2 * s.n)
                    for gr in range(2):
                        last = s_.activation(part[i][:, 0, gr, :], ps[:, gr * T:(gr + 1) * T], ACT.Identity,
                                             bias=bqk2[:, i, gr:gr + 1])
                    last.then_inc(part1_ready, 1)

            def project_v(s):
                act.wait_ge(V_done, s.n + 1)
                if later(s, 2):
                    act.wait_ge(mix_done, NH * (s.n - 1))
                for odd in range(2):
                    last = s_.activation(vpad[s.par][:, :, :, 48 * odd:48 * odd + DH],
                                         ps_a[:].rearrange("p (t h o d) -> p t h o d", t=TT, o=2, d=DH)[:, :, :, odd, :], ACT.Copy)
                last.then_inc(vpad_ready, 1)

            def weights(s, h):
                act.wait_ge(sc_ready, NH * s.n + h + 1)
                if later(s) or h >= 2:
                    act.wait_ge(turn_done, NH * s.n + h - 1)
                for t in range(TT):
                    c0, c1 = (0, P) if t == 0 else (P, 3 * P)
                    last = s_.activation(pr[h % 2][:, c0:c1], sc[h % 2][:, c0:c1], ACT.Exp, bias=nmax[:, h % 2, t:t + 1],
                                         scale=-1.0, accum_out=sums[s.par][:, t, h:h + 1])
                last.then_inc(pr_ready, 1)

            def evacuate(s, h):
                if h % 2 == 0:
                    return
                act.wait_ge(turn_done, NH * s.n + h + 1)
                if later(s) or h >= 2:
                    act.wait_ge(mix_done, NH * s.n + h - 1)
                s_.activation(prT[1][:], ps_t[1][:, 0:3 * P], ACT.Copy).then_inc(prT_odd, 1)

            def take_mix(s):
                act.wait_ge(mix_done, NH * s.n + NH)
                if later(s):
                    act.wait_ge(ynT_ready, s.n)
                s_.activation(yT[:].rearrange("p g t -> p (g t)"), ps_y[:], ACT.Copy).then_inc(yT_ready, 1)

            def router_turn(s):
                act.wait_ge(xfT_done, s.n + 1)
                if later(s):
                    act.wait_ge(logits_done, s.n)
                s_.activation(xfT[:].rearrange("p c t -> p (c t)"), ps_c[:], ACT.Copy).then_inc(xfT_ready, 1)

            run_iterations(act, dict(embed_turn=embed_turn, tok_qkv=tok_qkv, tok_softmax=tok_softmax, tok_turn=tok_turn,
                                     norm_turn=norm_turn, project_qk=project_qk, project_v=project_v, weights=weights,
                                     evacuate=evacuate, take_mix=take_mix, router_turn=router_turn))

            act.wait_ge(tab_dve, 4)
            act.wait_ge(experts_loaded, EXPERTS_LOADED)

            def turned(i, b):
                act.wait_ge(e_xeT, i + 1)
                if not isinstance(i, int) or i >= 2:
                    act.wait_ge(e_h, i - 1)
                s_.activation(xeT[b][:].rearrange("p c t -> p (c t)"), ps_s[b][:, 0:D], ACT.Copy).then_inc(e_xeTs, 1)
                e = act.value_load(table[0:1, 0, bass.ds(i, 1)], min_val=0, max_val=E - 1)
                s_.activation(w1e[b][:, None, :], w1[:, bass.ds(e, 1), :], ACT.Copy).then_inc(e_w1, 1)

            def hidden_relu(i, b):
                act.wait_ge(e_h, i + 1)
                if not isinstance(i, int) or i >= 2:
                    act.wait_ge(e_y, i - 1)
                act.wait_ge(e_w1, i + 1)
                s_.activation(hT[b][0:HID, :], ps_t[b][0:HID, 0:P], ACT.Relu, bias=w1e[b][0:HID, CC * HID:]).then_inc(e_hs, 1)

            def step(i, b):
                turned(i + 1, 1 - b)
                hidden_relu(i, b)

            turned(0, 0)
            step(0, 0)
            step(1, 1)
            with act.Fori(1, MTILES // 2 - 1) as r:
                step(2 * r, 0)
                step(2 * r + 1, 1)
            step(MTILES - 2, 0)
            hidden_relu(MTILES - 1, 1)

        @block.vector
        def _(dve):
            v = nc.vector
            dve.wait_ge(loaded, ALL_LOADED)
            dve.wait_ge(pool_const, POOL_CONST)
            for h in range(NH):
                v.tensor_scalar(alibi[:, h, :], rel[:], slopes[h], 4.0, ALU.mult, ALU.mult).then_inc(dve_const, 1)
            v.tensor_tensor(wo[:], wo_a[:, 0, :], wo_a[:, 1, :], ALU.add).then_inc(dve_const, 1)
            v.tensor_scalar(bq_scaled[:], bqk[:, 0:1], DK ** -0.5, None, ALU.mult).then_inc(dve_const, 1)
            for i, col in enumerate((bv1[:, 0:1], bv2[:, 0:1], bv2[:, 1:2])):
                v.tensor_copy(bv_rep[:, i, :], col.to_broadcast([P, P]))
            v.memset(ones[:], 1.0)
            v.memset(acc[:], 0.0)
            v.memset(ones_col[:], 1.0)
            for i in range(2):
                v.memset(vpad[i][:], 0.0)
            v.memset(sums[0][:], 0.0).then_inc(dve_const, 1)
            dve.wait_ge(pe_const, 1)
            for i, dst in enumerate((tok_bias, attn_bias)):
                for t in range(TT):
                    last = v.tensor_tensor(dst[:, t, :], ps_c[:, i * D:(i + 1) * D], row_bias[:, i, :], ALU.add)
                last.then_inc(dve_const, 1)
            v.memset(sums[1][:], 0.0).then_inc(dve_const, 1)

            def tok_qkv(s):
                dve.wait_ge(qk_done, s.n + 1)
                if later(s):
                    dve.wait_ge(s1_done, s.n)
                dve.wait_ge(q_ready, s.n + 1)
                v.tensor_scalar(qkT[:, 1, :], ps_b[:, T:2 * T], bqk[:, 1:2], None, ALU.add).then_inc(k_ready, 1)
                dve.wait_ge(v_done, s.n + 1)
                if later(s):
                    dve.wait_ge(head_done, s.n)
                v.tensor_copy(v1[:].rearrange("p t d -> p (t d)"), ps_a[:, 0:TT * DK]).then_inc(v_ready, 1)

            def tok_softmax(s):
                dve.wait_ge(s1_done, s.n + 1)
                if later(s):
                    dve.wait_ge(p1_ready, s.n)
                v.tensor_reduce(nmax1[:], ps_b[:].rearrange("p (t k) -> p t k", t=TT), AX.X, ALU.max, negate=True).then_inc(nmax1_ready, 1)

            def tok_turn(s):
                dve.wait_ge(p1_ready, s.n + 1)
                v.reciprocal(rsum1[:], sum1[:]).then_inc(rsum1_ready, 1)

            def tok_mix(s):
                dve.wait_ge(head_done, s.n + 1)
                if later(s):
                    dve.wait_ge(out1_done, s.n)
                v.tensor_copy(headT[:], ps_b[:, 0:T]).then_inc(head_ready, 1)

            def tok_out(s):
                dve.wait_ge(out1_done, s.n + 1)
                dve.wait_ge(xb_ready, s.n + 1)
                dve.wait_ge(rsum1_ready, s.n + 1)
                for t in range(TT):
                    last = v.scalar_tensor_tensor(out=h0[:, t, :], in0=ps_a[:, t * D:(t + 1) * D], scalar=rsum1[:, t:t + 1],
                                                  in1=xb[:, t, :], op0=ALU.mult, op1=ALU.add)
                last.then_inc(h0_ready, 1)

            def stats(i, src, s):
                for t in range(TT):
                    last = v.bn_stats(bn[i][:, t, :], src[:, t, :])
                last.then_inc(bn_ready[i], 1)
                wait_alone(dve, passed_dve, bn_ready[i], s.n + 1)
                for t in range(TT):
                    last = v.bn_aggr(mv[i][:, t, :], bn[i][:, t, :])
                last.then_inc(mv_ready[i], 1)

            def normalize(i, dst, src):
                for t in range(TT):
                    last = v.tensor_scalar(dst[:, t, :], src[:, t, :], mv[i][:, t, 0:1], rstd[i][:, t:t + 1], ALU.subtract, ALU.mult)
                return last

            def stats1(s):
                dve.wait_ge(h0_ready, s.n + 1)
                if later(s):
                    dve.wait_ge(rstd_ready[0], s.n)
                stats(0, h0, s)

            def norm1(s):
                dve.wait_ge(rstd_ready[0], s.n + 1)
                if later(s):
                    dve.wait_ge(xg_ready, s.n)
                normalize(0, xhat, h0).then_inc(xhat_ready, 1)

            def stats2(s):
                dve.wait_ge(h1_ready, s.n + 1)
                stats(1, h1, s)

            def norm2(s):
                dve.wait_ge(rstd_ready[1], s.n + 1)
                if later(s):
                    dve.wait_ge(xnT_done, s.n)
                normalize(1, xn, h1).then_inc(xn_ready, 1)

            def project_qk(s):
                for i, ps in enumerate((ps_a, ps_b)):
                    dve.wait_ge(part1_ready, 2 * s.n + i + 1)
                    if later(s):
                        dve.wait_ge(part3_ready, 2 * s.n)
                    for gr in range(2):
                        last = v.scalar_tensor_tensor(out=rest[i][:, gr, :], in0=ps[:, gr * T:(gr + 1) * T],
                                                      scalar=bqk2[:, i, gr:gr + 1], in1=part[i][:, 0, gr, :],
                                                      op0=ALU.add, op1=ALU.subtract)
                    last.then_inc(rest_ready, 1)

            def weights(s, h):
                if later(s) or h >= 2:
                    dve.wait_ge(pr_ready, NH * s.n + h - 1)
                wait_alone(dve, passed_dve, scores_done, NH * s.n + h + 1)
                for t in range(TT):
                    c0, c1 = (0, P) if t == 0 else (P, 3 * P)
                    last = v.tensor_tensor_reduce(out=sc[h % 2][:, c0:c1], in0=ps_s[h % 2][:, c0:c1], in1=alibi[:, h, c0:c1],
                                                  scale=-(DH ** -0.5), scalar=3e38, op0=ALU.add, op1=ALU.min,
                                                  accum_out=nmax[:, h % 2, t:t + 1])
                last.then_inc(sc_ready, 1)

            def evacuate(s, h):
                if h % 2:
                    return
                dve.wait_ge(turn_done, NH * s.n + h + 1)
                if later(s) or h >= 2:
                    dve.wait_ge(mix_done, NH * s.n + h - 1)
                v.tensor_copy(prT[0][:], ps_t[0][:, 0:3 * P]).then_inc(prT_even, 1)

            def recip(s):
                dve.wait_ge(pr_ready, NH * s.n + NH)
                if later(s):
                    dve.wait_ge(rexp_ready, s.n)
                v.reciprocal(rsums[:], sums[s.par][:]).then_inc(rsums_ready, 1)

            def scale_mix(s):
                dve.wait_ge(rT_done, s.n + 1)
                dve.wait_ge(yT_ready, s.n + 1)
                if later(s):
                    dve.wait_ge(out2_done, s.n)
                v.tensor_tensor(ynT[:].rearrange("p g t -> p (g t)"), yT[:].rearrange("p g t -> p (g t)"), ps_c[:], ALU.mult).then_inc(ynT_ready, 1)

            def stats3(s):
                dve.wait_ge(out2_done, s.n + 1)
                dve.wait_ge(h1b_ready, s.n + 1)
                if later(s, 2):
                    dve.wait_ge(h2_out[s.par], 16 * s.pair)
                v.tensor_tensor(h2[s.par][:].rearrange("p t c -> p (t c)"), ps_c[:], h1b[s.par][:].rearrange("p t c -> p (t c)"),
                                ALU.add).then_inc(h2_ready, 1)
                dve.wait_ge(h2_ready, s.n + 1)
                stats(2, h2[s.par], s)

            def norm3(s):
                dve.wait_ge(rstd_ready[2], s.n + 1)
                if later(s):
                    dve.wait_ge(xfT_done, s.n)
                normalize(2, xf, h2[s.par]).then_inc(xf_ready, 1)

            def choose(s):
                dve.wait_ge(logits_done, s.n + 1)
                wide = [P, TT, E]
                v.tensor_tensor(lg[:].rearrange("p t e -> p (t e)"), ps_c[:, 0:TT * E], router_b[:].rearrange("p t e -> p (t e)"),
                                ALU.add).then_inc(route, 1)
                dve.wait_ge(route, 5 * s.n + 1)
                v.tensor_reduce(top[:], lg[:], AX.X, ALU.max).then_inc(route, 1)
                dve.wait_ge(route, 5 * s.n + 2)
                v.tensor_tensor(eq[:], lg[:], top[:, :, None].to_broadcast(wide), ALU.is_equal).then_inc(route, 1)
                dve.wait_ge(route, 5 * s.n + 3)
                v.tensor_tensor(onehot_f[:], eq[:], rev[:], ALU.mult).then_inc(route, 1)
                dve.wait_ge(route, 5 * s.n + 4)
                v.tensor_reduce(best[:], onehot_f[:], AX.X, ALU.max).then_inc(route, 1)
                dve.wait_ge(route, 5 * s.n + 5)
                if later(s):
                    dve.wait_ge(acc_ready, s.n)
                v.tensor_tensor(onehot[:], rev[:], best[:, :, None].to_broadcast(wide), ALU.is_equal).then_inc(onehot_ready, 1)

            def place(s):
                dve.wait_ge(rank_done, s.n + 1)
                if later(s, 2):
                    dve.wait_ge(placed[s.par], 32 * s.pair)
                v.tensor_tensor(place_m[:].rearrange("p t e -> p (t e)"), ps_c[:, 0:TT * E], onehot[:].rearrange("p t e -> p (t e)"),
                                ALU.mult).then_inc(place_step, 1)
                dve.wait_ge(place_step, 2 * s.n + 1)
                v.tensor_reduce(place_f[:], place_m[:], AX.X, ALU.add).then_inc(place_step, 1)
                dve.wait_ge(place_step, 2 * s.n + 2)
                v.tensor_copy(place_i[s.par][:], place_f[:]).then_inc(place_ready, 1)

            run_iterations(dve, dict(tok_qkv=tok_qkv, tok_softmax=tok_softmax, tok_turn=tok_turn, tok_mix=tok_mix, tok_out=tok_out,
                                     stats1=stats1, norm1=norm1, stats2=stats2, norm2=norm2, project_qk=project_qk, weights=weights,
                                     evacuate=evacuate, recip=recip, scale_mix=scale_mix, stats3=stats3, norm3=norm3, choose=choose,
                                     place=place))

            for i in range(NB):
                v.memset(he[i], 0.0).then_inc(he_clear, 1)
            for i in range(2):
                v.memset(hT[i][HID:HID + 1, :], 1.0)
            dve.wait_ge(tab_pe, 1)
            v.tensor_copy(count[:], ps_c[0:E, 0:1]).then_inc(tab_dve, 1)
            dve.wait_ge(tab_dve, 1)
            v.tensor_scalar(below, iota_t[:, 0:NTILE], float(P), count[:, 0:1], ALU.mult, ALU.is_lt).then_inc(route, 1)
            dve.wait_ge(route, 5 * NS + 1)
            v.tensor_reduce(ntiles[:], below, AX.X, ALU.add).then_inc(tab_dve, 1)
            dve.wait_ge(tab_pe, 2)
            v.tensor_copy(cum[:], ps_c[0:E, 1:2]).then_inc(route, 1)
            dve.wait_ge(route, 5 * NS + 2)
            v.tensor_scalar(passed, iota_t[:], cum[:, 0:1], None, ALU.is_ge).then_inc(tab_dve, 1)
            dve.wait_ge(tab_pe, 3)
            experts, skipped = ps_c[0:1, 0:MTILES], ps_c[0:1, MTILES:2 * MTILES]
            v.scalar_tensor_tensor(out=tab_f[:, 0, :], in0=experts, scalar=float(NTOK // P), in1=iota_t[0:1, :],
                                   op0=ALU.mult, op1=ALU.add)
            v.tensor_scalar(tab_f[:, 1, :], experts, float(E - 1), None, ALU.min)
            v.tensor_copy(tab_f[:, 2, :], skipped).then_inc(route, 1)
            dve.wait_ge(route, 5 * NS + 3)
            v.tensor_tensor(tab_f[:, 3, :], tab_f[:, 0, :], tab_f[:, 2, :], ALU.subtract).then_inc(route, 1)
            dve.wait_ge(route, 5 * NS + 4)
            v.tensor_copy(table[:, 0, :], tab_f[:, 1, :])
            v.tensor_scalar(table[:, 1, :], tab_f[:, 3, :], float(P), None, ALU.mult).then_inc(tab_dve, 1)

            def e_norm(i, b, turn):
                dve.wait_ge(he_in[b], 16 * (turn + 1))
                if not isinstance(i, int) or i >= NB:
                    dve.wait_ge(oe_out[b], 16 * turn)
                v.tensor_copy(oid[b], eid[b]).then_inc(e_oid, 1)
                v.bn_stats(ebn[b], he[b]).then_inc(e_bn, 1)
                wait_alone(dve, passed_dve, e_bn, i + 1)
                v.bn_aggr(emv[b], ebn[b]).then_inc(e_mv, 1)

            def e_scale(i, b, b2):
                dve.wait_ge(e_rs, i + 1)
                if not isinstance(i, int) or i >= 2:
                    dve.wait_ge(e_xeT, i - 1)
                v.tensor_scalar(xe[b2], he[b], emv[b][:, 0:1], ers[b][:, 0:1], ALU.subtract, ALU.mult).then_inc(e_xe, 1)

            def e_out(i, b, b2):
                dve.wait_ge(e_y, i + 1)
                v.scalar_tensor_tensor(out=oe[b], in0=(ps_a, ps_b)[b2][:, 0:D], scalar=0.0, in1=he[b],
                                       op0=ALU.max, op1=ALU.add).then_inc(e_o, 1)

            e_norm(0, 0, 0)
            e_norm(1, 1, 0)
            e_scale(0, 0, 0)
            e_scale(1, 1, 1)
            e_norm(2, 2, 0)
            e_out(0, 0, 0)

            def steps(r):
                for u in range(NB):
                    e_norm(NB * r + u + 3, (u + 3) % NB, r + (u + 3) // NB)
                    e_scale(NB * r + u + 2, (u + 2) % NB, u % 2)
                    e_out(NB * r + u + 1, (u + 1) % NB, (u + 1) % 2)

            steps(0)
            with dve.Fori(1, MTILES // NB - 1) as r:
                steps(r)
            e_norm(MTILES - 1, NB - 1, MTILES // NB - 1)
            e_scale(MTILES - 2, NB - 2, 0)
            e_out(MTILES - 3, 1, 1)
            e_scale(MTILES - 1, NB - 1, 1)
            e_out(MTILES - 2, 2, 0)
            e_out(MTILES - 1, 3, 1)

        @block.tensor
        def _(pe):
            m = nc.tensor
            pe.wait_ge(loaded, ALL_LOADED)
            pe.wait_ge(dve_const, NH + 3)
            m.matmul(ps_c[:, 0:D], bv_rep[:, 0, :], wo[:], start=True, stop=True)
            m.matmul(ps_c[:, D:2 * D], bv_rep[:, 1, :], wo2[:, 0, :], start=True, stop=False)
            m.matmul(ps_c[:, D:2 * D], bv_rep[:, 2, :], wo2[:, 1, :], start=False, stop=True).then_inc(pe_const, 1)
            pe.wait_ge(dve_const, DVE_CONST)

            def turn_tokens(dst, src):
                for c in range(CC):
                    for t in range(TT):
                        last = m.transpose(dst[:, c * T + t * P:c * T + (t + 1) * P], src[:, t, c * P:(c + 1) * P], ident[:])
                return last

            def by_channel(dst, w, xt):
                for c in range(CC):
                    last = m.matmul(dst, w[c], xt[:, c, :], start=(c == 0), stop=(c == CC - 1))
                return last

            def by_token(dst, xt, w, n):
                for t in range(TT):
                    for c in range(CC):
                        last = m.matmul(dst[:, t * n:(t + 1) * n], xt[:, c, t * P:(t + 1) * P], w[:, c, :],
                                        start=(c == 0), stop=(c == CC - 1))
                return last

            def embed_turn(s):
                pe.wait_ge(x_ready, s.n + 1)
                if later(s):
                    pe.wait_ge(vpad_ready, s.n)
                turn_tokens(ps_a, x[s.par]).then_inc(xT_done, 1)

            def tok_qkv(s):
                pe.wait_ge(xT_ready, s.n + 1)
                if later(s):
                    pe.wait_ge(rest_ready, 2 * s.n)
                by_channel(ps_b[:, 0:T], [wq[:, c, :] for c in range(CC)], xT)
                by_channel(ps_b[:, T:2 * T], [wk[:, c, :] for c in range(CC)], xT).then_inc(qk_done, 1)
                by_token(ps_a, xT, wv, DK).then_inc(v_done, 1)

            def tok_scores(s):
                pe.wait_ge(q_ready, s.n + 1)
                pe.wait_ge(k_ready, s.n + 1)
                for t in range(TT):
                    last = m.matmul(ps_b[:, t * T:(t + 1) * T], qkT[:, 0, t * P:(t + 1) * P], qkT[:, 1, :], start=True, stop=True)
                last.then_inc(s1_done, 1)

            def tok_turn(s):
                pe.wait_ge(p1_ready, s.n + 1)
                pe.wait_ge(v_ready, s.n + 1)
                turn_tokens(ps_a, p1).then_inc(pT1_done, 1)

            def tok_mix(s):
                pe.wait_ge(pT1_ready, s.n + 1)
                by_channel(ps_b[:, 0:T], [v1[:, t, :] for t in range(TT)], pT1).then_inc(head_done, 1)

            def tok_out(s):
                pe.wait_ge(head_ready, s.n + 1)
                for t in range(TT):
                    last = m.matmul(ps_a[:, t * D:(t + 1) * D], headT[:, t * P:(t + 1) * P], wo[:], start=True, stop=True)
                last.then_inc(out1_done, 1)

            def norm_turn(s):
                pe.wait_ge(xn_ready, s.n + 1)
                turn_tokens(ps_b, xn).then_inc(xnT_done, 1)

            def project_qk(s):
                pe.wait_ge(xnT_ready, s.n + 1)
                pe.wait_ge(h0_ready, s.n + 1)
                for gr in range(2):
                    last = by_channel(ps_a[:, gr * T:(gr + 1) * T], [wq2[:, c, gr * P:(gr + 1) * P] for c in range(CC)], xnT)
                last.then_inc(Q_done, 1)
                for gr in range(2):
                    last = by_channel(ps_b[:, gr * T:(gr + 1) * T], [wk2[:, c, gr * P:(gr + 1) * P] for c in range(CC)], xnT)
                last.then_inc(K_done, 1)

            def project_v(s):
                pe.wait_ge(rest_ready, 2 * s.n + 1)
                by_token(ps_a, xnT, wv2, D).then_inc(V_done, 1)

            def scores(s, h):
                if h == 0:
                    pe.wait_ge(stacked[s.par], 192 * (s.pair + 1))
                if later(s) or h >= 2:
                    pe.wait_ge(sc_ready, NH * s.n + h - 1)
                q, k, dst = qst[s.par], kst[s.par], ps_s[h % 2]
                m.matmul(dst[:, 0:P], q[:, h, 0:P], k[:, h, 0:P], start=True, stop=True)
                m.matmul(dst[:, P:3 * P], q[:, h, P:2 * P], k[:, h, :], start=True, stop=True).then_inc(scores_done, 1)

            def turn(s, h):
                pe.wait_ge(pr_ready, NH * s.n + h + 1)
                if later(s) or h >= 2:
                    pe.wait_ge((prT_even, prT_odd)[h % 2], NH // 2 * s.n + h // 2)
                for i in range(3):
                    last = m.transpose(ps_t[h % 2][:, i * P:(i + 1) * P], pr[h % 2][:, i * P:(i + 1) * P], ident[:])
                last.then_inc(turn_done, 1)

            def mix(s, h):
                pe.wait_ge((prT_even, prT_odd)[h % 2], NH // 2 * s.n + h // 2 + 1)
                if h == 0:
                    pe.wait_ge(vpad_ready, s.n + 1)
                    if later(s):
                        pe.wait_ge(yT_ready, s.n)
                gr, quad, odd = h // 8, h % 8 // 2, h % 2
                rows = slice(32 * quad, 32 * quad + 32)
                w = vpad[s.par][:, :, h // 2, 32 * odd:32 * odd + 32]
                m.matmul(ps_y[rows, gr * T:(gr + 1) * T], w[:, 0, :], prT[h % 2][:, 0:T], start=(odd == 0), stop=False,
                         skip_group_check=True)
                m.matmul(ps_y[rows, gr * T + P:(gr + 1) * T], w[:, 1, :], prT[h % 2][:, T:3 * P], start=False, stop=(odd == 1),
                         skip_group_check=True).then_inc(mix_done, 1)

            def recip_turn(s):
                pe.wait_ge(rexp_ready, s.n + 1)
                if later(s):
                    pe.wait_ge(place_step, 2 * s.n)
                turn_tokens(ps_c, rexp).then_inc(rT_done, 1)

            def out2(s):
                pe.wait_ge(ynT_ready, s.n + 1)
                by_token(ps_c, ynT, wo2, D).then_inc(out2_done, 1)

            def router_turn(s):
                pe.wait_ge(xf_ready, s.n + 1)
                turn_tokens(ps_c, xf).then_inc(xfT_done, 1)

            def logits(s):
                pe.wait_ge(xfT_ready, s.n + 1)
                by_token(ps_c, xfT, router, E).then_inc(logits_done, 1)

            def rank(s):
                pe.wait_ge(onehot_ready, s.n + 1)
                if later(s):
                    pe.wait_ge(acc_ready, s.n)
                for t in range(TT):
                    dst = ps_c[:, t * E:(t + 1) * E]
                    m.matmul(dst, ones[:], base[:], start=True, stop=False)
                    m.matmul(dst, ones[:], acc[:], start=False, stop=False)
                    if t:
                        m.matmul(dst, ones[:], onehot[:, 0, :], start=False, stop=False)
                    last = m.matmul(dst, tri[:], onehot[:, t, :], start=False, stop=True)
                last.then_inc(rank_done, 1)

            run_iterations(pe, dict(embed_turn=embed_turn, tok_qkv=tok_qkv, tok_scores=tok_scores, tok_turn=tok_turn,
                                    tok_mix=tok_mix, tok_out=tok_out, norm_turn=norm_turn, project_qk=project_qk, project_v=project_v,
                                    scores=scores, turn=turn, mix=mix, recip_turn=recip_turn, out2=out2, router_turn=router_turn,
                                    logits=logits, rank=rank))

            pe.wait_ge(acc_ready, NS)
            pe.wait_ge(place_step, 2 * NS)
            m.matmul(ps_c[0:E, 0:1], acc[:], ones[:, 0:1], start=True, stop=True).then_inc(tab_pe, 1)
            pe.wait_ge(tab_dve, 2)
            m.matmul(ps_c[0:E, 1:2], tri_inc[:], ntiles[:], start=True, stop=True).then_inc(tab_pe, 1)
            pe.wait_ge(tab_dve, 3)
            m.matmul(ps_c[0:1, 0:MTILES], ones_col[:], passed, start=True, stop=True)
            m.matmul(ps_c[0:1, MTILES:2 * MTILES], ntiles[:], passed, start=True, stop=True).then_inc(tab_pe, 1)
            pe.wait_ge(tab_dve, 4)
            pe.wait_ge(experts_loaded, EXPERTS_LOADED)

            def e_turn(i, b):
                pe.wait_ge(e_xe, i + 1)
                if not isinstance(i, int) or i >= 2:
                    pe.wait_ge(e_xeTs, i - 1)
                for c in range(CC):
                    last = m.transpose(ps_s[b][:, c * P:(c + 1) * P], xe[b][:, c * P:(c + 1) * P], ident[:])
                last.then_inc(e_xeT, 1)

            def e_hidden(i, b):
                pe.wait_ge(e_xeTs, i + 1)
                pe.wait_ge(e_w1, i + 1)
                if not isinstance(i, int) or i >= 2:
                    pe.wait_ge(e_hs, i - 1)
                for c in range(CC):
                    last = m.matmul(ps_t[b][0:HID, 0:P], w1e[b][:, c * HID:(c + 1) * HID], xeT[b][:, c, :], start=(c == 0), stop=(c == CC - 1))
                last.then_inc(e_h, 1)

            def e_output(i, b):
                e = pe.value_load(table[0:1, 0, bass.ds(i, 1)], min_val=0, max_val=E - 1)
                pe.wait_ge(e_hs, i + 1)
                if not isinstance(i, int) or i >= 2:
                    pe.wait_ge(e_o, i - 1)
                m.matmul((ps_a, ps_b)[b][:, 0:D], hT[b][:], w2[:, bass.ds(e, 1), :], start=True, stop=True).then_inc(e_y, 1)

            def step(i, b):
                e_turn(i + 1, 1 - b)
                e_output(i, b)
                e_hidden(i + 1, 1 - b)

            e_turn(0, 0)
            e_hidden(0, 0)
            step(0, 0)
            step(1, 1)
            with pe.Fori(1, MTILES // 2 - 1) as r:
                step(2 * r, 0)
                step(2 * r + 1, 1)
            step(MTILES - 2, 0)
            e_output(MTILES - 1, 1)


def kernel(**inputs):
    import numpy as np
    import concourse.bacc as bacc
    from concourse.bass_utils import run_bass_kernel_spmd

    i = {k: np.asarray(v) for k, v in inputs.items()}
    tok, attn, ffn = (lambda n: i["L0_tok_" + n]), (lambda n: i["L0_attn_" + n]), (lambda n: i["L0_ffn_" + n])
    half = NH // 2

    def head_cols(w):
        return w.reshape(-1, half, 2, DH).transpose(0, 2, 3, 1).reshape(-1, D)

    arrays = {
        "ids": i["x"].reshape(NS, TT, P).transpose(0, 2, 1),
        "tok_emb": tok("tok_emb"), "pos_emb": tok("pos_emb"),
        "wqT": tok("wq").T, "wkT": tok("wk").T, "wvT": tok("wv").T, "woT": tok("wo").T,
        "bq": tok("bq")[:, None], "bk": tok("bk")[:, None], "bv": tok("bv")[:, None], "bo": tok("bo"),
        "gamma": tok("gamma"), "beta": tok("beta"),
        "wq2T": head_cols(attn("Wq").T), "wk2T": head_cols(attn("Wk").T), "wv2T": attn("Wv").T, "wo2T": attn("Wo").T,
        "bq2": head_cols(attn("bq")).reshape(2, P).T, "bk2": head_cols(attn("bk")).reshape(2, P).T,
        "bv2": attn("bv").reshape(2, P).T, "bo2": attn("bo"),
        "routerT": ffn("router_w").T, "router_b": ffn("router_b"),
        "w1": ffn("weights1"), "b1T": ffn("bias1").T, "w2": ffn("weights2"), "b2": ffn("bias2"),
    }
    arrays = {k: np.ascontiguousarray(v) for k, v in arrays.items()}
    nc = bacc.Bacc("TRN2", target_bir_lowering=False, num_devices=1)
    args = {k: nc.dram_tensor(f"in_{k}_dram", v.shape, mybir.dt.from_np(v.dtype), kind="ExternalInput").ap()
            for k, v in arrays.items()}
    args["out"] = nc.dram_tensor("out_dram", (NTOK, D), F32, kind="ExternalOutput").ap()
    build(nc, args)
    r = run_bass_kernel_spmd(nc, [{f"in_{k}_dram": v for k, v in arrays.items()}], core_ids=[0])
    return r.results[0]["out_dram"].reshape(NS, T, D)
```

```python
from contextlib import ExitStack

import concourse.bass as bass
from concourse import mybir

F32 = mybir.dt.float32
BF16 = mybir.dt.bfloat16
I32 = mybir.dt.int32
ALU = mybir.AluOpType
ACT = mybir.ActivationFunctionType
AX = mybir.AxisListType

P = 128
NS, T = 64, 256
D = 256
DK = 128
NH, DH = 16, 16
E, HID = 32, 64
EPS = 1e-5
TT = T // P
CC = D // P
NTOK = NS * T
NTILE = NTOK // P
MTILES = NTILE + E
PARTS = 6
QPART = (0, 1, 2, 0, 1, 0)
KPART = (0, 0, 0, 1, 1, 2)
MASKED = -1e30
ROW = D + 2
SLOTS = NH

PLACES = {
    "gather": dict(Pool=-47.2),
    "embed": dict(Pool=-44.3),
    "ids": dict(SP=-43.43),
    "embed_turn": dict(ACT=-37.04, PE=-36.99),
    "tok_qkv": dict(ACT=-35.86, PE=-34.74, DVE=-33.5),
    "rstd1": dict(Pool=-34.49),
    "tok_scores": dict(PE=-32.75),
    "tok_softmax": dict(ACT=-31.99, DVE=-31.61),
    "tok_turn": dict(ACT=-31.27, PE=-30.89, DVE=-27.96),
    "tok_mix": dict(PE=-29.52, DVE=-29.37),
    "tok_out": dict(PE=-27.59, DVE=-27.44),
    "stats1": dict(DVE=-26.44),
    "affine": dict(Pool=-23.9),
    "norm1": dict(DVE=-22.08),
    "rstd2": dict(Pool=-19.24),
    "residual": dict(Pool=-18.42),
    "stats2": dict(DVE=-15.57),
    "norm2": dict(DVE=-12.18),
    "norm_turn": dict(ACT=-12.1, PE=-11.57),
    "split": dict(Pool=-11.53),
    "stack": dict(SP=-10.64),
    "project_qk": dict(ACT=-9.92, PE=-9.09, DVE=-7.74),
    "project_v": dict(PE=-6.95, ACT=-6.69),
    "scores": dict(PE=0),
    "weights": dict(ACT=0.75, DVE=0.85),
    "turn": dict(PE=2.76),
    "evacuate": dict(DVE=2.89, ACT=2.97),
    "mix": dict(PE=4.68),
    "recip": dict(Pool=10.25, DVE=16.85),
    "rstd3": dict(Pool=17.5),
    "take_mix": dict(ACT=18.11),
    "recip_turn": dict(PE=19.54),
    "scale_mix": dict(DVE=20.2),
    "out2": dict(PE=21.17),
    "stats3": dict(DVE=22.26),
    "norm3": dict(DVE=24.89),
    "router_turn": dict(PE=25.47, ACT=25.49),
    "rank": dict(Pool=25.8, PE=31.05),
    "place": dict(Pool=25.91, DVE=31.87),
    "logits": dict(PE=27.36),
    "choose": dict(DVE=30.29),
    "store": dict(SP=31.04),
}
BY_HEAD = ("scores", "weights", "turn", "evacuate", "mix")
AHEAD = -int(min(min(places.values()) for places in PLACES.values()) // NH)
BEHIND = 1 + int(max(max(places.values()) for name, places in PLACES.items() if name not in BY_HEAD) // NH)

class Seq:

    def __init__(self, n, par, pair):
        self.n, self.par, self.pair = n, par, pair


def seq_at(pair, k):
    if isinstance(pair, int):
        n = 2 * pair + k
        return Seq(n, n % 2, n // 2) if 0 <= n < NS else None
    return Seq(2 * pair + k, k % 2, pair + k // 2)


def later(s, k=1):
    return not isinstance(s.n, int) or s.n >= k


def next_or_last(s):
    return min(s.n + 2, NS) if isinstance(s.n, int) else s.n + 2


def plan(engine):
    steps = []
    for name, places in PLACES.items():
        if engine in places:
            for head in range(NH) if name in BY_HEAD else (None,):
                at = places[engine] + (head or 0)
                steps.append((at % NH, name, -int(at // NH), () if head is None else (head,)))
    return [step[1:] for step in sorted(steps, key=lambda step: (step[0], step[1]))]


def run_iterations(eng, engine, ops):
    steps = plan(engine)

    def iteration(pair, k):
        for name, ahead, head in steps:
            s = seq_at(pair, k + ahead)
            if s is not None:
                ops[name](s, *head)

    for it in range(-AHEAD, 3):
        iteration(0, it)
    last = (NS - 1 - AHEAD) // 2
    with eng.Fori(1, last) as pair:
        iteration(pair, 1)
        iteration(pair, 2)
    for it in range(2 * last + 1, NS + BEHIND):
        iteration(0, it)


def build(nc, a):
    slopes = [float((2.0 ** -0.5) * (2.0 ** -0.5) ** i) for i in range(NH)]
    out = a["out"]
    hidden = nc.dram_tensor("hidden_dram", (NTOK, ROW), F32)
    LIST = (E + 2) * NTOK
    lists = nc.dram_tensor("lists_dram", (LIST, 1), I32)

    with ExitStack() as ctx:
        def sb(name, shape, dt=F32):
            return ctx.enter_context(nc.sbuf_tensor(name, shape, dt))

        def sem(name):
            return ctx.enter_context(nc.semaphore(name))

        wq, wk, wv = (sb(n, [P, CC, DK]) for n in ("wq", "wk", "wv"))
        wo = sb("wo", [P, D])
        bqk = sb("bqk", [P, 2])
        bq_scaled = sb("bq_scaled", [P, 1])
        wq2, wk2, wv2, wo2 = (sb(n, [P, CC, D]) for n in ("wq2", "wk2", "wv2", "wo2"))
        bqk2 = sb("bqk2", [P, 2, 2])
        bv1 = sb("bv1", [P, 1])
        bv2 = sb("bv2", [P, 2])
        pos = sb("pos", [P, TT, D])
        tok_bias = sb("tok_bias", [P, TT, D])
        attn_bias = sb("attn_bias", [P, TT, D])
        gamma = sb("gamma", [P, TT, D])
        beta = sb("beta", [P, TT, D])
        router = sb("router", [P, CC, E])
        router_b = sb("router_b", [P, TT, E])
        w1 = sb("w1", [P, E, CC * HID + 1])
        w2 = sb("w2", [HID + 1, E, D])
        ident = sb("ident", [P, P])
        minus_half = sb("minus_half", [P, TT])
        alibi = sb("alibi", [P, NH, 3 * P])
        tri = sb("tri", [P, P], BF16)
        ones = sb("ones", [P, P], BF16)
        rev = sb("rev", [P, TT, E])
        base = sb("base", [P, E], BF16)
        number = [sb(f"number{i}", [P, TT], I32) for i in range(2)]
        two_sequences = sb("two_sequences", [P, TT], I32)

        ids = [sb(f"ids{i}", [P, TT], I32) for i in range(2)]
        x = [sb(f"x{i}", [P, TT, D]) for i in range(2)]
        xb = sb("xb", [P, TT, D])
        xT = sb("xT", [P, CC, T])
        qkT = sb("qkT", [P, 2, T])
        v1 = sb("v1", [P, TT, DK])
        nmax1, sum1, rsum1 = (sb(n, [P, TT]) for n in ("nmax1", "sum1", "rsum1"))
        p1 = sb("p1", [P, TT, T])
        pT1 = sb("pT1", [P, TT, T])
        headT = sb("headT", [P, T])
        h0 = sb("h0", [P, TT, D])
        bn = [sb(f"bn{i}", [P, TT, 6]) for i in range(3)]
        mv = [sb(f"mv{i}", [P, TT, 2]) for i in range(2)]
        ve = [sb(f"ve{i}", [P, TT]) for i in range(3)]
        rstd = [sb(f"rstd{i}", [P, TT]) for i in range(2)]
        xhat = sb("xhat", [P, TT, D])
        xg = sb("xg", [P, TT, D])
        h1 = sb("h1", [P, TT, D])
        h1b = [sb(f"h1b{i}", [P, TT, D]) for i in range(2)]
        xn = sb("xn", [P, TT, D])
        xnT = sb("xnT", [P, CC, T])
        part = [sb(f"part{i}", [P, 3, 2, T], BF16) for i in range(2)]
        rest = [sb(f"rest{i}", [P, 2, T]) for i in range(2)]
        qst = [sb(f"qst{i}", [PARTS * DH, NH, T], BF16) for i in range(2)]
        kst = [sb(f"kst{i}", [PARTS * DH, NH, T], BF16) for i in range(2)]
        vpad = [sb(f"vpad{i}", [P, TT, NH // 2, 4 * DH]) for i in range(2)]
        sc = [sb(f"sc{i}", [P, 3 * P]) for i in range(2)]
        nmax = sb("nmax", [P, 2, TT])
        pr = [sb(f"pr{i}", [P, 3 * P]) for i in range(2)]
        prT = [sb(f"prT{i}", [P, 3 * P]) for i in range(2)]
        sums = [sb(f"sums{i}", [P, TT, NH]) for i in range(2)]
        rsums = sb("rsums", [P, TT, NH])
        rexp = sb("rexp", [P, TT, D])
        yT, ynT = sb("yT", [P, 2, T]), sb("ynT", [P, 2, T])
        h2 = [sb(f"h2{i}", [P, TT, ROW]) for i in range(2)]
        xf = sb("xf", [P, TT, D])
        xfT = sb("xfT", [P, CC, T])
        lg, eq, onehot_f = (sb(n, [P, TT, E]) for n in ("lg", "eq", "onehot_f"))
        top, best = sb("top", [P, TT]), sb("best", [P, TT])
        onehot = sb("onehot", [P, TT, E], BF16)
        acc = sb("acc", [P, E], BF16)
        place_m = sb("place_m", [P, TT, E])
        place_f = sb("place_f", [P, TT])
        place_i = [sb(f"place_i{i}", [P, TT], I32) for i in range(2)]
        iota_t = sb("iota_t", [E, MTILES])
        count = sb("count", [E, 1])
        ntiles = sb("ntiles", [E, 1])
        tri_inc = sb("tri_inc", [E, E])
        cum = sb("cum", [E, 1])
        ones_col = sb("ones_col", [E, 1])
        table = sb("table", [1, 2, MTILES], I32)
        NB = 8
        eoid = sb("eoid", [P, 2 * NB], I32)
        eid = [eoid[:, i:i + 1] for i in range(NB)]
        oid = [eoid[:, NB + i:NB + i + 1] for i in range(NB)]

        spare, at = alibi[:].rearrange("p h k -> p (h k)"), [0]

        def in_alibi(width, rows=P):
            at[0] += width
            return spare[0:rows, at[0] - width:at[0]]

        he = [in_alibi(ROW) for _ in range(NB)]
        xe = [in_alibi(D) for _ in range(2)]
        xeT = [in_alibi(D).rearrange("p (c t) -> p c t", c=CC) for _ in range(2)]
        w1e = [in_alibi(CC * HID + 1) for _ in range(2)]
        hT = [in_alibi(P, HID + 1) for _ in range(2)]
        below = in_alibi(NTILE, E)
        passed = in_alibi(MTILES, E)
        tab_f = in_alibi(4 * MTILES, 1).rearrange("p (n t) -> p n t", n=4)
        oe = [t[:, i, :] for t in (h0, h1b[0], h1b[1], xn) for i in range(TT)]
        wo_a = xhat[:]
        row_bias = xg[:]
        bv_rep = rexp[:].rearrange("p t (a k) -> p (t a) k", a=2)
        sentinel = h2[0][:, 0, 0:D].bitcast(I32)
        rel = pT1[:].rearrange("p t k -> p (t k)")[:, 0:3 * P]

        def bank(name):
            return ctx.enter_context(nc.psum_tensor(name, [P, 512], F32))

        ps_s = [bank("ps_s0"), bank("ps_s1")]
        ps_t = [bank("ps_t0"), bank("ps_t1")]
        ps_y = bank("ps_y")
        ps_a, ps_b = bank("ps_a"), bank("ps_b")
        ps_c = bank("ps_c")

        loaded = sem("loaded")
        experts_loaded = sem("experts_loaded")
        lists_clear = sem("lists_clear")
        pool_const = sem("pool_const")
        dve_const = sem("dve_const")
        pe_const = sem("pe_const")
        ids_in = [sem(f"ids_in{i}") for i in range(2)]
        rows_in = [sem(f"rows_in{i}") for i in range(2)]
        stacked = [sem(f"stacked{i}") for i in range(2)]
        h2_out = [sem(f"h2_out{i}") for i in range(2)]
        placed = [sem(f"placed{i}") for i in range(2)]
        x_ready, xb_ready = sem("x_ready"), sem("xb_ready")
        ve_ready = [sem(f"ve_ready{i}") for i in range(3)]
        rstd_ready = [sem(f"rstd_ready{i}") for i in range(3)]
        xg_ready, h1_ready, h1b_ready = sem("xg_ready"), sem("h1_ready"), sem("h1b_ready")
        part2_ready, part3_ready = sem("part2_ready"), sem("part3_ready")
        rexp_ready = sem("rexp_ready")
        number_ready = sem("number_ready")
        acc_half, acc_ready = sem("acc_half"), sem("acc_ready")
        xT_done, qk_done, v_done, s1_done, pT1_done = (sem(n) for n in ("xT_done", "qk_done", "v_done", "s1_done", "pT1_done"))
        head_done, out1_done, xnT_done = sem("head_done"), sem("out1_done"), sem("xnT_done")
        Q_done, K_done, V_done = sem("Q_done"), sem("K_done"), sem("V_done")
        scores_done, turn_done, mix_done = sem("scores_done"), sem("turn_done"), sem("mix_done")
        rT_done, out2_done, xfT_done, logits_done, rank_done = (sem(n) for n in ("rT_done", "out2_done", "xfT_done", "logits_done", "rank_done"))
        xT_ready, q_ready, p1_ready, pT1_ready, xnT_ready = (sem(n) for n in ("xT_ready", "q_ready", "p1_ready", "pT1_ready", "xnT_ready"))
        part1_ready = sem("part1_ready")
        vpad_ready = sem("vpad_ready")
        pr_ready = sem("pr_ready")
        prT_odd = sem("prT_odd")
        yT_ready, xfT_ready = sem("yT_ready"), sem("xfT_ready")
        k_ready, v_ready, nmax1_ready, rsum1_ready, head_ready, h0_ready = (
            sem(n) for n in ("k_ready", "v_ready", "nmax1_ready", "rsum1_ready", "head_ready", "h0_ready"))
        bn_ready = [sem(f"bn_ready{i}") for i in range(3)]
        mv_ready = [sem(f"mv_ready{i}") for i in range(3)]
        xhat_ready, xn_ready = sem("xhat_ready"), sem("xn_ready")
        rest_ready = sem("rest_ready")
        sc_ready = sem("sc_ready")
        prT_even = sem("prT_even")
        rsums_ready, ynT_ready, h2_ready, xf_ready = (sem(n) for n in ("rsums_ready", "ynT_ready", "h2_ready", "xf_ready"))
        route = sem("route")
        onehot_ready = sem("onehot_ready")
        place_step, place_ready = sem("place_step"), sem("place_ready")
        tab_pe, tab_dve = sem("tab_pe"), sem("tab_dve")
        eid_in = [sem(f"eid_in{i}") for i in range(NB)]
        he_in = [sem(f"he_in{i}") for i in range(NB)]
        oe_out = [sem(f"oe_out{i}") for i in range(NB)]
        he_clear = sem("he_clear")
        e_xe = sem("e_xe")
        e_xeT, e_xeTs, e_w1, e_h, e_hs, e_y, e_o, e_oid = (sem(n) for n in ("e_xeT", "e_xeTs", "e_w1", "e_h", "e_hs", "e_y", "e_o", "e_oid"))

        def moments(i, s):
            if i == 2:
                return h2[s.par][:, :, D:ROW], h2[s.par][:, :, D + 1]
            return mv[i][:], rstd[i][:]

        passed_sp, passed_pool, passed_dve = sem("passed_sp"), sem("passed_pool"), sem("passed_dve")

        def wait_alone(eng, passed_waits, semaphore, value):
            eng.wait_ge(semaphore, value)
            eng.sem_inc(passed_waits, 1)

        row = lambda v: v.rearrange("(a n) -> a n", a=1)
        LOADS = [
            (pos[:], a["pos_emb"][0:T, :].rearrange("(t p) c -> p t c", p=P)),
            (wq[:], a["wqT"].rearrange("(c p) d -> p c d", p=P)), (wk[:], a["wkT"].rearrange("(c p) d -> p c d", p=P)),
            (wv[:], a["wvT"].rearrange("(c p) d -> p c d", p=P)), (wo_a, a["woT"].rearrange("(c p) d -> p c d", p=P)),
            (bqk[:, 0:1], a["bq"]), (bqk[:, 1:2], a["bk"]), (bv1[:], a["bv"]),
            (row_bias[:, 0, :], row(a["bo"]).to_broadcast([P, D])), (row_bias[:, 1, :], row(a["bo2"]).to_broadcast([P, D])),
            (gamma[:, 0, :], row(a["gamma"]).to_broadcast([P, D])), (gamma[:, 1, :], row(a["gamma"]).to_broadcast([P, D])),
            (beta[:, 0, :], row(a["beta"]).to_broadcast([P, D])), (beta[:, 1, :], row(a["beta"]).to_broadcast([P, D])),
            (wq2[:], a["wq2T"].rearrange("(c p) d -> p c d", p=P)), (wk2[:], a["wk2T"].rearrange("(c p) d -> p c d", p=P)),
            (wv2[:], a["wv2T"].rearrange("(c p) d -> p c d", p=P)), (wo2[:], a["wo2T"].rearrange("(c p) d -> p c d", p=P)),
            (bqk2[:, 0, :], a["bq2"]), (bqk2[:, 1, :], a["bk2"]), (bv2[:], a["bv2"]),
            (router[:], a["routerT"].rearrange("(c p) e -> p c e", p=P)),
            (router_b[:, 0, :], row(a["router_b"]).to_broadcast([P, E])), (router_b[:, 1, :], row(a["router_b"]).to_broadcast([P, E])),
        ]
        EXPERT_LOADS = [(w1[:, :, c * HID:(c + 1) * HID], a["w1"][:, c * P:(c + 1) * P, :].rearrange("e p m -> p e m"))
                        for c in range(CC)]
        EXPERT_LOADS += [(w1[0:HID, :, CC * HID:], a["b1T"].rearrange("m (e a) -> m e a", a=1)),
                         (w2[0:HID, :, :], a["w2"].rearrange("e m d -> m e d")), (w2[HID:HID + 1, :, :], a["b2"].rearrange("(a e) d -> a e d", a=1))]
        ALL_LOADED = 16 * len(LOADS)
        EXPERTS_LOADED = 16 * len(EXPERT_LOADS)
        POOL_CONST = 19
        DVE_CONST = NH + 6

        block = ctx.enter_context(nc.Block())

        @block.sync
        def _(sp):
            for dst, src in LOADS:
                sp.dma_start(dst, src).then_inc(loaded, 16)
            sp.wait_ge(pool_const, POOL_CONST)
            for dst, src in EXPERT_LOADS:
                sp.dma_start(dst, src, allow_slow_non_contiguous=True).then_inc(experts_loaded, 16)
            for i in range(LIST // (P * 256)):
                sp.dma_start(lists[i * P * 256:(i + 1) * P * 256, :].rearrange("(p n) a -> p (n a)", p=P),
                             sentinel).then_inc(lists_clear, 16)

            def load_ids(s):
                sp.wait_ge(pool_const, POOL_CONST)
                if later(s, 2):
                    sp.wait_ge(rows_in[s.par], 32 * s.pair)
                sp.dma_start(ids[s.par][:], a["ids"][bass.ds(s.n, 1), :, :].rearrange("a p t -> (a p) t")
                             ).then_inc(ids_in[s.par], 16)

            def stack(s):
                sp.wait_ge(pool_const, POOL_CONST)
                if later(s, 2):
                    sp.wait_ge(scores_done, NH * (s.n - 1))
                for p, made in enumerate((part1_ready, part2_ready, part3_ready)):
                    for i, dst, which in ((0, qst, QPART), (1, kst, KPART)):
                        wait_alone(sp, passed_sp, made, 2 * s.n + i + 1)
                        for b in range(PARTS):
                            if which[b] == p:
                                sp.dma_start(dst[s.par][DH * b:DH * (b + 1), :, :], part[i][:, p, :, :]
                                             ).then_inc(stacked[s.par], 16)

            def store_h2(s):
                sp.wait_ge(pool_const, POOL_CONST)
                sp.wait_ge(rstd_ready[2], s.n + 1)
                sp.dma_start(hidden[bass.ds(s.n * T, T), :].rearrange("(t p) c -> p t c", p=P), h2[s.par][:]
                             ).then_inc(h2_out[s.par], 16)

            run_iterations(sp, "SP", dict(ids=load_ids, stack=stack, store=store_h2))

            sp.wait_ge(tab_dve, 4)
            for i in range(2):
                sp.wait_ge(placed[i], 32 * (NS // 2))
                sp.wait_ge(h2_out[i], 16 * (NS // 2))

            def load_tile(i, b):
                at = sp.value_load(table[0:1, 1, bass.ds(i, 1)], min_val=0, max_val=LIST - P)
                sp.dma_start(eid[b], lists[bass.ds(at, P), :]).then_inc(eid_in[b], 16)

            for b in range(NB):
                load_tile(b, b)
            with sp.Fori(0, MTILES // NB - 1) as r:
                for b in range(NB):
                    sp.wait_ge(pool_const, POOL_CONST)
                    sp.wait_ge(e_oid, NB * r + b + 1)
                    sp.wait_ge(he_in[b], 16 * (r + 1))
                    load_tile(NB * r + b + NB, b)

        @block.gpsimd
        def _(pool):
            g = nc.gpsimd
            g.memset(ident[:], 0.0).then_inc(pool_const, 1)
            g.memset(tri[:], 1.0).then_inc(pool_const, 1)
            g.memset(tri_inc[:], 1.0).then_inc(pool_const, 1)
            g.iota(rel[:, 0:P], [[1, P]], base=0, channel_multiplier=-1, allow_small_or_imprecise_dtypes=True).then_inc(pool_const, 1)
            g.iota(rel[:, P:3 * P], [[1, 2 * P]], base=-P, channel_multiplier=-1, allow_small_or_imprecise_dtypes=True).then_inc(pool_const, 1)
            pool.wait_ge(pool_const, 5)
            g.affine_select(out=ident[:], in_=ident[:], compare_op=ALU.not_equal, fill=1.0, base=0,
                            pattern=[[-1, P]], channel_multiplier=1).then_inc(pool_const, 1)
            g.affine_select(out=tri[:], in_=tri[:], compare_op=ALU.is_gt, fill=0.0, base=0,
                            pattern=[[1, P]], channel_multiplier=-1).then_inc(pool_const, 1)
            g.affine_select(out=tri_inc[:], in_=tri_inc[:], compare_op=ALU.is_ge, fill=0.0, base=0,
                            pattern=[[1, E]], channel_multiplier=-1).then_inc(pool_const, 1)
            g.affine_select(out=rel[:, 0:P], in_=rel[:, 0:P], compare_op=ALU.is_ge, fill=MASKED, base=0,
                            pattern=[[-1, P]], channel_multiplier=1).then_inc(pool_const, 1)
            g.affine_select(out=rel[:, P:3 * P], in_=rel[:, P:3 * P], compare_op=ALU.is_ge, fill=MASKED, base=P,
                            pattern=[[-1, 2 * P]], channel_multiplier=1).then_inc(pool_const, 1)
            g.memset(minus_half[:], -0.5).then_inc(pool_const, 1)
            g.memset(sentinel, NTOK).then_inc(pool_const, 1)
            g.memset(w1[:, :, CC * HID:], 0.0).then_inc(pool_const, 1)
            g.iota(rev[:], [[0, TT], [-1, E]], base=E, channel_multiplier=0, allow_small_or_imprecise_dtypes=True).then_inc(pool_const, 1)
            g.iota(base[:], [[NTOK // P, E]], base=0, channel_multiplier=0, allow_small_or_imprecise_dtypes=True).then_inc(pool_const, 1)
            for i in range(2):
                g.iota(number[i][:], [[P, TT]], base=i * T, channel_multiplier=1).then_inc(pool_const, 1)
            g.iota(two_sequences[:], [[0, TT]], base=2 * T, channel_multiplier=0).then_inc(pool_const, 1)
            g.iota(iota_t[:], [[1, MTILES]], base=0, channel_multiplier=0, allow_small_or_imprecise_dtypes=True).then_inc(pool_const, 1)
            pool.wait_ge(loaded, ALL_LOADED)
            pool.wait_ge(dve_const, DVE_CONST)
            pool.wait_ge(lists_clear, 16 * (LIST // (P * 256)))

            def gather(s):
                if later(s, 2):
                    pool.wait_ge(xT_done, s.n - 1)
                    pool.wait_ge(xb_ready, s.n - 1)
                wait_alone(pool, passed_pool, ids_in[s.par], 16 * (s.pair + 1))
                for t in range(TT):
                    g.indirect_dma_start(out=x[s.par][:, t, :], out_offset=None, in_=a["tok_emb"],
                                         in_offset=bass.IndirectOffsetOnAxis(ap=ids[s.par][:, t:t + 1], axis=0)
                                         ).then_inc(rows_in[s.par], 16)

            def embed(s):
                pool.wait_ge(rows_in[s.par], 32 * (s.pair + 1))
                g.tensor_tensor(x[s.par][:], x[s.par][:], pos[:], ALU.add).then_inc(x_ready, 1)
                pool.wait_ge(x_ready, s.n + 1)
                if later(s):
                    pool.wait_ge(h0_ready, s.n)
                g.tensor_tensor(xb[:], x[s.par][:], tok_bias[:], ALU.add).then_inc(xb_ready, 1)

            def rstd_of(i):
                def f(s):
                    wait_alone(pool, passed_pool, mv_ready[i], s.n + 1)
                    g.tensor_scalar(ve[i][:], moments(i, s)[0][:, :, 1], EPS, None, ALU.add).then_inc(ve_ready[i], 1)
                    pool.wait_ge(ve_ready[i], s.n + 1)
                    g.tensor_tensor(moments(i, s)[1], ve[i][:], minus_half[:], ALU.pow).then_inc(rstd_ready[i], 1)
                return f

            def affine(s):
                pool.wait_ge(xhat_ready, s.n + 1)
                g.tensor_tensor(xg[:], xhat[:], gamma[:], ALU.mult).then_inc(xg_ready, 1)
                pool.wait_ge(xg_ready, s.n + 1)
                if later(s):
                    pool.wait_ge(xn_ready, s.n)
                    pool.wait_ge(h1b_ready, s.n)
                g.tensor_tensor(h1[:], xg[:], beta[:], ALU.add).then_inc(h1_ready, 1)

            def residual(s):
                pool.wait_ge(h1_ready, s.n + 1)
                if later(s, 2):
                    pool.wait_ge(h2_ready, s.n - 1)
                g.tensor_tensor(h1b[s.par][:], h1[:], attn_bias[:], ALU.add).then_inc(h1b_ready, 1)

            def split(s):
                for i in range(2):
                    if later(s):
                        pool.wait_ge(stacked[1 - s.par], 192 * (s.pair + s.par))
                    wait_alone(pool, passed_pool, rest_ready, 2 * s.n + i + 1)
                    g.tensor_copy(part[i][:, 1, :, :], rest[i][:]).then_inc(part2_ready, 1)
                    pool.wait_ge(part2_ready, 2 * s.n + i + 1)
                    g.tensor_tensor(part[i][:, 2, :, :], rest[i][:], part[i][:, 1, :, :], ALU.subtract).then_inc(part3_ready, 1)

            def recip(s):
                if later(s):
                    pool.wait_ge(rT_done, s.n)
                wait_alone(pool, passed_pool, rsums_ready, s.n + 1)
                g.tensor_copy(rexp[:].rearrange("p t (h d) -> p t h d", d=DH),
                              rsums[:, :, :, None].to_broadcast([P, TT, NH, DH])).then_inc(rexp_ready, 1)

            def rank(s):
                pool.wait_ge(rank_done, s.n + 1)
                g.tensor_tensor(acc[:], acc[:], onehot[:, 0, :], ALU.add).then_inc(acc_half, 1)
                pool.wait_ge(acc_half, s.n + 1)
                g.tensor_tensor(acc[:], acc[:], onehot[:, 1, :], ALU.add).then_inc(acc_ready, 1)

            def place(s):
                pool.wait_ge(place_ready, s.n + 1)
                if later(s, 2):
                    pool.wait_ge(placed[s.par], 32 * s.pair)
                    g.tensor_tensor(number[s.par][:], number[s.par][:], two_sequences[:], ALU.add).then_inc(number_ready, 1)
                    wait_alone(pool, passed_pool, number_ready, s.n - 1)
                for t in range(TT):
                    g.indirect_dma_start(out=lists[:, :], out_offset=bass.IndirectOffsetOnAxis(ap=place_i[s.par][:, t:t + 1], axis=0),
                                         in_=number[s.par][:, t:t + 1], in_offset=None).then_inc(placed[s.par], 16)

            run_iterations(pool, "Pool", dict(gather=gather, embed=embed, rstd1=rstd_of(0), rstd2=rstd_of(1), rstd3=rstd_of(2), affine=affine,
                                      residual=residual, split=split, recip=recip, rank=rank, place=place))

            def fetch(i, b, turn):
                if isinstance(i, int) and i < NB:
                    pool.wait_ge(he_clear, NB)
                else:
                    pool.wait_ge(e_o, i - NB + 1)
                wait_alone(pool, passed_pool, eid_in[b], 16 * (turn + 1))
                g.indirect_dma_start(out=he[b], out_offset=None, in_=hidden[:, :],
                                     in_offset=bass.IndirectOffsetOnAxis(ap=eid[b], axis=0),
                                     bounds_check=NTOK - 1, oob_is_err=False).then_inc(he_in[b], 16)

            def send(i, b):
                wait_alone(pool, passed_pool, e_o, i + 1)
                g.indirect_dma_start(out=out, out_offset=bass.IndirectOffsetOnAxis(ap=oid[b], axis=0),
                                     in_=oe[b], in_offset=None, bounds_check=NTOK - 1, oob_is_err=False).then_inc(oe_out[b], 16)

            FETCH = 5

            def step(r, u):
                fetch(NB * r + u + FETCH, (u + FETCH) % NB, r + (u + FETCH) // NB)
                send(NB * r + u, u)

            for i in range(FETCH):
                fetch(i, i, 0)
            for u in range(NB):
                step(0, u)
            with pool.Fori(1, MTILES // NB - 1) as r:
                for u in range(NB):
                    step(r, u)
            for u in range(NB - FETCH):
                step(MTILES // NB - 1, u)
            for i in range(MTILES - FETCH, MTILES):
                send(i, i % NB)
            for b in range(NB):
                pool.wait_ge(oe_out[b], 16 * (MTILES // NB))

        @block.scalar
        def _(act):
            s_ = nc.scalar
            act.wait_ge(loaded, ALL_LOADED)
            act.wait_ge(dve_const, DVE_CONST)

            def embed_turn(s):
                act.wait_ge(xT_done, s.n + 1)
                if later(s):
                    act.wait_ge(v_done, s.n)
                s_.activation(xT[:].rearrange("p c t -> p (c t)"), ps_a[:], ACT.Copy).then_inc(xT_ready, 1)

            def tok_qkv(s):
                act.wait_ge(qk_done, s.n + 1)
                if later(s):
                    act.wait_ge(s1_done, s.n)
                s_.activation(qkT[:, 0, :], ps_b[:, 0:T], ACT.Identity, bias=bq_scaled[:, 0:1], scale=DK ** -0.5).then_inc(q_ready, 1)

            def tok_softmax(s):
                act.wait_ge(nmax1_ready, s.n + 1)
                if later(s):
                    act.wait_ge(pT1_done, s.n)
                    act.wait_ge(rsum1_ready, s.n)
                for t in range(TT):
                    last = s_.activation(p1[:, t, :], ps_b[:, t * T:(t + 1) * T], ACT.Exp, bias=nmax1[:, t:t + 1],
                                         accum_out=sum1[:, t:t + 1])
                last.then_inc(p1_ready, 1)

            def tok_turn(s):
                act.wait_ge(pT1_done, s.n + 1)
                if later(s):
                    act.wait_ge(head_done, s.n)
                s_.activation(pT1[:].rearrange("p c t -> p (c t)"), ps_a[:], ACT.Copy).then_inc(pT1_ready, 1)

            def norm_turn(s):
                act.wait_ge(xnT_done, s.n + 1)
                if later(s):
                    act.wait_ge(V_done, s.n)
                s_.activation(xnT[:].rearrange("p c t -> p (c t)"), ps_b[:], ACT.Copy).then_inc(xnT_ready, 1)

            def project_qk(s):
                for i, (done, ps) in enumerate(((Q_done, ps_a), (K_done, ps_b))):
                    act.wait_ge(done, s.n + 1)
                    if later(s):
                        act.wait_ge(stacked[1 - s.par], 192 * (s.pair + s.par))
                        act.wait_ge(part3_ready, 2 * s.n)
                    for gr in range(2):
                        last = s_.activation(part[i][:, 0, gr, :], ps[:, gr * T:(gr + 1) * T], ACT.Identity,
                                             bias=bqk2[:, i, gr:gr + 1])
                    last.then_inc(part1_ready, 1)

            def project_v(s):
                act.wait_ge(V_done, s.n + 1)
                if later(s, 2):
                    act.wait_ge(mix_done, NH * (s.n - 1))
                for odd in range(2):
                    last = s_.activation(vpad[s.par][:, :, :, 48 * odd:48 * odd + DH],
                                         ps_a[:].rearrange("p (t h o d) -> p t h o d", t=TT, o=2, d=DH)[:, :, :, odd, :], ACT.Copy)
                last.then_inc(vpad_ready, 1)

            def weights(s, h):
                act.wait_ge(sc_ready, NH * s.n + h + 1)
                if later(s) or h >= 2:
                    act.wait_ge(turn_done, NH * s.n + h - 1)
                for t in range(TT):
                    c0, c1 = (0, P) if t == 0 else (P, 3 * P)
                    last = s_.activation(pr[h % 2][:, c0:c1], sc[h % 2][:, c0:c1], ACT.Exp, bias=nmax[:, h % 2, t:t + 1],
                                         scale=-1.0, accum_out=sums[s.par][:, t, h:h + 1])
                last.then_inc(pr_ready, 1)

            def evacuate(s, h):
                if h % 2 == 0:
                    return
                act.wait_ge(turn_done, NH * s.n + h + 1)
                if later(s) or h >= 2:
                    act.wait_ge(mix_done, NH * s.n + h - 1)
                s_.activation(prT[1][:], ps_t[1][:, 0:3 * P], ACT.Copy).then_inc(prT_odd, 1)

            def take_mix(s):
                act.wait_ge(mix_done, NH * s.n + NH)
                if later(s):
                    act.wait_ge(ynT_ready, s.n)
                s_.activation(yT[:].rearrange("p g t -> p (g t)"), ps_y[:], ACT.Copy).then_inc(yT_ready, 1)

            def router_turn(s):
                act.wait_ge(xfT_done, s.n + 1)
                if later(s):
                    act.wait_ge(logits_done, s.n)
                s_.activation(xfT[:].rearrange("p c t -> p (c t)"), ps_c[:], ACT.Copy).then_inc(xfT_ready, 1)

            run_iterations(act, "ACT", dict(embed_turn=embed_turn, tok_qkv=tok_qkv, tok_softmax=tok_softmax, tok_turn=tok_turn,
                                     norm_turn=norm_turn, project_qk=project_qk, project_v=project_v, weights=weights,
                                     evacuate=evacuate, take_mix=take_mix, router_turn=router_turn))

            act.wait_ge(tab_dve, 4)
            act.wait_ge(experts_loaded, EXPERTS_LOADED)

            def turned(i, b):
                e = act.value_load(table[0:1, 0, bass.ds(i, 1)], min_val=0, max_val=E - 1)
                if not isinstance(i, int) or i >= 2:
                    act.wait_ge(e_hs, i - 1)
                s_.activation(w1e[b][:, None, :], w1[:, bass.ds(e, 1), :], ACT.Copy).then_inc(e_w1, 1)
                act.wait_ge(e_xeT, i + 1)
                s_.activation(xeT[b][:].rearrange("p c t -> p (c t)"), ps_s[b][:, 0:D], ACT.Copy).then_inc(e_xeTs, 1)

            def hidden_relu(i, b):
                act.wait_ge(e_h, i + 1)
                if not isinstance(i, int) or i >= 2:
                    act.wait_ge(e_y, i - 1)
                act.wait_ge(e_w1, i + 1)
                s_.activation(hT[b][0:HID, :], ps_t[b][0:HID, 0:P], ACT.Relu, bias=w1e[b][0:HID, CC * HID:]).then_inc(e_hs, 1)

            def step(i, b):
                turned(i + 1, 1 - b)
                hidden_relu(i, b)

            turned(0, 0)
            step(0, 0)
            step(1, 1)
            with act.Fori(1, MTILES // 2 - 1) as r:
                step(2 * r, 0)
                step(2 * r + 1, 1)
            step(MTILES - 2, 0)
            hidden_relu(MTILES - 1, 1)

        @block.vector
        def _(dve):
            v = nc.vector
            dve.wait_ge(loaded, ALL_LOADED)
            dve.wait_ge(pool_const, POOL_CONST)
            for h in range(NH):
                v.tensor_scalar(alibi[:, h, :], rel, slopes[h], 4.0, ALU.mult, ALU.mult).then_inc(dve_const, 1)
            v.tensor_tensor(wo[:], wo_a[:, 0, :], wo_a[:, 1, :], ALU.add).then_inc(dve_const, 1)
            v.tensor_scalar(bq_scaled[:], bqk[:, 0:1], DK ** -0.5, None, ALU.mult).then_inc(dve_const, 1)
            for i, col in enumerate((bv1[:, 0:1], bv2[:, 0:1], bv2[:, 1:2])):
                v.tensor_copy(bv_rep[:, i, :], col.to_broadcast([P, P]))
            v.memset(ones[:], 1.0)
            v.memset(acc[:], 0.0)
            v.memset(ones_col[:], 1.0)
            for i in range(2):
                v.memset(vpad[i][:], 0.0)
            v.memset(sums[0][:], 0.0).then_inc(dve_const, 1)
            dve.wait_ge(pe_const, 1)
            for i, dst in enumerate((tok_bias, attn_bias)):
                for t in range(TT):
                    last = v.tensor_tensor(dst[:, t, :], ps_c[:, i * D:(i + 1) * D], row_bias[:, i, :], ALU.add)
                last.then_inc(dve_const, 1)
            v.memset(sums[1][:], 0.0).then_inc(dve_const, 1)

            def tok_qkv(s):
                dve.wait_ge(qk_done, s.n + 1)
                if later(s):
                    dve.wait_ge(s1_done, s.n)
                dve.wait_ge(q_ready, s.n + 1)
                v.tensor_scalar(qkT[:, 1, :], ps_b[:, T:2 * T], bqk[:, 1:2], None, ALU.add).then_inc(k_ready, 1)
                dve.wait_ge(v_done, s.n + 1)
                if later(s):
                    dve.wait_ge(head_done, s.n)
                v.tensor_copy(v1[:].rearrange("p t d -> p (t d)"), ps_a[:, 0:TT * DK]).then_inc(v_ready, 1)

            def tok_softmax(s):
                dve.wait_ge(s1_done, s.n + 1)
                if later(s):
                    dve.wait_ge(p1_ready, s.n)
                v.tensor_reduce(nmax1[:], ps_b[:].rearrange("p (t k) -> p t k", t=TT), AX.X, ALU.max, negate=True).then_inc(nmax1_ready, 1)

            def tok_turn(s):
                dve.wait_ge(p1_ready, s.n + 1)
                v.reciprocal(rsum1[:], sum1[:]).then_inc(rsum1_ready, 1)

            def tok_mix(s):
                dve.wait_ge(head_done, s.n + 1)
                if later(s):
                    dve.wait_ge(out1_done, s.n)
                v.tensor_copy(headT[:], ps_b[:, 0:T]).then_inc(head_ready, 1)

            def tok_out(s):
                dve.wait_ge(out1_done, s.n + 1)
                dve.wait_ge(xb_ready, s.n + 1)
                dve.wait_ge(rsum1_ready, s.n + 1)
                for t in range(TT):
                    last = v.scalar_tensor_tensor(out=h0[:, t, :], in0=ps_a[:, t * D:(t + 1) * D], scalar=rsum1[:, t:t + 1],
                                                  in1=xb[:, t, :], op0=ALU.mult, op1=ALU.add)
                last.then_inc(h0_ready, 1)

            def stats(i, src, s):
                for t in range(TT):
                    last = v.bn_stats(bn[i][:, t, :], src[:, t, 0:D])
                last.then_inc(bn_ready[i], 1)
                wait_alone(dve, passed_dve, bn_ready[i], s.n + 1)
                for t in range(TT):
                    last = v.bn_aggr(moments(i, s)[0][:, t, :], bn[i][:, t, :])
                last.then_inc(mv_ready[i], 1)

            def normalize(i, dst, src, s):
                mean, scale = moments(i, s)
                for t in range(TT):
                    last = v.tensor_scalar(dst[:, t, :], src[:, t, 0:D], mean[:, t, 0:1], scale[:, t:t + 1], ALU.subtract, ALU.mult)
                return last

            def stats1(s):
                dve.wait_ge(h0_ready, s.n + 1)
                if later(s):
                    dve.wait_ge(rstd_ready[0], s.n)
                stats(0, h0, s)

            def norm1(s):
                dve.wait_ge(rstd_ready[0], s.n + 1)
                if later(s):
                    dve.wait_ge(xg_ready, s.n)
                normalize(0, xhat, h0, s).then_inc(xhat_ready, 1)

            def stats2(s):
                dve.wait_ge(h1_ready, s.n + 1)
                stats(1, h1, s)

            def norm2(s):
                dve.wait_ge(rstd_ready[1], s.n + 1)
                if later(s):
                    dve.wait_ge(xnT_done, s.n)
                normalize(1, xn, h1, s).then_inc(xn_ready, 1)

            def project_qk(s):
                for i, ps in enumerate((ps_a, ps_b)):
                    dve.wait_ge(part1_ready, 2 * s.n + i + 1)
                    if later(s):
                        dve.wait_ge(part3_ready, 2 * s.n)
                    for gr in range(2):
                        last = v.scalar_tensor_tensor(out=rest[i][:, gr, :], in0=ps[:, gr * T:(gr + 1) * T],
                                                      scalar=bqk2[:, i, gr:gr + 1], in1=part[i][:, 0, gr, :],
                                                      op0=ALU.add, op1=ALU.subtract)
                    last.then_inc(rest_ready, 1)

            def weights(s, h):
                if later(s) or h >= 2:
                    dve.wait_ge(pr_ready, NH * s.n + h - 1)
                wait_alone(dve, passed_dve, scores_done, NH * s.n + h + 1)
                for t in range(TT):
                    c0, c1 = (0, P) if t == 0 else (P, 3 * P)
                    last = v.tensor_tensor_reduce(out=sc[h % 2][:, c0:c1], in0=ps_s[h % 2][:, c0:c1], in1=alibi[:, h, c0:c1],
                                                  scale=-(DH ** -0.5), scalar=3e38, op0=ALU.add, op1=ALU.min,
                                                  accum_out=nmax[:, h % 2, t:t + 1])
                last.then_inc(sc_ready, 1)

            def evacuate(s, h):
                if h % 2:
                    return
                dve.wait_ge(turn_done, NH * s.n + h + 1)
                if later(s) or h >= 2:
                    dve.wait_ge(mix_done, NH * s.n + h - 1)
                v.tensor_copy(prT[0][:], ps_t[0][:, 0:3 * P]).then_inc(prT_even, 1)

            def recip(s):
                dve.wait_ge(pr_ready, NH * s.n + NH)
                if later(s):
                    dve.wait_ge(rexp_ready, s.n)
                v.reciprocal(rsums[:], sums[s.par][:]).then_inc(rsums_ready, 1)

            def scale_mix(s):
                dve.wait_ge(rT_done, s.n + 1)
                dve.wait_ge(yT_ready, s.n + 1)
                if later(s):
                    dve.wait_ge(out2_done, s.n)
                v.tensor_tensor(ynT[:].rearrange("p g t -> p (g t)"), yT[:].rearrange("p g t -> p (g t)"), ps_c[:], ALU.mult).then_inc(ynT_ready, 1)

            def stats3(s):
                dve.wait_ge(out2_done, s.n + 1)
                dve.wait_ge(h1b_ready, s.n + 1)
                if later(s, 2):
                    dve.wait_ge(h2_out[s.par], 16 * s.pair)
                v.tensor_tensor(h2[s.par][:, :, 0:D], ps_c[:].rearrange("p (t c) -> p t c", t=TT), h1b[s.par][:],
                                ALU.add).then_inc(h2_ready, 1)
                dve.wait_ge(h2_ready, s.n + 1)
                stats(2, h2[s.par], s)

            def norm3(s):
                dve.wait_ge(rstd_ready[2], s.n + 1)
                if later(s):
                    dve.wait_ge(xfT_done, s.n)
                normalize(2, xf, h2[s.par], s).then_inc(xf_ready, 1)

            def choose(s):
                dve.wait_ge(logits_done, s.n + 1)
                wide = [P, TT, E]
                v.tensor_tensor(lg[:].rearrange("p t e -> p (t e)"), ps_c[:, 0:TT * E], router_b[:].rearrange("p t e -> p (t e)"),
                                ALU.add).then_inc(route, 1)
                dve.wait_ge(route, 5 * s.n + 1)
                v.tensor_reduce(top[:], lg[:], AX.X, ALU.max).then_inc(route, 1)
                dve.wait_ge(route, 5 * s.n + 2)
                v.tensor_tensor(eq[:], lg[:], top[:, :, None].to_broadcast(wide), ALU.is_equal).then_inc(route, 1)
                dve.wait_ge(route, 5 * s.n + 3)
                v.tensor_tensor(onehot_f[:], eq[:], rev[:], ALU.mult).then_inc(route, 1)
                dve.wait_ge(route, 5 * s.n + 4)
                v.tensor_reduce(best[:], onehot_f[:], AX.X, ALU.max).then_inc(route, 1)
                dve.wait_ge(route, 5 * s.n + 5)
                if later(s):
                    dve.wait_ge(acc_ready, s.n)
                v.tensor_tensor(onehot[:], rev[:], best[:, :, None].to_broadcast(wide), ALU.is_equal).then_inc(onehot_ready, 1)

            def place(s):
                dve.wait_ge(rank_done, s.n + 1)
                if later(s, 2):
                    dve.wait_ge(placed[s.par], 32 * s.pair)
                v.tensor_tensor(place_m[:].rearrange("p t e -> p (t e)"), ps_c[:, 0:TT * E], onehot[:].rearrange("p t e -> p (t e)"),
                                ALU.mult).then_inc(place_step, 1)
                dve.wait_ge(place_step, 2 * s.n + 1)
                v.tensor_reduce(place_f[:], place_m[:], AX.X, ALU.add).then_inc(place_step, 1)
                dve.wait_ge(place_step, 2 * s.n + 2)
                v.tensor_copy(place_i[s.par][:], place_f[:]).then_inc(place_ready, 1)

            run_iterations(dve, "DVE", dict(tok_qkv=tok_qkv, tok_softmax=tok_softmax, tok_turn=tok_turn, tok_mix=tok_mix, tok_out=tok_out,
                                     stats1=stats1, norm1=norm1, stats2=stats2, norm2=norm2, project_qk=project_qk, weights=weights,
                                     evacuate=evacuate, recip=recip, scale_mix=scale_mix, stats3=stats3, norm3=norm3, choose=choose,
                                     place=place))

            for i in range(NB):
                v.memset(he[i], 0.0).then_inc(he_clear, 1)
            for i in range(2):
                v.memset(hT[i][HID:HID + 1, :], 1.0)
            dve.wait_ge(tab_pe, 1)
            v.tensor_copy(count[:], ps_c[0:E, 0:1]).then_inc(tab_dve, 1)
            dve.wait_ge(tab_dve, 1)
            v.tensor_scalar(below, iota_t[:, 0:NTILE], float(P), count[:, 0:1], ALU.mult, ALU.is_lt).then_inc(route, 1)
            dve.wait_ge(route, 5 * NS + 1)
            v.tensor_reduce(ntiles[:], below, AX.X, ALU.add).then_inc(tab_dve, 1)
            dve.wait_ge(tab_pe, 2)
            v.tensor_copy(cum[:], ps_c[0:E, 1:2]).then_inc(route, 1)
            dve.wait_ge(route, 5 * NS + 2)
            v.tensor_scalar(passed, iota_t[:], cum[:, 0:1], None, ALU.is_ge).then_inc(tab_dve, 1)
            dve.wait_ge(tab_pe, 3)
            experts, skipped = ps_c[0:1, 0:MTILES], ps_c[0:1, MTILES:2 * MTILES]
            v.scalar_tensor_tensor(out=tab_f[:, 0, :], in0=experts, scalar=float(NTOK // P), in1=iota_t[0:1, :],
                                   op0=ALU.mult, op1=ALU.add)
            v.tensor_scalar(tab_f[:, 1, :], experts, float(E - 1), None, ALU.min)
            v.tensor_copy(tab_f[:, 2, :], skipped).then_inc(route, 1)
            dve.wait_ge(route, 5 * NS + 3)
            v.tensor_tensor(tab_f[:, 3, :], tab_f[:, 0, :], tab_f[:, 2, :], ALU.subtract).then_inc(route, 1)
            dve.wait_ge(route, 5 * NS + 4)
            v.tensor_copy(table[:, 0, :], tab_f[:, 1, :])
            v.tensor_scalar(table[:, 1, :], tab_f[:, 3, :], float(P), None, ALU.mult).then_inc(tab_dve, 1)

            def e_take(i, b, turn):
                dve.wait_ge(he_in[b], 16 * (turn + 1))
                if not isinstance(turn, int) or turn:
                    dve.wait_ge(oe_out[b], 16 * turn)
                v.tensor_copy(oid[b], eid[b]).then_inc(e_oid, 1)
                if not isinstance(i, int) or i >= 2:
                    dve.wait_ge(e_xeT, i - 1)
                v.tensor_scalar(xe[b % 2], he[b][:, 0:D], he[b][:, D:D + 1], he[b][:, D + 1:ROW], ALU.subtract, ALU.mult).then_inc(e_xe, 1)

            def e_out(i, b):
                dve.wait_ge(e_y, i + 1)
                v.scalar_tensor_tensor(out=oe[b], in0=(ps_a, ps_b)[b % 2][:, 0:D], scalar=0.0, in1=he[b][:, 0:D],
                                       op0=ALU.max, op1=ALU.add).then_inc(e_o, 1)

            TAKE = 3

            def step(r, u):
                e_take(NB * r + u + TAKE, (u + TAKE) % NB, r + (u + TAKE) // NB)
                e_out(NB * r + u, u)

            for i in range(TAKE):
                e_take(i, i, 0)
            for u in range(NB):
                step(0, u)
            with dve.Fori(1, MTILES // NB - 1) as r:
                for u in range(NB):
                    step(r, u)
            for u in range(NB - TAKE):
                step(MTILES // NB - 1, u)
            for i in range(MTILES - TAKE, MTILES):
                e_out(i, i % NB)

        @block.tensor
        def _(pe):
            m = nc.tensor
            pe.wait_ge(loaded, ALL_LOADED)
            pe.wait_ge(dve_const, NH + 3)
            m.matmul(ps_c[:, 0:D], bv_rep[:, 0, :], wo[:], start=True, stop=True)
            m.matmul(ps_c[:, D:2 * D], bv_rep[:, 1, :], wo2[:, 0, :], start=True, stop=False)
            m.matmul(ps_c[:, D:2 * D], bv_rep[:, 2, :], wo2[:, 1, :], start=False, stop=True).then_inc(pe_const, 1)
            pe.wait_ge(dve_const, DVE_CONST)

            def turn_tokens(dst, src):
                for c in range(CC):
                    for t in range(TT):
                        last = m.transpose(dst[:, c * T + t * P:c * T + (t + 1) * P], src[:, t, c * P:(c + 1) * P], ident[:])
                return last

            def by_channel(dst, w, xt):
                for c in range(CC):
                    last = m.matmul(dst, w[c], xt[:, c, :], start=(c == 0), stop=(c == CC - 1))
                return last

            def by_token(dst, xt, w, n):
                for t in range(TT):
                    for c in range(CC):
                        last = m.matmul(dst[:, t * n:(t + 1) * n], xt[:, c, t * P:(t + 1) * P], w[:, c, :],
                                        start=(c == 0), stop=(c == CC - 1))
                return last

            def embed_turn(s):
                pe.wait_ge(x_ready, s.n + 1)
                if later(s, 2):
                    pe.wait_ge(vpad_ready, s.n - 1)
                if later(s):
                    pe.wait_ge(h0_ready, s.n)
                turn_tokens(ps_a, x[s.par]).then_inc(xT_done, 1)

            def tok_qkv(s):
                pe.wait_ge(xT_ready, s.n + 1)
                if later(s, 2):
                    pe.wait_ge(rest_ready, 2 * s.n - 2)
                by_channel(ps_b[:, 0:T], [wq[:, c, :] for c in range(CC)], xT)
                by_channel(ps_b[:, T:2 * T], [wk[:, c, :] for c in range(CC)], xT).then_inc(qk_done, 1)
                by_token(ps_a, xT, wv, DK).then_inc(v_done, 1)

            def tok_scores(s):
                pe.wait_ge(q_ready, s.n + 1)
                pe.wait_ge(k_ready, s.n + 1)
                for t in range(TT):
                    last = m.matmul(ps_b[:, t * T:(t + 1) * T], qkT[:, 0, t * P:(t + 1) * P], qkT[:, 1, :], start=True, stop=True)
                last.then_inc(s1_done, 1)

            def tok_turn(s):
                pe.wait_ge(p1_ready, s.n + 1)
                pe.wait_ge(v_ready, s.n + 1)
                turn_tokens(ps_a, p1).then_inc(pT1_done, 1)

            def tok_mix(s):
                pe.wait_ge(pT1_ready, s.n + 1)
                by_channel(ps_b[:, 0:T], [v1[:, t, :] for t in range(TT)], pT1).then_inc(head_done, 1)

            def tok_out(s):
                pe.wait_ge(head_ready, s.n + 1)
                for t in range(TT):
                    last = m.matmul(ps_a[:, t * D:(t + 1) * D], headT[:, t * P:(t + 1) * P], wo[:], start=True, stop=True)
                last.then_inc(out1_done, 1)

            def norm_turn(s):
                pe.wait_ge(xn_ready, s.n + 1)
                pe.wait_ge(head_ready, next_or_last(s))
                turn_tokens(ps_b, xn).then_inc(xnT_done, 1)

            def project_qk(s):
                pe.wait_ge(xnT_ready, s.n + 1)
                pe.wait_ge(h0_ready, next_or_last(s))
                for gr in range(2):
                    last = by_channel(ps_a[:, gr * T:(gr + 1) * T], [wq2[:, c, gr * P:(gr + 1) * P] for c in range(CC)], xnT)
                last.then_inc(Q_done, 1)
                for gr in range(2):
                    last = by_channel(ps_b[:, gr * T:(gr + 1) * T], [wk2[:, c, gr * P:(gr + 1) * P] for c in range(CC)], xnT)
                last.then_inc(K_done, 1)

            def project_v(s):
                pe.wait_ge(rest_ready, 2 * s.n + 1)
                by_token(ps_a, xnT, wv2, D).then_inc(V_done, 1)

            def scores(s, h):
                if h == 0:
                    pe.wait_ge(stacked[s.par], 192 * (s.pair + 1))
                if later(s) or h >= 2:
                    pe.wait_ge(sc_ready, NH * s.n + h - 1)
                q, k, dst = qst[s.par], kst[s.par], ps_s[h % 2]
                m.matmul(dst[:, 0:P], q[:, h, 0:P], k[:, h, 0:P], start=True, stop=True)
                m.matmul(dst[:, P:3 * P], q[:, h, P:2 * P], k[:, h, :], start=True, stop=True).then_inc(scores_done, 1)

            def turn(s, h):
                pe.wait_ge(pr_ready, NH * s.n + h + 1)
                if later(s) or h >= 2:
                    pe.wait_ge((prT_even, prT_odd)[h % 2], NH // 2 * s.n + h // 2)
                for i in range(3):
                    last = m.transpose(ps_t[h % 2][:, i * P:(i + 1) * P], pr[h % 2][:, i * P:(i + 1) * P], ident[:])
                last.then_inc(turn_done, 1)

            def mix(s, h):
                pe.wait_ge((prT_even, prT_odd)[h % 2], NH // 2 * s.n + h // 2 + 1)
                if h == 0:
                    pe.wait_ge(vpad_ready, s.n + 1)
                    if later(s):
                        pe.wait_ge(yT_ready, s.n)
                gr, quad, odd = h // 8, h % 8 // 2, h % 2
                rows = slice(32 * quad, 32 * quad + 32)
                w = vpad[s.par][:, :, h // 2, 32 * odd:32 * odd + 32]
                m.matmul(ps_y[rows, gr * T:(gr + 1) * T], w[:, 0, :], prT[h % 2][:, 0:T], start=(odd == 0), stop=False,
                         skip_group_check=True)
                m.matmul(ps_y[rows, gr * T + P:(gr + 1) * T], w[:, 1, :], prT[h % 2][:, T:3 * P], start=False, stop=(odd == 1),
                         skip_group_check=True).then_inc(mix_done, 1)

            def recip_turn(s):
                pe.wait_ge(rexp_ready, s.n + 1)
                if later(s):
                    pe.wait_ge(place_step, 2 * s.n)
                turn_tokens(ps_c, rexp).then_inc(rT_done, 1)

            def out2(s):
                pe.wait_ge(ynT_ready, s.n + 1)
                by_token(ps_c, ynT, wo2, D).then_inc(out2_done, 1)

            def router_turn(s):
                pe.wait_ge(xf_ready, s.n + 1)
                turn_tokens(ps_c, xf).then_inc(xfT_done, 1)

            def logits(s):
                pe.wait_ge(xfT_ready, s.n + 1)
                by_token(ps_c, xfT, router, E).then_inc(logits_done, 1)

            def rank(s):
                pe.wait_ge(onehot_ready, s.n + 1)
                if later(s):
                    pe.wait_ge(acc_ready, s.n)
                for t in range(TT):
                    dst = ps_c[:, t * E:(t + 1) * E]
                    m.matmul(dst, ones[:], base[:], start=True, stop=False)
                    m.matmul(dst, ones[:], acc[:], start=False, stop=False)
                    if t:
                        m.matmul(dst, ones[:], onehot[:, 0, :], start=False, stop=False)
                    last = m.matmul(dst, tri[:], onehot[:, t, :], start=False, stop=True)
                last.then_inc(rank_done, 1)

            run_iterations(pe, "PE", dict(embed_turn=embed_turn, tok_qkv=tok_qkv, tok_scores=tok_scores, tok_turn=tok_turn,
                                    tok_mix=tok_mix, tok_out=tok_out, norm_turn=norm_turn, project_qk=project_qk, project_v=project_v,
                                    scores=scores, turn=turn, mix=mix, recip_turn=recip_turn, out2=out2, router_turn=router_turn,
                                    logits=logits, rank=rank))

            pe.wait_ge(acc_ready, NS)
            pe.wait_ge(place_step, 2 * NS)
            m.matmul(ps_c[0:E, 0:1], acc[:], ones[:, 0:1], start=True, stop=True).then_inc(tab_pe, 1)
            pe.wait_ge(tab_dve, 2)
            m.matmul(ps_c[0:E, 1:2], tri_inc[:], ntiles[:], start=True, stop=True).then_inc(tab_pe, 1)
            pe.wait_ge(tab_dve, 3)
            m.matmul(ps_c[0:1, 0:MTILES], ones_col[:], passed, start=True, stop=True)
            m.matmul(ps_c[0:1, MTILES:2 * MTILES], ntiles[:], passed, start=True, stop=True).then_inc(tab_pe, 1)
            pe.wait_ge(tab_dve, 4)
            pe.wait_ge(experts_loaded, EXPERTS_LOADED)

            def e_turn(i, b):
                pe.wait_ge(e_xe, i + 1)
                if not isinstance(i, int) or i >= 2:
                    pe.wait_ge(e_xeTs, i - 1)
                for c in range(CC):
                    last = m.transpose(ps_s[b][:, c * P:(c + 1) * P], xe[b][:, c * P:(c + 1) * P], ident[:])
                last.then_inc(e_xeT, 1)

            def e_hidden(i, b):
                pe.wait_ge(e_xeTs, i + 1)
                pe.wait_ge(e_w1, i + 1)
                if not isinstance(i, int) or i >= 2:
                    pe.wait_ge(e_hs, i - 1)
                for c in range(CC):
                    last = m.matmul(ps_t[b][0:HID, 0:P], w1e[b][:, c * HID:(c + 1) * HID], xeT[b][:, c, :], start=(c == 0), stop=(c == CC - 1))
                last.then_inc(e_h, 1)

            def e_output(i, b, e):
                pe.wait_ge(e_hs, i + 1)
                if not isinstance(i, int) or i >= 2:
                    pe.wait_ge(e_o, i - 1)
                m.matmul((ps_a, ps_b)[b][:, 0:D], hT[b][:], w2[:, bass.ds(e, 1), :], start=True, stop=True).then_inc(e_y, 1)

            def expert_of(i):
                return pe.value_load(table[0:1, 0, bass.ds(i, 1)], min_val=0, max_val=E - 1)

            def step(i, b):
                e = expert_of(i - 1)
                e_turn(i + 1, 1 - b)
                e_hidden(i, b)
                e_output(i - 1, 1 - b, e)

            e_turn(0, 0)
            e_turn(1, 1)
            e_hidden(0, 0)
            step(1, 1)
            step(2, 0)
            with pe.Fori(1, (MTILES - 2) // 2) as r:
                step(2 * r + 1, 1)
                step(2 * r + 2, 0)
            e_hidden(MTILES - 1, 1)
            for i in range(MTILES - 2, MTILES):
                e_output(i, i % 2, expert_of(i))


def kernel(**inputs):
    import numpy as np
    import concourse.bacc as bacc
    from concourse.bass_utils import run_bass_kernel_spmd

    i = {k: np.asarray(v) for k, v in inputs.items()}
    tok, attn, ffn = (lambda n: i["L0_tok_" + n]), (lambda n: i["L0_attn_" + n]), (lambda n: i["L0_ffn_" + n])
    half = NH // 2

    def head_cols(w):
        return w.reshape(-1, half, 2, DH).transpose(0, 2, 3, 1).reshape(-1, D)

    arrays = {
        "ids": i["x"].reshape(NS, TT, P).transpose(0, 2, 1),
        "tok_emb": tok("tok_emb"), "pos_emb": tok("pos_emb"),
        "wqT": tok("wq").T, "wkT": tok("wk").T, "wvT": tok("wv").T, "woT": tok("wo").T,
        "bq": tok("bq")[:, None], "bk": tok("bk")[:, None], "bv": tok("bv")[:, None], "bo": tok("bo"),
        "gamma": tok("gamma"), "beta": tok("beta"),
        "wq2T": head_cols(attn("Wq").T), "wk2T": head_cols(attn("Wk").T), "wv2T": attn("Wv").T, "wo2T": attn("Wo").T,
        "bq2": head_cols(attn("bq")).reshape(2, P).T, "bk2": head_cols(attn("bk")).reshape(2, P).T,
        "bv2": attn("bv").reshape(2, P).T, "bo2": attn("bo"),
        "routerT": ffn("router_w").T, "router_b": ffn("router_b"),
        "w1": ffn("weights1"), "b1T": ffn("bias1").T, "w2": ffn("weights2"), "b2": ffn("bias2"),
    }
    arrays = {k: np.ascontiguousarray(v) for k, v in arrays.items()}
    nc = bacc.Bacc("TRN2", target_bir_lowering=False, num_devices=1)
    args = {k: nc.dram_tensor(f"in_{k}_dram", v.shape, mybir.dt.from_np(v.dtype), kind="ExternalInput").ap()
            for k, v in arrays.items()}
    args["out"] = nc.dram_tensor("out_dram", (NTOK, D), F32, kind="ExternalOutput").ap()
    build(nc, args)
    r = run_bass_kernel_spmd(nc, [{f"in_{k}_dram": v for k, v in arrays.items()}], core_ids=[0])
    return r.results[0]["out_dram"].reshape(NS, T, D)
```

```python
from contextlib import ExitStack

import concourse.bass as bass
from concourse import mybir

F32 = mybir.dt.float32
BF16 = mybir.dt.bfloat16
I32 = mybir.dt.int32
ALU = mybir.AluOpType
ACT = mybir.ActivationFunctionType
AX = mybir.AxisListType

P = 128
NS, T = 64, 256
D = 256
DK = 128
NH, DH = 16, 16
E, HID = 32, 64
EPS = 1e-5
TT = T // P
CC = D // P
NTOK = NS * T
NTILE = NTOK // P
MTILES = NTILE + E
PARTS = 6
QPART = (0, 1, 2, 0, 1, 0)
KPART = (0, 0, 0, 1, 1, 2)
MASKED = -1e30
ROW = D + 2

PLACES = {
    "ids": dict(SP=-47.36),
    "gather": dict(Pool=-44.83),
    "embed": dict(Pool=-39.79),
    "embed_turn": dict(ACT=-37.3, PE=-36.18),
    "tok_qk": dict(ACT=-35.25, PE=-35.19, DVE=-34.32),
    "tok_v": dict(PE=-32.03, DVE=-31.86),
    "tok_scores": dict(PE=-32.92),
    "tok_softmax": dict(DVE=-32.97, ACT=-32.85),
    "tok_turn": dict(ACT=-31.68, PE=-31, DVE=-29.76),
    "tok_mix": dict(PE=-29.95, DVE=-29.52),
    "tok_out": dict(PE=-28.61, DVE=-26.04),
    "stats1": dict(DVE=-25.47),
    "aggregate1": dict(DVE=-25.32),
    "rstd1": dict(Pool=-22.07),
    "norm1": dict(DVE=-18.58),
    "affine": dict(Pool=-15.07),
    "residual": dict(Pool=-0.65),
    "stats2": dict(DVE=-14.34),
    "aggregate2": dict(DVE=-13.54),
    "rstd2": dict(Pool=-11.4),
    "norm2": dict(DVE=-11.75),
    "norm_turn": dict(PE=-10.86, ACT=-10.21),
    "project_q": dict(ACT=-9.3, PE=-8.23, DVE=-6.54),
    "project_k": dict(PE=-7.04, ACT=-6.86, DVE=-5.45),
    "project_v": dict(ACT=-5.89, PE=-5.71),
    "split_q": dict(Pool=-4.92),
    "split_k": dict(Pool=-3.97),
    "stack": dict(SP=8.83),
    "scores": dict(PE=0),
    "weights": dict(ACT=0.64, DVE=0.66),
    "turn": dict(PE=2.75),
    "evacuate": dict(ACT=1.98, DVE=2.7),
    "mix": dict(PE=4.09),
    "recip": dict(DVE=17.43, Pool=20.05),
    "take_mix": dict(ACT=17.65),
    "recip_turn": dict(PE=20.59),
    "scale_mix": dict(DVE=21.76),
    "out2": dict(PE=23.29),
    "hidden_rows": dict(DVE=23.35),
    "stats3": dict(DVE=23.72),
    "aggregate3": dict(DVE=24.07),
    "rstd3": dict(Pool=26.42),
    "store": dict(SP=37.67),
    "norm3": dict(DVE=26.46),
    "router_turn": dict(ACT=26.14, PE=26.75),
    "logits": dict(PE=28.28),
    "add_bias": dict(DVE=28.45),
    "find_top": dict(DVE=29.4),
    "match_top": dict(DVE=29.78),
    "number_matches": dict(DVE=30.85),
    "find_first": dict(DVE=31.06),
    "choose": dict(DVE=32.12),
    "rank": dict(PE=35.11, Pool=45.22),
    "pick_rank": dict(DVE=35.23),
    "sum_rank": dict(DVE=36.66),
    "place": dict(DVE=36.95, Pool=40.13),
}
BY_HEAD = ("scores", "weights", "turn", "evacuate", "mix")
AHEAD = -int(min(min(places.values()) for places in PLACES.values()) // NH)
BEHIND = 1 + int(max(max(places.values()) for name, places in PLACES.items() if name not in BY_HEAD) // NH)

class Seq:

    def __init__(self, n, par, pair):
        self.n, self.par, self.pair = n, par, pair


def seq_at(pair, k):
    if isinstance(pair, int):
        n = 2 * pair + k
        return Seq(n, n % 2, n // 2) if 0 <= n < NS else None
    return Seq(2 * pair + k, k % 2, pair + k // 2)


def later(s, k=1):
    return not isinstance(s.n, int) or s.n >= k


def is_first(s):
    return isinstance(s.n, int) and s.n == 0


def next_or_last(s):
    return min(s.n + 2, NS) if isinstance(s.n, int) else s.n + 2


def plan(engine):
    steps = []
    for name, places in PLACES.items():
        if engine in places:
            for head in range(NH) if name in BY_HEAD else (None,):
                at = places[engine] + (head or 0)
                steps.append((at % NH, name, -int(at // NH), () if head is None else (head,)))
    return [step[1:] for step in sorted(steps, key=lambda step: (step[0], step[1]))]


def run_iterations(eng, engine, ops):
    steps = plan(engine)

    def iteration(pair, k):
        for name, ahead, head in steps:
            s = seq_at(pair, k + ahead)
            if s is not None:
                ops[name](s, *head)

    first = (BEHIND + 1) // 2
    for it in range(-AHEAD, 2 * first + 1):
        iteration(0, it)
    last = (NS - 1 - AHEAD) // 2
    with eng.Fori(first, last) as pair:
        iteration(pair, 1)
        iteration(pair, 2)
    for it in range(2 * last + 1, NS + BEHIND):
        iteration(0, it)


def build(nc, a):
    slopes = [float((2.0 ** -0.5) * (2.0 ** -0.5) ** i) for i in range(NH)]
    out = a["out"]
    hidden = nc.dram_tensor("hidden_dram", (NTOK, ROW), F32)
    LIST = (E + 2) * NTOK
    lists = nc.dram_tensor("lists_dram", (LIST, 1), I32)

    with ExitStack() as ctx:
        def sb(name, shape, dt=F32):
            return ctx.enter_context(nc.sbuf_tensor(name, shape, dt))

        def sem(name):
            return ctx.enter_context(nc.semaphore(name))

        wq, wk, wv = (sb(n, [P, CC, DK]) for n in ("wq", "wk", "wv"))
        wo = sb("wo", [P, D])
        bqk = sb("bqk", [P, 2])
        bq_scaled = sb("bq_scaled", [P, 1])
        wq2, wk2, wv2, wo2 = (sb(n, [P, CC, D]) for n in ("wq2", "wk2", "wv2", "wo2"))
        bqk2 = sb("bqk2", [P, 2, 2])
        bv1 = sb("bv1", [P, 1])
        bv2 = sb("bv2", [P, 2])
        pos = sb("pos", [P, TT, D])
        tok_bias = sb("tok_bias", [P, TT, D])
        attn_bias = sb("attn_bias", [P, TT, D])
        gamma = sb("gamma", [P, TT, D])
        beta = sb("beta", [P, TT, D])
        router = sb("router", [P, CC, E])
        router_b = sb("router_b", [P, TT, E])
        w1 = sb("w1", [P, E, CC * HID + 1])
        w2 = sb("w2", [HID + 1, E, D])
        ident = sb("ident", [P, P])
        minus_half = sb("minus_half", [P, TT])
        alibi = sb("alibi", [P, NH, 3 * P])
        tri = sb("tri", [P, P], BF16)
        ones = sb("ones", [P, P], BF16)
        rev = sb("rev", [P, TT, E])
        base = sb("base", [P, E], BF16)
        number = [sb(f"number{i}", [P, TT], I32) for i in range(2)]
        two_sequences = sb("two_sequences", [P, TT], I32)

        ids = [sb(f"ids{i}", [P, TT], I32) for i in range(2)]
        x = [sb(f"x{i}", [P, TT, D]) for i in range(2)]
        xb = sb("xb", [P, TT, D])
        xT = sb("xT", [P, CC, T])
        qkT = sb("qkT", [P, 2, T])
        v1 = sb("v1", [P, TT, DK])
        nmax1, sum1, rsum1 = (sb(n, [P, TT]) for n in ("nmax1", "sum1", "rsum1"))
        p1 = sb("p1", [P, TT, T])
        pT1 = sb("pT1", [P, TT, T])
        headT = sb("headT", [P, T])
        h0 = sb("h0", [P, TT, D])
        bn = [sb(f"bn{i}", [P, TT, 6]) for i in range(3)]
        mv = [sb(f"mv{i}", [P, TT, 2]) for i in range(2)]
        ve = [sb(f"ve{i}", [P, TT]) for i in range(3)]
        rstd = [sb(f"rstd{i}", [P, TT]) for i in range(2)]
        xhat = sb("xhat", [P, TT, D])
        xg = sb("xg", [P, TT, D])
        h1 = sb("h1", [P, TT, D])
        h1b = [sb(f"h1b{i}", [P, TT, D]) for i in range(2)]
        xn = sb("xn", [P, TT, D])
        xnT = sb("xnT", [P, CC, T])
        part = [sb(f"part{i}", [P, 3, 2, T], BF16) for i in range(2)]
        rest = [sb(f"rest{i}", [P, 2, T]) for i in range(2)]
        qst = [sb(f"qst{i}", [PARTS * DH, NH, T], BF16) for i in range(2)]
        kst = [sb(f"kst{i}", [PARTS * DH, NH, T], BF16) for i in range(2)]
        vpad = [sb(f"vpad{i}", [P, TT, NH // 2, 4 * DH]) for i in range(2)]
        sc = [sb(f"sc{i}", [P, 3 * P]) for i in range(2)]
        nmax = sb("nmax", [P, 2, TT])
        pr = [sb(f"pr{i}", [P, 3 * P]) for i in range(2)]
        prT = [sb(f"prT{i}", [P, 3 * P]) for i in range(2)]
        sums = [sb(f"sums{i}", [P, TT, NH]) for i in range(2)]
        rsums = sb("rsums", [P, TT, NH])
        rexp = sb("rexp", [P, TT, D])
        yT, ynT = sb("yT", [P, 2, T]), sb("ynT", [P, 2, T])
        h2 = [sb(f"h2{i}", [P, TT, ROW]) for i in range(2)]
        xf = sb("xf", [P, TT, D])
        xfT = sb("xfT", [P, CC, T])
        lg, eq, onehot_f = (sb(n, [P, TT, E]) for n in ("lg", "eq", "onehot_f"))
        top, best = sb("top", [P, TT]), sb("best", [P, TT])
        onehot = sb("onehot", [P, TT, E], BF16)
        acc = sb("acc", [P, E], BF16)
        place_m = sb("place_m", [P, TT, E])
        place_f = sb("place_f", [P, TT])
        place_i = [sb(f"place_i{i}", [P, TT], I32) for i in range(2)]
        iota_t = sb("iota_t", [E, MTILES])
        count = sb("count", [E, 1])
        ntiles = sb("ntiles", [E, 1])
        tri_inc = sb("tri_inc", [E, E])
        cum = sb("cum", [E, 1])
        ones_col = sb("ones_col", [E, 1])
        table = sb("table", [1, 2, MTILES], I32)
        NB = 8
        eoid = sb("eoid", [P, 2 * NB], I32)
        eid = [eoid[:, i:i + 1] for i in range(NB)]
        oid = [eoid[:, NB + i:NB + i + 1] for i in range(NB)]

        spare, at = alibi[:].rearrange("p h k -> p (h k)"), [0]

        def in_alibi(width, rows=P):
            at[0] += width
            return spare[0:rows, at[0] - width:at[0]]

        he = [in_alibi(ROW) for _ in range(NB)]
        xe = [in_alibi(D) for _ in range(2)]
        xeT = [in_alibi(D).rearrange("p (c t) -> p c t", c=CC) for _ in range(2)]
        w1e = [in_alibi(CC * HID + 1) for _ in range(2)]
        hT = [in_alibi(P, HID + 1) for _ in range(2)]
        below = in_alibi(NTILE, E)
        passed = in_alibi(MTILES, E)
        tab_f = in_alibi(4 * MTILES, 1).rearrange("p (n t) -> p n t", n=4)
        oe = [t[:, i, :] for t in (h0, h1b[0], h1b[1], xn) for i in range(TT)]
        wo_a = xhat[:]
        row_bias = xg[:]
        bv_rep = rexp[:].rearrange("p t (a k) -> p (t a) k", a=2)
        sentinel = h2[0][:, 0, 0:D].bitcast(I32)
        rel = pT1[:].rearrange("p t k -> p (t k)")[:, 0:3 * P]

        def bank(name):
            return ctx.enter_context(nc.psum_tensor(name, [P, 512], F32))

        ps_s = [bank("ps_s0"), bank("ps_s1")]
        ps_t = [bank("ps_t0"), bank("ps_t1")]
        ps_y = bank("ps_y")
        ps_a, ps_b = bank("ps_a"), bank("ps_b")
        ps_c = bank("ps_c")

        first_loaded = sem("first_loaded")
        pos_loaded = sem("pos_loaded")
        loaded = sem("loaded")
        experts_loaded = sem("experts_loaded")
        lists_clear = sem("lists_clear")
        pool_const = sem("pool_const")
        dve_const = sem("dve_const")
        pe_const = sem("pe_const")
        ids_in = [sem(f"ids_in{i}") for i in range(2)]
        rows_in = [sem(f"rows_in{i}") for i in range(2)]
        stacked = [sem(f"stacked{i}") for i in range(2)]
        h2_out = [sem(f"h2_out{i}") for i in range(2)]
        placed = [sem(f"placed{i}") for i in range(2)]
        x_ready, xb_ready = sem("x_ready"), sem("xb_ready")
        ve_ready = [sem(f"ve_ready{i}") for i in range(3)]
        rstd_ready = [sem(f"rstd_ready{i}") for i in range(3)]
        xg_ready, h1_ready, h1b_ready = sem("xg_ready"), sem("h1_ready"), sem("h1b_ready")
        part2_ready, part3_ready = sem("part2_ready"), sem("part3_ready")
        rexp_ready = sem("rexp_ready")
        number_ready = sem("number_ready")
        acc_half, acc_ready = sem("acc_half"), sem("acc_ready")
        xT_done, qk_done, v_done, s1_done, pT1_done = (sem(n) for n in ("xT_done", "qk_done", "v_done", "s1_done", "pT1_done"))
        head_done, out1_done, xnT_done = sem("head_done"), sem("out1_done"), sem("xnT_done")
        Q_done, K_done, V_done = sem("Q_done"), sem("K_done"), sem("V_done")
        scores_done, turn_done, mix_done = sem("scores_done"), sem("turn_done"), sem("mix_done")
        rT_done, out2_done, xfT_done, logits_done, rank_done = (sem(n) for n in ("rT_done", "out2_done", "xfT_done", "logits_done", "rank_done"))
        xT_ready, q_ready, p1_ready, pT1_ready, xnT_ready = (sem(n) for n in ("xT_ready", "q_ready", "p1_ready", "pT1_ready", "xnT_ready"))
        part1_ready = sem("part1_ready")
        vpad_ready = sem("vpad_ready")
        pr_ready = sem("pr_ready")
        prT_odd = sem("prT_odd")
        yT_ready, xfT_ready = sem("yT_ready"), sem("xfT_ready")
        k_ready, v_ready, nmax1_ready, rsum1_ready, head_ready, h0_ready = (
            sem(n) for n in ("k_ready", "v_ready", "nmax1_ready", "rsum1_ready", "head_ready", "h0_ready"))
        bn_ready = [sem(f"bn_ready{i}") for i in range(3)]
        mv_ready = [sem(f"mv_ready{i}") for i in range(3)]
        xhat_ready, xn_ready = sem("xhat_ready"), sem("xn_ready")
        rest_ready = sem("rest_ready")
        sc_ready = sem("sc_ready")
        prT_even = sem("prT_even")
        rsums_ready, ynT_ready, h2_ready, xf_ready = (sem(n) for n in ("rsums_ready", "ynT_ready", "h2_ready", "xf_ready"))
        route = sem("route")
        onehot_ready = sem("onehot_ready")
        place_step, place_ready = sem("place_step"), sem("place_ready")
        tab_pe, tab_dve = sem("tab_pe"), sem("tab_dve")
        eid_in = [sem(f"eid_in{i}") for i in range(NB)]
        he_in = [sem(f"he_in{i}") for i in range(NB)]
        oe_out = [sem(f"oe_out{i}") for i in range(NB)]
        he_clear = sem("he_clear")
        e_xe = sem("e_xe")
        e_xeT, e_xeTs, e_w1, e_h, e_hs, e_y, e_o, e_oid = (sem(n) for n in ("e_xeT", "e_xeTs", "e_w1", "e_h", "e_hs", "e_y", "e_o", "e_oid"))

        def moments(i, s):
            if i == 2:
                return h2[s.par][:, :, D:ROW], h2[s.par][:, :, D + 1]
            return mv[i][:], rstd[i][:]

        passed_sp, passed_pool, passed_dve = sem("passed_sp"), sem("passed_pool"), sem("passed_dve")

        def wait_alone(eng, passed_waits, semaphore, value):
            eng.wait_ge(semaphore, value)
            eng.sem_inc(passed_waits, 1)

        row = lambda v: v.rearrange("(a n) -> a n", a=1)
        FIRST_LOADS = [
            (wq[:], a["wqT"].rearrange("(c p) d -> p c d", p=P)), (wk[:], a["wkT"].rearrange("(c p) d -> p c d", p=P)),
            (wv[:], a["wvT"].rearrange("(c p) d -> p c d", p=P)), (wo_a, a["woT"].rearrange("(c p) d -> p c d", p=P)),
            (wo2[:], a["wo2T"].rearrange("(c p) d -> p c d", p=P)),
            (bqk[:, 0:1], a["bq"]), (bqk[:, 1:2], a["bk"]), (bv1[:], a["bv"]), (bv2[:], a["bv2"]),
            (row_bias[:, 0, :], row(a["bo"]).to_broadcast([P, D])), (row_bias[:, 1, :], row(a["bo2"]).to_broadcast([P, D])),
        ]
        LOADS = [
            (gamma[:, 0, :], row(a["gamma"]).to_broadcast([P, D])), (gamma[:, 1, :], row(a["gamma"]).to_broadcast([P, D])),
            (beta[:, 0, :], row(a["beta"]).to_broadcast([P, D])), (beta[:, 1, :], row(a["beta"]).to_broadcast([P, D])),
            (wq2[:], a["wq2T"].rearrange("(c p) d -> p c d", p=P)), (wk2[:], a["wk2T"].rearrange("(c p) d -> p c d", p=P)),
            (wv2[:], a["wv2T"].rearrange("(c p) d -> p c d", p=P)),
            (bqk2[:, 0, :], a["bq2"]), (bqk2[:, 1, :], a["bk2"]),
            (router[:], a["routerT"].rearrange("(c p) e -> p c e", p=P)),
            (router_b[:, 0, :], row(a["router_b"]).to_broadcast([P, E])), (router_b[:, 1, :], row(a["router_b"]).to_broadcast([P, E])),
        ]
        EXPERT_LOADS = [(w1[:, :, c * HID:(c + 1) * HID], a["w1"][:, c * P:(c + 1) * P, :].rearrange("e p m -> p e m"))
                        for c in range(CC)]
        EXPERT_LOADS += [(w1[0:HID, :, CC * HID:], a["b1T"].rearrange("m (e a) -> m e a", a=1)),
                         (w2[0:HID, :, :], a["w2"].rearrange("e m d -> m e d")), (w2[HID:HID + 1, :, :], a["b2"].rearrange("(a e) d -> a e d", a=1))]
        FIRST_LOADED = 16 * len(FIRST_LOADS)
        ALL_LOADED = 16 * len(LOADS)
        EXPERTS_LOADED = 16 * len(EXPERT_LOADS)
        POOL_CONST = 19
        BIAS_ROWS, DVE_CONST = 5, 6

        block = ctx.enter_context(nc.Block())

        @block.sync
        def _(sp):
            for dst, src in FIRST_LOADS:
                sp.dma_start(dst, src).then_inc(first_loaded, 16)

            def settled():
                sp.wait_ge(pool_const, POOL_CONST)

            def set_up(n):
                if n == 0:
                    sp.dma_start(pos[:], a["pos_emb"][0:T, :].rearrange("(t p) c -> p t c", p=P)).then_inc(pos_loaded, 16)
                    for dst, src in LOADS:
                        sp.dma_start(dst, src).then_inc(loaded, 16)
                if n == 2:
                    for i in range(LIST // (P * 256)):
                        sp.dma_start(lists[i * P * 256:(i + 1) * P * 256, :].rearrange("(p n) a -> p (n a)", p=P),
                                     sentinel).then_inc(lists_clear, 16)
                for dst, src in {3: EXPERT_LOADS[:1], 4: EXPERT_LOADS[1:3], 5: EXPERT_LOADS[3:]}.get(n, ()):
                    sp.dma_start(dst, src, allow_slow_non_contiguous=True).then_inc(experts_loaded, 16)

            def load_ids(s):
                settled()
                if later(s, 2):
                    sp.wait_ge(rows_in[s.par], 32 * s.pair)
                sp.dma_start(ids[s.par][:], a["ids"][bass.ds(s.n, 1), :, :].rearrange("a p t -> (a p) t")
                             ).then_inc(ids_in[s.par], 16)
                if isinstance(s.n, int):
                    set_up(s.n)

            def stack(s):
                settled()
                if later(s, 2):
                    sp.wait_ge(scores_done, NH * (s.n - 1))
                for p, made in enumerate((part1_ready, part2_ready, part3_ready)):
                    for i, dst, which in ((0, qst, QPART), (1, kst, KPART)):
                        wait_alone(sp, passed_sp, made, 2 * s.n + i + 1)
                        for b in range(PARTS):
                            if which[b] == p:
                                sp.dma_start(dst[s.par][DH * b:DH * (b + 1), :, :], part[i][:, p, :, :]
                                             ).then_inc(stacked[s.par], 16)

            def store_h2(s):
                settled()
                sp.wait_ge(rstd_ready[2], s.n + 1)
                sp.dma_start(hidden[bass.ds(s.n * T, T), :].rearrange("(t p) c -> p t c", p=P), h2[s.par][:]
                             ).then_inc(h2_out[s.par], 16)

            run_iterations(sp, "SP", dict(ids=load_ids, stack=stack, store=store_h2))

            sp.wait_ge(tab_dve, 4)
            for i in range(2):
                sp.wait_ge(placed[i], 32 * (NS // 2))
                sp.wait_ge(h2_out[i], 16 * (NS // 2))

            def load_tile(i, b):
                at = sp.value_load(table[0:1, 1, bass.ds(i, 1)], min_val=0, max_val=LIST - P)
                sp.dma_start(eid[b], lists[bass.ds(at, P), :]).then_inc(eid_in[b], 16)

            for b in range(NB):
                load_tile(b, b)
            with sp.Fori(0, MTILES // NB - 1) as r:
                for b in range(NB):
                    settled()
                    sp.wait_ge(e_oid, NB * r + b + 1)
                    sp.wait_ge(he_in[b], 16 * (r + 1))
                    load_tile(NB * r + b + NB, b)

        @block.gpsimd
        def _(pool):
            g = nc.gpsimd
            g.memset(ident[:], 0.0).then_inc(pool_const, 1)
            g.memset(tri[:], 1.0).then_inc(pool_const, 1)
            g.memset(tri_inc[:], 1.0).then_inc(pool_const, 1)
            g.iota(rel[:, 0:P], [[1, P]], base=0, channel_multiplier=-1, allow_small_or_imprecise_dtypes=True).then_inc(pool_const, 1)
            g.iota(rel[:, P:3 * P], [[1, 2 * P]], base=-P, channel_multiplier=-1, allow_small_or_imprecise_dtypes=True).then_inc(pool_const, 1)
            pool.wait_ge(pool_const, 5)
            g.affine_select(out=ident[:], in_=ident[:], compare_op=ALU.not_equal, fill=1.0, base=0,
                            pattern=[[-1, P]], channel_multiplier=1).then_inc(pool_const, 1)
            g.affine_select(out=tri[:], in_=tri[:], compare_op=ALU.is_gt, fill=0.0, base=0,
                            pattern=[[1, P]], channel_multiplier=-1).then_inc(pool_const, 1)
            g.affine_select(out=tri_inc[:], in_=tri_inc[:], compare_op=ALU.is_ge, fill=0.0, base=0,
                            pattern=[[1, E]], channel_multiplier=-1).then_inc(pool_const, 1)
            g.affine_select(out=rel[:, 0:P], in_=rel[:, 0:P], compare_op=ALU.is_ge, fill=MASKED, base=0,
                            pattern=[[-1, P]], channel_multiplier=1).then_inc(pool_const, 1)
            g.affine_select(out=rel[:, P:3 * P], in_=rel[:, P:3 * P], compare_op=ALU.is_ge, fill=MASKED, base=P,
                            pattern=[[-1, 2 * P]], channel_multiplier=1).then_inc(pool_const, 1)
            g.memset(minus_half[:], -0.5).then_inc(pool_const, 1)
            g.memset(sentinel, NTOK).then_inc(pool_const, 1)
            g.memset(w1[:, :, CC * HID:], 0.0).then_inc(pool_const, 1)
            g.iota(rev[:], [[0, TT], [-1, E]], base=E, channel_multiplier=0, allow_small_or_imprecise_dtypes=True).then_inc(pool_const, 1)
            g.iota(base[:], [[NTOK // P, E]], base=0, channel_multiplier=0, allow_small_or_imprecise_dtypes=True).then_inc(pool_const, 1)
            for i in range(2):
                g.iota(number[i][:], [[P, TT]], base=i * T, channel_multiplier=1).then_inc(pool_const, 1)
            g.iota(two_sequences[:], [[0, TT]], base=2 * T, channel_multiplier=0).then_inc(pool_const, 1)
            g.iota(iota_t[:], [[1, MTILES]], base=0, channel_multiplier=0, allow_small_or_imprecise_dtypes=True).then_inc(pool_const, 1)

            def gather(s):
                if later(s, 2):
                    pool.wait_ge(xT_done, s.n - 1)
                    pool.wait_ge(xb_ready, s.n - 1)
                wait_alone(pool, passed_pool, ids_in[s.par], 16 * (s.pair + 1))
                for t in range(TT):
                    g.indirect_dma_start(out=x[s.par][:, t, :], out_offset=None, in_=a["tok_emb"],
                                         in_offset=bass.IndirectOffsetOnAxis(ap=ids[s.par][:, t:t + 1], axis=0)
                                         ).then_inc(rows_in[s.par], 16)

            def embed(s):
                if is_first(s):
                    pool.wait_ge(pos_loaded, 16)
                    pool.wait_ge(dve_const, BIAS_ROWS)
                pool.wait_ge(rows_in[s.par], 32 * (s.pair + 1))
                g.tensor_tensor(x[s.par][:], x[s.par][:], pos[:], ALU.add).then_inc(x_ready, 1)
                pool.wait_ge(x_ready, s.n + 1)
                if later(s):
                    pool.wait_ge(h0_ready, s.n)
                g.tensor_tensor(xb[:], x[s.par][:], tok_bias[:], ALU.add).then_inc(xb_ready, 1)

            def rstd_of(i):
                def f(s):
                    wait_alone(pool, passed_pool, mv_ready[i], s.n + 1)
                    g.tensor_scalar(ve[i][:], moments(i, s)[0][:, :, 1], EPS, None, ALU.add).then_inc(ve_ready[i], 1)
                    pool.wait_ge(ve_ready[i], s.n + 1)
                    g.tensor_tensor(moments(i, s)[1], ve[i][:], minus_half[:], ALU.pow).then_inc(rstd_ready[i], 1)
                return f

            def affine(s):
                if is_first(s):
                    pool.wait_ge(loaded, ALL_LOADED)
                pool.wait_ge(xhat_ready, s.n + 1)
                g.tensor_tensor(xg[:], xhat[:], gamma[:], ALU.mult).then_inc(xg_ready, 1)
                pool.wait_ge(xg_ready, s.n + 1)
                if later(s):
                    pool.wait_ge(xn_ready, s.n)
                    pool.wait_ge(h1b_ready, s.n)
                g.tensor_tensor(h1[:], xg[:], beta[:], ALU.add).then_inc(h1_ready, 1)

            def residual(s):
                pool.wait_ge(h1_ready, s.n + 1)
                if later(s, 2):
                    pool.wait_ge(h2_ready, s.n - 1)
                g.tensor_tensor(h1b[s.par][:], h1[:], attn_bias[:], ALU.add).then_inc(h1b_ready, 1)

            def split(i):
                def f(s):
                    if later(s):
                        pool.wait_ge(stacked[1 - s.par], 192 * (s.pair + s.par))
                    wait_alone(pool, passed_pool, rest_ready, 2 * s.n + i + 1)
                    g.tensor_copy(part[i][:, 1, :, :], rest[i][:]).then_inc(part2_ready, 1)
                    pool.wait_ge(part2_ready, 2 * s.n + i + 1)
                    g.tensor_tensor(part[i][:, 2, :, :], rest[i][:], part[i][:, 1, :, :], ALU.subtract).then_inc(part3_ready, 1)
                return f

            def recip(s):
                if later(s):
                    pool.wait_ge(rT_done, s.n)
                wait_alone(pool, passed_pool, rsums_ready, s.n + 1)
                g.tensor_copy(rexp[:].rearrange("p t (h d) -> p t h d", d=DH),
                              rsums[:, :, :, None].to_broadcast([P, TT, NH, DH])).then_inc(rexp_ready, 1)

            def rank(s):
                pool.wait_ge(rank_done, s.n + 1)
                g.tensor_tensor(acc[:], acc[:], onehot[:, 0, :], ALU.add).then_inc(acc_half, 1)
                pool.wait_ge(acc_half, s.n + 1)
                g.tensor_tensor(acc[:], acc[:], onehot[:, 1, :], ALU.add).then_inc(acc_ready, 1)

            def place(s):
                if is_first(s):
                    pool.wait_ge(lists_clear, 16 * (LIST // (P * 256)))
                pool.wait_ge(place_ready, s.n + 1)
                if later(s, 2):
                    pool.wait_ge(placed[s.par], 32 * s.pair)
                    g.tensor_tensor(number[s.par][:], number[s.par][:], two_sequences[:], ALU.add).then_inc(number_ready, 1)
                    wait_alone(pool, passed_pool, number_ready, s.n - 1)
                for t in range(TT):
                    g.indirect_dma_start(out=lists[:, :], out_offset=bass.IndirectOffsetOnAxis(ap=place_i[s.par][:, t:t + 1], axis=0),
                                         in_=number[s.par][:, t:t + 1], in_offset=None).then_inc(placed[s.par], 16)

            run_iterations(pool, "Pool", dict(gather=gather, embed=embed, rstd1=rstd_of(0), rstd2=rstd_of(1), rstd3=rstd_of(2), affine=affine,
                                      residual=residual, split_q=split(0), split_k=split(1), recip=recip, rank=rank, place=place))

            def fetch(i, b, turn):
                if isinstance(i, int) and i < NB:
                    pool.wait_ge(he_clear, NB)
                else:
                    pool.wait_ge(e_o, i - NB + 1)
                wait_alone(pool, passed_pool, eid_in[b], 16 * (turn + 1))
                g.indirect_dma_start(out=he[b], out_offset=None, in_=hidden[:, :],
                                     in_offset=bass.IndirectOffsetOnAxis(ap=eid[b], axis=0),
                                     bounds_check=NTOK - 1, oob_is_err=False).then_inc(he_in[b], 16)

            def send(i, b):
                wait_alone(pool, passed_pool, e_o, i + 1)
                g.indirect_dma_start(out=out, out_offset=bass.IndirectOffsetOnAxis(ap=oid[b], axis=0),
                                     in_=oe[b], in_offset=None, bounds_check=NTOK - 1, oob_is_err=False).then_inc(oe_out[b], 16)

            FETCH = 5

            def step(r, u):
                fetch(NB * r + u + FETCH, (u + FETCH) % NB, r + (u + FETCH) // NB)
                send(NB * r + u, u)

            for i in range(FETCH):
                fetch(i, i, 0)
            for u in range(NB):
                step(0, u)
            with pool.Fori(1, MTILES // NB - 1) as r:
                for u in range(NB):
                    step(r, u)
            for u in range(NB - FETCH):
                step(MTILES // NB - 1, u)
            for i in range(MTILES - FETCH, MTILES):
                send(i, i % NB)
            for b in range(NB):
                pool.wait_ge(oe_out[b], 16 * (MTILES // NB))

        @block.scalar
        def _(act):
            s_ = nc.scalar
            act.wait_ge(first_loaded, FIRST_LOADED)
            act.wait_ge(dve_const, BIAS_ROWS)

            def embed_turn(s):
                act.wait_ge(xT_done, s.n + 1)
                if later(s):
                    act.wait_ge(v_done, s.n)
                s_.activation(xT[:].rearrange("p c t -> p (c t)"), ps_a[:], ACT.Copy).then_inc(xT_ready, 1)

            def tok_qk(s):
                act.wait_ge(qk_done, s.n + 1)
                if later(s):
                    act.wait_ge(s1_done, s.n)
                s_.activation(qkT[:, 0, :], ps_b[:, 0:T], ACT.Identity, bias=bq_scaled[:, 0:1], scale=DK ** -0.5).then_inc(q_ready, 1)

            def tok_softmax(s):
                act.wait_ge(nmax1_ready, s.n + 1)
                if later(s):
                    act.wait_ge(pT1_done, s.n)
                    act.wait_ge(rsum1_ready, s.n)
                for t in range(TT):
                    last = s_.activation(p1[:, t, :], ps_b[:, t * T:(t + 1) * T], ACT.Exp, bias=nmax1[:, t:t + 1],
                                         accum_out=sum1[:, t:t + 1])
                last.then_inc(p1_ready, 1)

            def tok_turn(s):
                if is_first(s):
                    act.wait_ge(dve_const, DVE_CONST)
                act.wait_ge(pT1_done, s.n + 1)
                if later(s):
                    act.wait_ge(head_done, s.n)
                s_.activation(pT1[:].rearrange("p c t -> p (c t)"), ps_a[:], ACT.Copy).then_inc(pT1_ready, 1)

            def norm_turn(s):
                act.wait_ge(xnT_done, s.n + 1)
                if later(s):
                    act.wait_ge(V_done, s.n)
                s_.activation(xnT[:].rearrange("p c t -> p (c t)"), ps_b[:], ACT.Copy).then_inc(xnT_ready, 1)

            def project(i):
                done, ps = ((Q_done, ps_a), (K_done, ps_b))[i]

                def f(s):
                    if is_first(s):
                        act.wait_ge(loaded, ALL_LOADED)
                    act.wait_ge(done, s.n + 1)
                    if later(s):
                        act.wait_ge(stacked[1 - s.par], 192 * (s.pair + s.par))
                        act.wait_ge(part3_ready, 2 * s.n)
                    for gr in range(2):
                        last = s_.activation(part[i][:, 0, gr, :], ps[:, gr * T:(gr + 1) * T], ACT.Identity,
                                             bias=bqk2[:, i, gr:gr + 1])
                    last.then_inc(part1_ready, 1)
                return f

            def project_v(s):
                act.wait_ge(V_done, s.n + 1)
                if later(s, 2):
                    act.wait_ge(mix_done, NH * (s.n - 1))
                for odd in range(2):
                    last = s_.activation(vpad[s.par][:, :, :, 48 * odd:48 * odd + DH],
                                         ps_a[:].rearrange("p (t h o d) -> p t h o d", t=TT, o=2, d=DH)[:, :, :, odd, :], ACT.Copy)
                last.then_inc(vpad_ready, 1)

            def weights(s, h):
                act.wait_ge(sc_ready, NH * s.n + h + 1)
                if later(s) or h >= 2:
                    act.wait_ge(turn_done, NH * s.n + h - 1)
                for t in range(TT):
                    c0, c1 = (0, P) if t == 0 else (P, 3 * P)
                    last = s_.activation(pr[h % 2][:, c0:c1], sc[h % 2][:, c0:c1], ACT.Exp, bias=nmax[:, h % 2, t:t + 1],
                                         scale=-1.0, accum_out=sums[s.par][:, t, h:h + 1])
                last.then_inc(pr_ready, 1)

            def evacuate(s, h):
                if h % 2 == 0:
                    return
                act.wait_ge(turn_done, NH * s.n + h + 1)
                if later(s) or h >= 2:
                    act.wait_ge(mix_done, NH * s.n + h - 1)
                s_.activation(prT[1][:], ps_t[1][:, 0:3 * P], ACT.Copy).then_inc(prT_odd, 1)

            def take_mix(s):
                act.wait_ge(mix_done, NH * s.n + NH)
                if later(s):
                    act.wait_ge(ynT_ready, s.n)
                s_.activation(yT[:].rearrange("p g t -> p (g t)"), ps_y[:], ACT.Copy).then_inc(yT_ready, 1)

            def router_turn(s):
                act.wait_ge(xfT_done, s.n + 1)
                if later(s):
                    act.wait_ge(logits_done, s.n)
                s_.activation(xfT[:].rearrange("p c t -> p (c t)"), ps_c[:], ACT.Copy).then_inc(xfT_ready, 1)

            run_iterations(act, "ACT", dict(embed_turn=embed_turn, tok_qk=tok_qk, tok_softmax=tok_softmax, tok_turn=tok_turn,
                                     norm_turn=norm_turn, project_q=project(0), project_k=project(1), project_v=project_v, weights=weights,
                                     evacuate=evacuate, take_mix=take_mix, router_turn=router_turn))

            act.wait_ge(tab_dve, 4)
            act.wait_ge(experts_loaded, EXPERTS_LOADED)

            def turned(i, b):
                e = act.value_load(table[0:1, 0, bass.ds(i, 1)], min_val=0, max_val=E - 1)
                if not isinstance(i, int) or i >= 2:
                    act.wait_ge(e_hs, i - 1)
                s_.activation(w1e[b][:, None, :], w1[:, bass.ds(e, 1), :], ACT.Copy).then_inc(e_w1, 1)
                act.wait_ge(e_xeT, i + 1)
                s_.activation(xeT[b][:].rearrange("p c t -> p (c t)"), ps_s[b][:, 0:D], ACT.Copy).then_inc(e_xeTs, 1)

            def hidden_relu(i, b):
                act.wait_ge(e_h, i + 1)
                if not isinstance(i, int) or i >= 2:
                    act.wait_ge(e_y, i - 1)
                act.wait_ge(e_w1, i + 1)
                s_.activation(hT[b][0:HID, :], ps_t[b][0:HID, 0:P], ACT.Relu, bias=w1e[b][0:HID, CC * HID:]).then_inc(e_hs, 1)

            def step(i, b):
                turned(i + 1, 1 - b)
                hidden_relu(i, b)

            turned(0, 0)
            step(0, 0)
            step(1, 1)
            with act.Fori(1, MTILES // 2 - 1) as r:
                step(2 * r, 0)
                step(2 * r + 1, 1)
            step(MTILES - 2, 0)
            hidden_relu(MTILES - 1, 1)

        @block.vector
        def _(dve):
            v = nc.vector
            dve.wait_ge(first_loaded, FIRST_LOADED)
            v.tensor_tensor(wo[:], wo_a[:, 0, :], wo_a[:, 1, :], ALU.add).then_inc(dve_const, 1)
            v.tensor_scalar(bq_scaled[:], bqk[:, 0:1], DK ** -0.5, None, ALU.mult).then_inc(dve_const, 1)
            for i, col in enumerate((bv1[:, 0:1], bv2[:, 0:1], bv2[:, 1:2])):
                last = v.tensor_copy(bv_rep[:, i, :], col.to_broadcast([P, P]))
            last.then_inc(dve_const, 1)
            v.memset(ones[:], 1.0)
            v.memset(acc[:], 0.0)
            v.memset(ones_col[:], 1.0)
            for i in range(2):
                v.memset(vpad[i][:], 0.0)
                v.memset(sums[i][:], 0.0)
            dve.wait_ge(pool_const, POOL_CONST)
            dve.wait_ge(pe_const, 1)
            for i, dst in enumerate((tok_bias, attn_bias)):
                for t in range(TT):
                    last = v.tensor_tensor(dst[:, t, :], ps_c[:, i * D:(i + 1) * D], row_bias[:, i, :], ALU.add)
                last.then_inc(dve_const, 1)
            for h in range(NH):
                last = v.tensor_scalar(alibi[:, h, :], rel, slopes[h], 4.0, ALU.mult, ALU.mult)
            last.then_inc(dve_const, 1)

            def tok_qk(s):
                dve.wait_ge(qk_done, s.n + 1)
                if later(s):
                    dve.wait_ge(s1_done, s.n)
                dve.wait_ge(q_ready, s.n + 1)
                v.tensor_scalar(qkT[:, 1, :], ps_b[:, T:2 * T], bqk[:, 1:2], None, ALU.add).then_inc(k_ready, 1)

            def tok_v(s):
                dve.wait_ge(v_done, s.n + 1)
                if later(s):
                    dve.wait_ge(head_done, s.n)
                v.tensor_copy(v1[:].rearrange("p t d -> p (t d)"), ps_a[:, 0:TT * DK]).then_inc(v_ready, 1)

            def tok_softmax(s):
                dve.wait_ge(s1_done, s.n + 1)
                if later(s):
                    dve.wait_ge(p1_ready, s.n)
                v.tensor_reduce(nmax1[:], ps_b[:].rearrange("p (t k) -> p t k", t=TT), AX.X, ALU.max, negate=True).then_inc(nmax1_ready, 1)

            def tok_turn(s):
                dve.wait_ge(p1_ready, s.n + 1)
                v.reciprocal(rsum1[:], sum1[:]).then_inc(rsum1_ready, 1)

            def tok_mix(s):
                dve.wait_ge(head_done, s.n + 1)
                if later(s):
                    dve.wait_ge(out1_done, s.n)
                v.tensor_copy(headT[:], ps_b[:, 0:T]).then_inc(head_ready, 1)

            def tok_out(s):
                dve.wait_ge(out1_done, s.n + 1)
                dve.wait_ge(xb_ready, s.n + 1)
                dve.wait_ge(rsum1_ready, s.n + 1)
                for t in range(TT):
                    last = v.scalar_tensor_tensor(out=h0[:, t, :], in0=ps_a[:, t * D:(t + 1) * D], scalar=rsum1[:, t:t + 1],
                                                  in1=xb[:, t, :], op0=ALU.mult, op1=ALU.add)
                last.then_inc(h0_ready, 1)

            def stats(i, src, s):
                for t in range(TT):
                    last = v.bn_stats(bn[i][:, t, :], src[:, t, 0:D])
                last.then_inc(bn_ready[i], 1)

            def aggregate(i, s):
                wait_alone(dve, passed_dve, bn_ready[i], s.n + 1)
                for t in range(TT):
                    last = v.bn_aggr(moments(i, s)[0][:, t, :], bn[i][:, t, :])
                last.then_inc(mv_ready[i], 1)

            def normalize(i, dst, src, s):
                mean, scale = moments(i, s)
                for t in range(TT):
                    last = v.tensor_scalar(dst[:, t, :], src[:, t, 0:D], mean[:, t, 0:1], scale[:, t:t + 1], ALU.subtract, ALU.mult)
                return last

            def stats1(s):
                dve.wait_ge(h0_ready, s.n + 1)
                if later(s):
                    dve.wait_ge(rstd_ready[0], s.n)
                stats(0, h0, s)

            def aggregate1(s):
                aggregate(0, s)

            def norm1(s):
                dve.wait_ge(rstd_ready[0], s.n + 1)
                if later(s):
                    dve.wait_ge(xg_ready, s.n)
                normalize(0, xhat, h0, s).then_inc(xhat_ready, 1)

            def stats2(s):
                dve.wait_ge(h1_ready, s.n + 1)
                stats(1, h1, s)

            def aggregate2(s):
                aggregate(1, s)

            def norm2(s):
                dve.wait_ge(rstd_ready[1], s.n + 1)
                if later(s):
                    dve.wait_ge(xnT_done, s.n)
                normalize(1, xn, h1, s).then_inc(xn_ready, 1)

            def project(i):
                ps = (ps_a, ps_b)[i]

                def f(s):
                    if is_first(s):
                        dve.wait_ge(loaded, ALL_LOADED)
                    dve.wait_ge(part1_ready, 2 * s.n + i + 1)
                    if later(s):
                        dve.wait_ge(part3_ready, 2 * s.n)
                    for gr in range(2):
                        last = v.scalar_tensor_tensor(out=rest[i][:, gr, :], in0=ps[:, gr * T:(gr + 1) * T],
                                                      scalar=bqk2[:, i, gr:gr + 1], in1=part[i][:, 0, gr, :],
                                                      op0=ALU.add, op1=ALU.subtract)
                    last.then_inc(rest_ready, 1)
                return f

            def weights(s, h):
                if later(s) or h >= 2:
                    dve.wait_ge(pr_ready, NH * s.n + h - 1)
                wait_alone(dve, passed_dve, scores_done, NH * s.n + h + 1)
                for t in range(TT):
                    c0, c1 = (0, P) if t == 0 else (P, 3 * P)
                    last = v.tensor_tensor_reduce(out=sc[h % 2][:, c0:c1], in0=ps_s[h % 2][:, c0:c1], in1=alibi[:, h, c0:c1],
                                                  scale=-(DH ** -0.5), scalar=3e38, op0=ALU.add, op1=ALU.min,
                                                  accum_out=nmax[:, h % 2, t:t + 1])
                last.then_inc(sc_ready, 1)

            def evacuate(s, h):
                if h % 2:
                    return
                dve.wait_ge(turn_done, NH * s.n + h + 1)
                if later(s) or h >= 2:
                    dve.wait_ge(mix_done, NH * s.n + h - 1)
                v.tensor_copy(prT[0][:], ps_t[0][:, 0:3 * P]).then_inc(prT_even, 1)

            def recip(s):
                dve.wait_ge(pr_ready, NH * s.n + NH)
                if later(s):
                    dve.wait_ge(rexp_ready, s.n)
                v.reciprocal(rsums[:], sums[s.par][:]).then_inc(rsums_ready, 1)

            def scale_mix(s):
                dve.wait_ge(rT_done, s.n + 1)
                dve.wait_ge(yT_ready, s.n + 1)
                if later(s):
                    dve.wait_ge(out2_done, s.n)
                v.tensor_tensor(ynT[:].rearrange("p g t -> p (g t)"), yT[:].rearrange("p g t -> p (g t)"), ps_c[:], ALU.mult).then_inc(ynT_ready, 1)

            def hidden_rows(s):
                dve.wait_ge(out2_done, s.n + 1)
                dve.wait_ge(h1b_ready, s.n + 1)
                if later(s, 2):
                    dve.wait_ge(h2_out[s.par], 16 * s.pair)
                v.tensor_tensor(h2[s.par][:, :, 0:D], ps_c[:].rearrange("p (t c) -> p t c", t=TT), h1b[s.par][:],
                                ALU.add).then_inc(h2_ready, 1)

            def stats3(s):
                dve.wait_ge(h2_ready, s.n + 1)
                stats(2, h2[s.par], s)

            def aggregate3(s):
                aggregate(2, s)

            def norm3(s):
                dve.wait_ge(rstd_ready[2], s.n + 1)
                if later(s):
                    dve.wait_ge(xfT_done, s.n)
                normalize(2, xf, h2[s.par], s).then_inc(xf_ready, 1)

            wide = [P, TT, E]

            def add_bias(s):
                dve.wait_ge(logits_done, s.n + 1)
                v.tensor_tensor(lg[:].rearrange("p t e -> p (t e)"), ps_c[:, 0:TT * E], router_b[:].rearrange("p t e -> p (t e)"),
                                ALU.add).then_inc(route, 1)

            def find_top(s):
                dve.wait_ge(route, 5 * s.n + 1)
                v.tensor_reduce(top[:], lg[:], AX.X, ALU.max).then_inc(route, 1)

            def match_top(s):
                dve.wait_ge(route, 5 * s.n + 2)
                v.tensor_tensor(eq[:], lg[:], top[:, :, None].to_broadcast(wide), ALU.is_equal).then_inc(route, 1)

            def number_matches(s):
                dve.wait_ge(route, 5 * s.n + 3)
                v.tensor_tensor(onehot_f[:], eq[:], rev[:], ALU.mult).then_inc(route, 1)

            def find_first(s):
                dve.wait_ge(route, 5 * s.n + 4)
                v.tensor_reduce(best[:], onehot_f[:], AX.X, ALU.max).then_inc(route, 1)

            def choose(s):
                dve.wait_ge(route, 5 * s.n + 5)
                if later(s):
                    dve.wait_ge(acc_ready, s.n)
                v.tensor_tensor(onehot[:], rev[:], best[:, :, None].to_broadcast(wide), ALU.is_equal).then_inc(onehot_ready, 1)

            def pick_rank(s):
                dve.wait_ge(rank_done, s.n + 1)
                v.tensor_tensor(place_m[:].rearrange("p t e -> p (t e)"), ps_c[:, 0:TT * E], onehot[:].rearrange("p t e -> p (t e)"),
                                ALU.mult).then_inc(place_step, 1)

            def sum_rank(s):
                dve.wait_ge(place_step, 2 * s.n + 1)
                v.tensor_reduce(place_f[:], place_m[:], AX.X, ALU.add).then_inc(place_step, 1)

            def place(s):
                dve.wait_ge(place_step, 2 * s.n + 2)
                if later(s, 2):
                    dve.wait_ge(placed[s.par], 32 * s.pair)
                v.tensor_copy(place_i[s.par][:], place_f[:]).then_inc(place_ready, 1)

            run_iterations(dve, "DVE", dict(tok_qk=tok_qk, tok_v=tok_v, tok_softmax=tok_softmax, tok_turn=tok_turn, tok_mix=tok_mix, tok_out=tok_out,
                                     stats1=stats1, norm1=norm1, stats2=stats2, norm2=norm2, project_q=project(0), project_k=project(1), weights=weights,
                                     evacuate=evacuate, recip=recip, scale_mix=scale_mix, hidden_rows=hidden_rows, stats3=stats3,
                                     aggregate1=aggregate1, aggregate2=aggregate2, aggregate3=aggregate3, norm3=norm3,
                                     add_bias=add_bias, find_top=find_top, match_top=match_top, number_matches=number_matches,
                                     find_first=find_first, choose=choose, pick_rank=pick_rank, sum_rank=sum_rank, place=place))

            for i in range(NB):
                v.memset(he[i], 0.0).then_inc(he_clear, 1)
            for i in range(2):
                v.memset(hT[i][HID:HID + 1, :], 1.0)
            dve.wait_ge(tab_pe, 1)
            v.tensor_copy(count[:], ps_c[0:E, 0:1]).then_inc(tab_dve, 1)
            dve.wait_ge(tab_dve, 1)
            v.tensor_scalar(below, iota_t[:, 0:NTILE], float(P), count[:, 0:1], ALU.mult, ALU.is_lt).then_inc(route, 1)
            dve.wait_ge(route, 5 * NS + 1)
            v.tensor_reduce(ntiles[:], below, AX.X, ALU.add).then_inc(tab_dve, 1)
            dve.wait_ge(tab_pe, 2)
            v.tensor_copy(cum[:], ps_c[0:E, 1:2]).then_inc(route, 1)
            dve.wait_ge(route, 5 * NS + 2)
            v.tensor_scalar(passed, iota_t[:], cum[:, 0:1], None, ALU.is_ge).then_inc(tab_dve, 1)
            dve.wait_ge(tab_pe, 3)
            experts, skipped = ps_c[0:1, 0:MTILES], ps_c[0:1, MTILES:2 * MTILES]
            v.scalar_tensor_tensor(out=tab_f[:, 0, :], in0=experts, scalar=float(NTOK // P), in1=iota_t[0:1, :],
                                   op0=ALU.mult, op1=ALU.add)
            v.tensor_scalar(tab_f[:, 1, :], experts, float(E - 1), None, ALU.min)
            v.tensor_copy(tab_f[:, 2, :], skipped).then_inc(route, 1)
            dve.wait_ge(route, 5 * NS + 3)
            v.tensor_tensor(tab_f[:, 3, :], tab_f[:, 0, :], tab_f[:, 2, :], ALU.subtract).then_inc(route, 1)
            dve.wait_ge(route, 5 * NS + 4)
            v.tensor_copy(table[:, 0, :], tab_f[:, 1, :])
            v.tensor_scalar(table[:, 1, :], tab_f[:, 3, :], float(P), None, ALU.mult).then_inc(tab_dve, 1)

            def e_take(i, b, turn):
                dve.wait_ge(he_in[b], 16 * (turn + 1))
                if not isinstance(turn, int) or turn:
                    dve.wait_ge(oe_out[b], 16 * turn)
                v.tensor_copy(oid[b], eid[b]).then_inc(e_oid, 1)
                if not isinstance(i, int) or i >= 2:
                    dve.wait_ge(e_xeT, i - 1)
                v.tensor_scalar(xe[b % 2], he[b][:, 0:D], he[b][:, D:D + 1], he[b][:, D + 1:ROW], ALU.subtract, ALU.mult).then_inc(e_xe, 1)

            def e_out(i, b):
                dve.wait_ge(e_y, i + 1)
                v.scalar_tensor_tensor(out=oe[b], in0=(ps_a, ps_b)[b % 2][:, 0:D], scalar=0.0, in1=he[b][:, 0:D],
                                       op0=ALU.max, op1=ALU.add).then_inc(e_o, 1)

            TAKE = 3

            def step(r, u):
                e_take(NB * r + u + TAKE, (u + TAKE) % NB, r + (u + TAKE) // NB)
                e_out(NB * r + u, u)

            for i in range(TAKE):
                e_take(i, i, 0)
            for u in range(NB):
                step(0, u)
            with dve.Fori(1, MTILES // NB - 1) as r:
                for u in range(NB):
                    step(r, u)
            for u in range(NB - TAKE):
                step(MTILES // NB - 1, u)
            for i in range(MTILES - TAKE, MTILES):
                e_out(i, i % NB)

        @block.tensor
        def _(pe):
            m = nc.tensor
            pe.wait_ge(first_loaded, FIRST_LOADED)
            pe.wait_ge(dve_const, 3)
            m.matmul(ps_c[:, 0:D], bv_rep[:, 0, :], wo[:], start=True, stop=True)
            m.matmul(ps_c[:, D:2 * D], bv_rep[:, 1, :], wo2[:, 0, :], start=True, stop=False)
            m.matmul(ps_c[:, D:2 * D], bv_rep[:, 2, :], wo2[:, 1, :], start=False, stop=True).then_inc(pe_const, 1)
            pe.wait_ge(dve_const, BIAS_ROWS)

            def turn_tokens(dst, src):
                for c in range(CC):
                    for t in range(TT):
                        last = m.transpose(dst[:, c * T + t * P:c * T + (t + 1) * P], src[:, t, c * P:(c + 1) * P], ident[:])
                return last

            def by_channel(dst, w, xt):
                for c in range(CC):
                    last = m.matmul(dst, w[c], xt[:, c, :], start=(c == 0), stop=(c == CC - 1))
                return last

            def by_token(dst, xt, w, n):
                for t in range(TT):
                    for c in range(CC):
                        last = m.matmul(dst[:, t * n:(t + 1) * n], xt[:, c, t * P:(t + 1) * P], w[:, c, :],
                                        start=(c == 0), stop=(c == CC - 1))
                return last

            def embed_turn(s):
                pe.wait_ge(x_ready, s.n + 1)
                if later(s, 2):
                    pe.wait_ge(vpad_ready, s.n - 1)
                if later(s):
                    pe.wait_ge(h0_ready, s.n)
                turn_tokens(ps_a, x[s.par]).then_inc(xT_done, 1)

            def tok_qk(s):
                pe.wait_ge(xT_ready, s.n + 1)
                if later(s, 2):
                    pe.wait_ge(rest_ready, 2 * s.n - 2)
                by_channel(ps_b[:, 0:T], [wq[:, c, :] for c in range(CC)], xT)
                by_channel(ps_b[:, T:2 * T], [wk[:, c, :] for c in range(CC)], xT).then_inc(qk_done, 1)

            def tok_v(s):
                pe.wait_ge(xT_ready, s.n + 1)
                by_token(ps_a, xT, wv, DK).then_inc(v_done, 1)

            def tok_scores(s):
                pe.wait_ge(q_ready, s.n + 1)
                pe.wait_ge(k_ready, s.n + 1)
                for t in range(TT):
                    last = m.matmul(ps_b[:, t * T:(t + 1) * T], qkT[:, 0, t * P:(t + 1) * P], qkT[:, 1, :], start=True, stop=True)
                last.then_inc(s1_done, 1)

            def tok_turn(s):
                pe.wait_ge(p1_ready, s.n + 1)
                pe.wait_ge(v_ready, s.n + 1)
                turn_tokens(ps_a, p1).then_inc(pT1_done, 1)

            def tok_mix(s):
                pe.wait_ge(pT1_ready, s.n + 1)
                by_channel(ps_b[:, 0:T], [v1[:, t, :] for t in range(TT)], pT1).then_inc(head_done, 1)

            def tok_out(s):
                pe.wait_ge(head_ready, s.n + 1)
                for t in range(TT):
                    last = m.matmul(ps_a[:, t * D:(t + 1) * D], headT[:, t * P:(t + 1) * P], wo[:], start=True, stop=True)
                last.then_inc(out1_done, 1)

            def norm_turn(s):
                pe.wait_ge(xn_ready, s.n + 1)
                pe.wait_ge(head_ready, next_or_last(s))
                turn_tokens(ps_b, xn).then_inc(xnT_done, 1)

            def project_q(s):
                if is_first(s):
                    pe.wait_ge(loaded, ALL_LOADED)
                pe.wait_ge(xnT_ready, s.n + 1)
                pe.wait_ge(h0_ready, next_or_last(s))
                for gr in range(2):
                    last = by_channel(ps_a[:, gr * T:(gr + 1) * T], [wq2[:, c, gr * P:(gr + 1) * P] for c in range(CC)], xnT)
                last.then_inc(Q_done, 1)

            def project_k(s):
                pe.wait_ge(xnT_ready, s.n + 1)
                for gr in range(2):
                    last = by_channel(ps_b[:, gr * T:(gr + 1) * T], [wk2[:, c, gr * P:(gr + 1) * P] for c in range(CC)], xnT)
                last.then_inc(K_done, 1)

            def project_v(s):
                pe.wait_ge(rest_ready, 2 * s.n + 1)
                by_token(ps_a, xnT, wv2, D).then_inc(V_done, 1)

            def scores(s, h):
                if h == 0:
                    pe.wait_ge(stacked[s.par], 192 * (s.pair + 1))
                if later(s) or h >= 2:
                    pe.wait_ge(sc_ready, NH * s.n + h - 1)
                q, k, dst = qst[s.par], kst[s.par], ps_s[h % 2]
                m.matmul(dst[:, 0:P], q[:, h, 0:P], k[:, h, 0:P], start=True, stop=True)
                m.matmul(dst[:, P:3 * P], q[:, h, P:2 * P], k[:, h, :], start=True, stop=True).then_inc(scores_done, 1)

            def turn(s, h):
                pe.wait_ge(pr_ready, NH * s.n + h + 1)
                if later(s) or h >= 2:
                    pe.wait_ge((prT_even, prT_odd)[h % 2], NH // 2 * s.n + h // 2)
                for i in range(3):
                    last = m.transpose(ps_t[h % 2][:, i * P:(i + 1) * P], pr[h % 2][:, i * P:(i + 1) * P], ident[:])
                last.then_inc(turn_done, 1)

            def mix(s, h):
                pe.wait_ge((prT_even, prT_odd)[h % 2], NH // 2 * s.n + h // 2 + 1)
                if h == 0:
                    pe.wait_ge(vpad_ready, s.n + 1)
                    if later(s):
                        pe.wait_ge(yT_ready, s.n)
                gr, quad, odd = h // 8, h % 8 // 2, h % 2
                rows = slice(32 * quad, 32 * quad + 32)
                w = vpad[s.par][:, :, h // 2, 32 * odd:32 * odd + 32]
                m.matmul(ps_y[rows, gr * T:(gr + 1) * T], w[:, 0, :], prT[h % 2][:, 0:T], start=(odd == 0), stop=False,
                         skip_group_check=True)
                m.matmul(ps_y[rows, gr * T + P:(gr + 1) * T], w[:, 1, :], prT[h % 2][:, T:3 * P], start=False, stop=(odd == 1),
                         skip_group_check=True).then_inc(mix_done, 1)

            def recip_turn(s):
                pe.wait_ge(rexp_ready, s.n + 1)
                if later(s):
                    pe.wait_ge(place_step, 2 * s.n - 1)
                turn_tokens(ps_c, rexp).then_inc(rT_done, 1)

            def out2(s):
                pe.wait_ge(ynT_ready, s.n + 1)
                by_token(ps_c, ynT, wo2, D).then_inc(out2_done, 1)

            def router_turn(s):
                pe.wait_ge(xf_ready, s.n + 1)
                turn_tokens(ps_c, xf).then_inc(xfT_done, 1)

            def logits(s):
                pe.wait_ge(xfT_ready, s.n + 1)
                by_token(ps_c, xfT, router, E).then_inc(logits_done, 1)

            def rank(s):
                pe.wait_ge(onehot_ready, s.n + 1)
                if later(s):
                    pe.wait_ge(acc_ready, s.n)
                for t in range(TT):
                    dst = ps_c[:, t * E:(t + 1) * E]
                    m.matmul(dst, ones[:], base[:], start=True, stop=False)
                    m.matmul(dst, ones[:], acc[:], start=False, stop=False)
                    if t:
                        m.matmul(dst, ones[:], onehot[:, 0, :], start=False, stop=False)
                    last = m.matmul(dst, tri[:], onehot[:, t, :], start=False, stop=True)
                last.then_inc(rank_done, 1)

            run_iterations(pe, "PE", dict(embed_turn=embed_turn, tok_qk=tok_qk, tok_v=tok_v, tok_scores=tok_scores, tok_turn=tok_turn,
                                    tok_mix=tok_mix, tok_out=tok_out, norm_turn=norm_turn, project_q=project_q, project_k=project_k, project_v=project_v,
                                    scores=scores, turn=turn, mix=mix, recip_turn=recip_turn, out2=out2, router_turn=router_turn,
                                    logits=logits, rank=rank))

            pe.wait_ge(acc_ready, NS)
            pe.wait_ge(place_step, 2 * NS)
            m.matmul(ps_c[0:E, 0:1], acc[:], ones[:, 0:1], start=True, stop=True).then_inc(tab_pe, 1)
            pe.wait_ge(tab_dve, 2)
            m.matmul(ps_c[0:E, 1:2], tri_inc[:], ntiles[:], start=True, stop=True).then_inc(tab_pe, 1)
            pe.wait_ge(tab_dve, 3)
            m.matmul(ps_c[0:1, 0:MTILES], ones_col[:], passed, start=True, stop=True)
            m.matmul(ps_c[0:1, MTILES:2 * MTILES], ntiles[:], passed, start=True, stop=True).then_inc(tab_pe, 1)
            pe.wait_ge(tab_dve, 4)
            pe.wait_ge(experts_loaded, EXPERTS_LOADED)

            def e_turn(i, b):
                pe.wait_ge(e_xe, i + 1)
                if not isinstance(i, int) or i >= 2:
                    pe.wait_ge(e_xeTs, i - 1)
                for c in range(CC):
                    last = m.transpose(ps_s[b][:, c * P:(c + 1) * P], xe[b][:, c * P:(c + 1) * P], ident[:])
                last.then_inc(e_xeT, 1)

            def e_hidden(i, b):
                pe.wait_ge(e_xeTs, i + 1)
                pe.wait_ge(e_w1, i + 1)
                if not isinstance(i, int) or i >= 2:
                    pe.wait_ge(e_hs, i - 1)
                for c in range(CC):
                    last = m.matmul(ps_t[b][0:HID, 0:P], w1e[b][:, c * HID:(c + 1) * HID], xeT[b][:, c, :], start=(c == 0), stop=(c == CC - 1))
                last.then_inc(e_h, 1)

            def e_output(i, b, e):
                pe.wait_ge(e_hs, i + 1)
                if not isinstance(i, int) or i >= 2:
                    pe.wait_ge(e_o, i - 1)
                m.matmul((ps_a, ps_b)[b][:, 0:D], hT[b][:], w2[:, bass.ds(e, 1), :], start=True, stop=True).then_inc(e_y, 1)

            def expert_of(i):
                return pe.value_load(table[0:1, 0, bass.ds(i, 1)], min_val=0, max_val=E - 1)

            def step(i, b):
                e = expert_of(i - 1)
                e_turn(i + 1, 1 - b)
                e_hidden(i, b)
                e_output(i - 1, 1 - b, e)

            e_turn(0, 0)
            e_turn(1, 1)
            e_hidden(0, 0)
            step(1, 1)
            step(2, 0)
            with pe.Fori(1, (MTILES - 2) // 2) as r:
                step(2 * r + 1, 1)
                step(2 * r + 2, 0)
            e_hidden(MTILES - 1, 1)
            for i in range(MTILES - 2, MTILES):
                e_output(i, i % 2, expert_of(i))


def kernel(**inputs):
    import numpy as np
    import concourse.bacc as bacc
    from concourse.bass_utils import run_bass_kernel_spmd

    i = {k: np.asarray(v) for k, v in inputs.items()}
    tok, attn, ffn = (lambda n: i["L0_tok_" + n]), (lambda n: i["L0_attn_" + n]), (lambda n: i["L0_ffn_" + n])
    half = NH // 2

    def head_cols(w):
        return w.reshape(-1, half, 2, DH).transpose(0, 2, 3, 1).reshape(-1, D)

    arrays = {
        "ids": i["x"].reshape(NS, TT, P).transpose(0, 2, 1),
        "tok_emb": tok("tok_emb"), "pos_emb": tok("pos_emb"),
        "wqT": tok("wq").T, "wkT": tok("wk").T, "wvT": tok("wv").T, "woT": tok("wo").T,
        "bq": tok("bq")[:, None], "bk": tok("bk")[:, None], "bv": tok("bv")[:, None], "bo": tok("bo"),
        "gamma": tok("gamma"), "beta": tok("beta"),
        "wq2T": head_cols(attn("Wq").T), "wk2T": head_cols(attn("Wk").T), "wv2T": attn("Wv").T, "wo2T": attn("Wo").T,
        "bq2": head_cols(attn("bq")).reshape(2, P).T, "bk2": head_cols(attn("bk")).reshape(2, P).T,
        "bv2": attn("bv").reshape(2, P).T, "bo2": attn("bo"),
        "routerT": ffn("router_w").T, "router_b": ffn("router_b"),
        "w1": ffn("weights1"), "b1T": ffn("bias1").T, "w2": ffn("weights2"), "b2": ffn("bias2"),
    }
    arrays = {k: np.ascontiguousarray(v) for k, v in arrays.items()}
    nc = bacc.Bacc("TRN2", target_bir_lowering=False, num_devices=1)
    args = {k: nc.dram_tensor(f"in_{k}_dram", v.shape, mybir.dt.from_np(v.dtype), kind="ExternalInput").ap()
            for k, v in arrays.items()}
    args["out"] = nc.dram_tensor("out_dram", (NTOK, D), F32, kind="ExternalOutput").ap()
    build(nc, args)
    r = run_bass_kernel_spmd(nc, [{f"in_{k}_dram": v for k, v in arrays.items()}], core_ids=[0])
    return r.results[0]["out_dram"].reshape(NS, T, D)
```
